# Optimizing a Trainium2 kernel written in Bass

```python
import numpy as np
import jax
import jax.numpy as jnp

def _softmax(x, axis=-1):
    return jax.nn.softmax(x, axis=axis)

def _gelu(x):
    return jax.nn.gelu(x, approximate=True)

def _silu(x):
    return jax.nn.silu(x)

def _sigmoid(x):
    return jax.nn.sigmoid(x)

def _layernorm(x, axis=-1, eps=1e-05):
    m = jnp.mean(x, axis=axis, keepdims=True)
    v = jnp.var(x, axis=axis, keepdims=True)
    return (x - m) / jnp.sqrt(v + eps)

def _scatter_add(tgt, idx, src, axis=0):
    return tgt.at[idx].add(src)

def _segment_sum(src, seg, n):
    return jax.ops.segment_sum(src, seg, n)
kernel_name = 'mk_hybrid_d1_jaxref_r8_fd46b3'

def setup_inputs(seed: int=0):
    np.random.seed(seed)
    _w = jnp.asarray

    def _L0_attn_a_setup():
        import jax, jax.numpy as jnp
        import numpy as np
        L, D, F, H = (4, 128, 256, 8)
        DH = D // H
        EPS = 1e-05

        def _layer_norm(x, scale, bias):
            mu = x.mean(-1, keepdims=True)
            var = x.var(-1, keepdims=True)
            return (x - mu) * jax.lax.rsqrt(var + EPS) * scale + bias

        def _rotate(x, cos, sin):
            x1, x2 = (x[..., 0::2], x[..., 1::2])
            r1 = x1 * cos - x2 * sin
            r2 = x1 * sin + x2 * cos
            return jnp.stack([r1, r2], axis=-1).reshape(x.shape)

        def _decay_matrix(S):
            gammas = 1.0 - jnp.exp(jnp.linspace(np.log(1 / 32), np.log(1 / 64), H)).astype(jnp.float32)
            n = jnp.arange(S)
            diff = (n[:, None] - n[None, :]).astype(jnp.float32)
            pw = jnp.exp(jnp.clip(diff, 0.0)[None] * jnp.log(gammas)[:, None, None])
            return jnp.where(diff[None] >= 0, pw, 0.0)

        def _retention(x, Wq, Wk, Wv, Wg, Wo, gn_s, gn_b, Dm, cos, sin):
            B, S, _ = x.shape
            Q = (x @ Wq).reshape(B, S, H, DH)
            K = (x @ Wk).reshape(B, S, H, DH)
            V = (x @ Wv).reshape(B, S, H, DH)
            Q = _rotate(Q, cos, sin)
            K = _rotate(K, cos, -sin)
            att = jnp.einsum('bnhd,bmhd->bhnm', Q, K) * Dm
            Y = jnp.einsum('bhnm,bmhd->bnhd', att, V)
            mu = Y.mean(-1, keepdims=True)
            var = Y.var(-1, keepdims=True)
            Y = (Y - mu) * jax.lax.rsqrt(var + EPS)
            Y = Y.reshape(B, S, D) * gn_s + gn_b
            G = jax.nn.swish(x @ Wg)
            return G * Y @ Wo
        key = jax.random.key(seed)
        ks = jax.random.split(key, 8)
        B, S = (4, 128)
        sd = 1.0 / np.sqrt(D)
        sf = 1.0 / np.sqrt(F)
        return {'X': jax.random.normal(ks[0], (B, S, D), jnp.float32), 'Wq': jax.random.normal(ks[1], (L, D, D), jnp.float32) * sd, 'Wk': jax.random.normal(ks[2], (L, D, D), jnp.float32) * sd, 'Wv': jax.random.normal(ks[3], (L, D, D), jnp.float32) * sd, 'Wg': jax.random.normal(ks[4], (L, D, D), jnp.float32) * sd, 'Wo': jax.random.normal(ks[5], (L, D, D), jnp.float32) * sd, 'W1': jax.random.normal(ks[6], (L, D, F), jnp.float32) * sd, 'W2': jax.random.normal(ks[7], (L, F, D), jnp.float32) * sf, 'ln_scale': jnp.ones((D,), jnp.float32), 'ln_bias': jnp.zeros((D,), jnp.float32), 'gn_scale': jnp.ones((L, D), jnp.float32), 'gn_bias': jnp.zeros((L, D), jnp.float32)}
    _L0_attn_a_in = _L0_attn_a_setup()

    def _L0_attn_b_setup():
        import jax, jax.numpy as jnp
        import numpy as np
        D_MODEL, HD_DIM, NUM_HEADS = (128, 256, 16)
        HEAD_DIM = HD_DIM // NUM_HEADS
        B, T = (4, 256)
        key = jax.random.key(seed)
        ks = jax.random.split(key, 10)
        s = 0.02
        x = jax.random.normal(ks[0], (B, T, D_MODEL), dtype=jnp.float32)
        conv_w = jax.random.normal(ks[1], (D_MODEL, 1, 4), dtype=jnp.float32) * s
        conv_b = jax.random.normal(ks[2], (D_MODEL,), dtype=jnp.float32) * s
        qk_w = jax.random.normal(ks[3], (HD_DIM, D_MODEL), dtype=jnp.float32) * s
        v_w = jnp.eye(HD_DIM, D_MODEL, dtype=jnp.float32)
        g_w = jax.random.normal(ks[4], (HD_DIM, D_MODEL), dtype=jnp.float32) * s
        g_b = jnp.full((HD_DIM,), 2.0, dtype=jnp.float32)
        o_w = jax.random.normal(ks[5], (D_MODEL, HD_DIM), dtype=jnp.float32) * s
        ln_g = jnp.ones((D_MODEL,), dtype=jnp.float32)
        ln_b = jnp.zeros((D_MODEL,), dtype=jnp.float32)
        idx = jnp.linspace(0.0, 1.0, HEAD_DIM)
        h = jnp.arange(NUM_HEADS, dtype=jnp.float32)[:, None]
        freqs = jnp.where(h > 0, (10.0 ** idx)[None, :] * h, 0.0).astype(jnp.float32)
        gamma = jnp.full((NUM_HEADS, 1, 1), 0.999, dtype=jnp.float32).at[0].set(1.0)
        return {'x': x, 'conv_w': conv_w, 'conv_b': conv_b, 'qk_w': qk_w, 'v_w': v_w, 'g_w': g_w, 'g_b': g_b, 'o_w': o_w, 'ln_g': ln_g, 'ln_b': ln_b, 'freqs': freqs, 'gamma': gamma}
    _L0_attn_b_in = _L0_attn_b_setup()

    def _L0_ffn_setup():
        import jax, jax.numpy as jnp
        import numpy as np
        B, S, H, F, E = (1, 256, 128, 256, 8)

        def _swiglu(x, wg, wu, wd):
            return jax.nn.silu(x @ wg.T) * (x @ wu.T) @ wd.T
        key = jax.random.key(seed)
        ks = jax.random.split(key, 8)
        sc = 1.0 / np.sqrt(H)
        scf = 1.0 / np.sqrt(F)
        return {'hidden_states': jax.random.normal(ks[0], (B, S, H), jnp.float32), 'gate_w': jax.random.normal(ks[1], (E, H), jnp.float32) * sc, 'shared_gate': jax.random.normal(ks[2], (F, H), jnp.float32) * sc, 'shared_up': jax.random.normal(ks[3], (F, H), jnp.float32) * sc, 'shared_down': jax.random.normal(ks[4], (H, F), jnp.float32) * scf, 'r_gate': jax.random.normal(ks[5], (E, F, H), jnp.float32) * sc, 'r_up': jax.random.normal(ks[6], (E, F, H), jnp.float32) * sc, 'r_down': jax.random.normal(ks[7], (E, H, F), jnp.float32) * scf}
    _L0_ffn_in = _L0_ffn_setup()
    _d = {'L0_attn_a_X': _L0_attn_a_in['X'], 'L0_attn_a_Wq': _L0_attn_a_in['Wq'], 'L0_attn_a_Wk': _L0_attn_a_in['Wk'], 'L0_attn_a_Wv': _L0_attn_a_in['Wv'], 'L0_attn_a_Wg': _L0_attn_a_in['Wg'], 'L0_attn_a_Wo': _L0_attn_a_in['Wo'], 'L0_attn_a_W1': _L0_attn_a_in['W1'], 'L0_attn_a_W2': _L0_attn_a_in['W2'], 'L0_attn_a_ln_scale': _L0_attn_a_in['ln_scale'], 'L0_attn_a_ln_bias': _L0_attn_a_in['ln_bias'], 'L0_attn_a_gn_scale': _L0_attn_a_in['gn_scale'], 'L0_attn_a_gn_bias': _L0_attn_a_in['gn_bias'], 'L0_attn_b_conv_w': _L0_attn_b_in['conv_w'], 'L0_attn_b_conv_b': _L0_attn_b_in['conv_b'], 'L0_attn_b_qk_w': _L0_attn_b_in['qk_w'], 'L0_attn_b_v_w': _L0_attn_b_in['v_w'], 'L0_attn_b_g_w': _L0_attn_b_in['g_w'], 'L0_attn_b_g_b': _L0_attn_b_in['g_b'], 'L0_attn_b_o_w': _L0_attn_b_in['o_w'], 'L0_attn_b_ln_g': _L0_attn_b_in['ln_g'], 'L0_attn_b_ln_b': _L0_attn_b_in['ln_b'], 'L0_attn_b_freqs': _L0_attn_b_in['freqs'], 'L0_attn_b_gamma': _L0_attn_b_in['gamma'], 'L0_ffn_gate_w': _L0_ffn_in['gate_w'], 'L0_ffn_shared_gate': _L0_ffn_in['shared_gate'], 'L0_ffn_shared_up': _L0_ffn_in['shared_up'], 'L0_ffn_shared_down': _L0_ffn_in['shared_down'], 'L0_ffn_r_gate': _L0_ffn_in['r_gate'], 'L0_ffn_r_up': _L0_ffn_in['r_up'], 'L0_ffn_r_down': _L0_ffn_in['r_down']}
    _x0 = _d['L0_attn_a_X']
    _d['L0_attn_a_X'] = jax.random.normal(jax.random.fold_in(jax.random.key(seed), 1), (1, 2048, 128), dtype=_x0.dtype)
    del _x0
    return _d

def reference(L0_attn_a_X, L0_attn_a_Wq, L0_attn_a_Wk, L0_attn_a_Wv, L0_attn_a_Wg, L0_attn_a_Wo, L0_attn_a_W1, L0_attn_a_W2, L0_attn_a_ln_scale, L0_attn_a_ln_bias, L0_attn_a_gn_scale, L0_attn_a_gn_bias, L0_attn_b_conv_w, L0_attn_b_conv_b, L0_attn_b_qk_w, L0_attn_b_v_w, L0_attn_b_g_w, L0_attn_b_g_b, L0_attn_b_o_w, L0_attn_b_ln_g, L0_attn_b_ln_b, L0_attn_b_freqs, L0_attn_b_gamma, L0_ffn_gate_w, L0_ffn_shared_gate, L0_ffn_shared_up, L0_ffn_shared_down, L0_ffn_r_gate, L0_ffn_r_up, L0_ffn_r_down):

    def _L0_attn_a_ref(X, Wq, Wk, Wv, Wg, Wo, W1, W2, ln_scale, ln_bias, gn_scale, gn_bias):
        import jax, jax.numpy as jnp
        import numpy as np
        L, D, F, H = (4, 128, 256, 8)
        DH = D // H
        EPS = 1e-05

        def _layer_norm(x, scale, bias):
            mu = x.mean(-1, keepdims=True)
            var = x.var(-1, keepdims=True)
            return (x - mu) * jax.lax.rsqrt(var + EPS) * scale + bias

        def _rotate(x, cos, sin):
            x1, x2 = (x[..., 0::2], x[..., 1::2])
            r1 = x1 * cos - x2 * sin
            r2 = x1 * sin + x2 * cos
            return jnp.stack([r1, r2], axis=-1).reshape(x.shape)

        def _decay_matrix(S):
            gammas = 1.0 - jnp.exp(jnp.linspace(np.log(1 / 32), np.log(1 / 64), H)).astype(jnp.float32)
            n = jnp.arange(S)
            diff = (n[:, None] - n[None, :]).astype(jnp.float32)
            pw = jnp.exp(jnp.clip(diff, 0.0)[None] * jnp.log(gammas)[:, None, None])
            return jnp.where(diff[None] >= 0, pw, 0.0)

        def _retention(x, Wq, Wk, Wv, Wg, Wo, gn_s, gn_b, Dm, cos, sin):
            B, S, _ = x.shape
            Q = (x @ Wq).reshape(B, S, H, DH)
            K = (x @ Wk).reshape(B, S, H, DH)
            V = (x @ Wv).reshape(B, S, H, DH)
            Q = _rotate(Q, cos, sin)
            K = _rotate(K, cos, -sin)
            att = jnp.einsum('bnhd,bmhd->bhnm', Q, K) * Dm
            Y = jnp.einsum('bhnm,bmhd->bnhd', att, V)
            mu = Y.mean(-1, keepdims=True)
            var = Y.var(-1, keepdims=True)
            Y = (Y - mu) * jax.lax.rsqrt(var + EPS)
            Y = Y.reshape(B, S, D) * gn_s + gn_b
            G = jax.nn.swish(x @ Wg)
            return G * Y @ Wo
        B, S, _ = X.shape
        pos = jnp.arange(S, dtype=jnp.float32)
        inv_freq = 1.0 / 10000.0 ** (jnp.arange(0, DH, 2, dtype=jnp.float32) / DH)
        ang = pos[:, None] * inv_freq[None, :]
        cos = jnp.cos(ang)[None, :, None, :]
        sin = jnp.sin(ang)[None, :, None, :]
        Dm = _decay_matrix(S)
        for i in range(L):
            Yr = _retention(_layer_norm(X, ln_scale, ln_bias), Wq[i], Wk[i], Wv[i], Wg[i], Wo[i], gn_scale[i], gn_bias[i], Dm, cos, sin) + X
            X = jax.nn.gelu(_layer_norm(Yr, ln_scale, ln_bias) @ W1[i]) @ W2[i] + Yr
        return X

    def _L0_attn_b_ref(x, conv_w, conv_b, qk_w, v_w, g_w, g_b, o_w, ln_g, ln_b, freqs, gamma):
        import jax, jax.numpy as jnp
        import numpy as np
        D_MODEL, HD_DIM, NUM_HEADS = (128, 256, 16)
        HEAD_DIM = HD_DIM // NUM_HEADS
        B, T = (4, 256)
        Bsz, Tlen, C = x.shape
        H, D = freqs.shape
        xc = jax.lax.conv_general_dilated(x.transpose(0, 2, 1), conv_w, window_strides=(1,), padding=[(3, 0)], feature_group_count=C, dimension_numbers=('NCH', 'OIH', 'NCH'))
        xc = (xc + conv_b[None, :, None]).transpose(0, 2, 1)
        qk = jnp.einsum('btc,ec->bte', xc, qk_w).reshape(Bsz, Tlen, H, D)
        nrm = jnp.maximum(jnp.sqrt(jnp.sum(qk * qk, axis=-1, keepdims=True)), 1e-12)
        q = qk / nrm
        k = q
        v = jnp.einsum('btc,ec->bte', xc, v_w).reshape(Bsz, Tlen, H, D)
        g = jax.nn.sigmoid(jnp.einsum('btc,ec->bte', xc, g_w) + g_b).reshape(Bsz, Tlen, H, D)
        t = jnp.arange(Tlen, dtype=x.dtype)[None, :, None, None]
        angles = t * freqs[None, None]
        k_sh = jnp.concatenate([jnp.zeros_like(k[:, :1]), k[:, :-1]], axis=1)
        state_r = (v * jnp.cos(angles) + v * k_sh) * g
        decay = jnp.power(gamma.reshape(1, 1, H, 1), t)
        mem_r = jnp.cumsum(state_r * decay, axis=1) / (decay + 1e-06)
        out = (mem_r * q).reshape(Bsz, Tlen, H * D)
        out = jnp.einsum('bte,ce->btc', out, o_w)
        mu = jnp.mean(out, axis=-1, keepdims=True)
        var = jnp.mean((out - mu) ** 2, axis=-1, keepdims=True)
        return (out - mu) / jnp.sqrt(var + 1e-05) * ln_g + ln_b

    def _L0_ffn_ref(hidden_states, gate_w, shared_gate, shared_up, shared_down, r_gate, r_up, r_down):
        import jax, jax.numpy as jnp
        import numpy as np
        B, S, H, F, E = (1, 256, 128, 256, 8)

        def _swiglu(x, wg, wu, wd):
            return jax.nn.silu(x @ wg.T) * (x @ wu.T) @ wd.T
        b, s, h = hidden_states.shape
        x = hidden_states.reshape(-1, h)
        shared_out = _swiglu(x, shared_gate, shared_up, shared_down)
        logits = x @ gate_w.T
        top_id = jnp.argmax(logits, axis=-1)
        score = jax.nn.sigmoid(jnp.max(logits, axis=-1))
        xs = x * score[:, None]

        def body(acc, ws):
            wg, wu, wd, e = ws
            xe = jnp.where((top_id == e)[:, None], xs, 0.0)
            return (acc + _swiglu(xe, wg, wu, wd), None)
        acc0 = jnp.zeros_like(x)
        routed_out, _ = jax.lax.scan(body, acc0, (r_gate, r_up, r_down, jnp.arange(E)))
        return (shared_out + routed_out).reshape(b, s, h)
    x = L0_attn_a_X
    x = x + _L0_attn_a_ref(_layernorm(x, axis=-1), L0_attn_a_Wq, L0_attn_a_Wk, L0_attn_a_Wv, L0_attn_a_Wg, L0_attn_a_Wo, L0_attn_a_W1, L0_attn_a_W2, L0_attn_a_ln_scale, L0_attn_a_ln_bias, L0_attn_a_gn_scale, L0_attn_a_gn_bias)
    x = x + _L0_ffn_ref(_layernorm(x, axis=-1), L0_ffn_gate_w, L0_ffn_shared_gate, L0_ffn_shared_up, L0_ffn_shared_down, L0_ffn_r_gate, L0_ffn_r_up, L0_ffn_r_down)
    x = x + _L0_attn_b_ref(_layernorm(x, axis=-1), L0_attn_b_conv_w, L0_attn_b_conv_b, L0_attn_b_qk_w, L0_attn_b_v_w, L0_attn_b_g_w, L0_attn_b_g_b, L0_attn_b_o_w, L0_attn_b_ln_g, L0_attn_b_ln_b, L0_attn_b_freqs, L0_attn_b_gamma)
    x = x + _L0_ffn_ref(_layernorm(x, axis=-1), L0_ffn_gate_w, L0_ffn_shared_gate, L0_ffn_shared_up, L0_ffn_shared_down, L0_ffn_r_gate, L0_ffn_r_up, L0_ffn_r_down)
    return x

_drawn_inputs = setup_inputs


def setup_inputs(seed=0):
    import zlib

    import numpy as np

    out = dict(_drawn_inputs(seed))
    spreads = {'L0_attn_a_ln_scale': (1.0, 0.2),
     'L0_attn_a_ln_bias': (0.0, 0.1),
     'L0_attn_a_gn_scale': (1.0, 0.2),
     'L0_attn_a_gn_bias': (0.0, 0.1),
     'L0_attn_b_g_b': (2.0, 0.6),
     'L0_attn_b_ln_g': (1.0, 0.2),
     'L0_attn_b_ln_b': (0.0, 0.1)}
    factors = {'L0_attn_b_g_w': 64.0}
    for name, (base, spread) in spreads.items():
        noise = np.random.default_rng([zlib.crc32(name.encode()), seed]).standard_normal(out[name].shape)
        drawn = base * np.exp(spread * noise) if base else spread * noise
        out[name] = jnp.asarray(drawn.astype(out[name].dtype))
    for name, factor in factors.items():
        out[name] = (out[name] * factor).astype(out[name].dtype)
    return out
```

```python
from contextlib import ExitStack

import numpy as np

import concourse.bass as bass
from concourse import mybir

ALU = mybir.AluOpType
ACT = mybir.ActivationFunctionType
AX = mybir.AxisListType
F32 = mybir.dt.float32
I32 = mybir.dt.int32

P = 128
T = 2048
NCH = T // P
D = 128
LAYERS, HEADS, DH, FA = 4, 8, 16, 256
GROUPS = NCH // 2
STEPS = LAYERS * GROUPS
EPS = 1e-5
EXPERTS, FE = 8, 256
TILES = NCH + EXPERTS
ROUND = 12582912.0
MAGIC = float(0x5F3759DF)


def routing_tables():
    earlier = (np.arange(P)[:, None] < np.arange(P)[None, :]).astype(np.float32)
    ones = np.ones((P, P), np.float32)
    rows = [EXPERTS - np.arange(EXPERTS), np.arange(TILES),
            (np.arange(EXPERTS * NCH) % NCH != 0)]
    return np.concatenate([earlier, ones] + [np.tile(r.astype(np.float32)[None], (P, 1)) for r in rows], 1)


def retention_tables():
    gam = (np.float32(1.0) - np.exp(np.linspace(np.log(1 / 32), np.log(1 / 64), HEADS))
           .astype(np.float32)).astype(np.float64)
    inv = (np.float32(1.0) / np.power(np.float32(10000.0), np.arange(0, DH, 2, dtype=np.float32)
                                      / np.float32(DH))).astype(np.float32)
    ang = (np.arange(T, dtype=np.float32)[:, None] * inv[None, :]).astype(np.float64)
    cos, sin = np.cos(ang), np.sin(ang)
    i = np.arange(T) % P
    up = gam[None, :] ** i[:, None]
    down = gam[None, :] ** (-i[:, None].astype(np.float64))
    ct = np.zeros((T, 2, HEADS, DH // 2, 2))
    st = np.zeros((T, 2, HEADS, DH // 2, 2))
    for a, (dec, sg) in enumerate(((up, 1.0), (down, -1.0))):
        ct[:, a] = (dec[:, :, None] * cos[:, None, :])[..., None]
        st[:, a, :, :, 0] = -sg * dec[:, :, None] * sin[:, None, :]
        st[:, a, :, :, 1] = sg * dec[:, :, None] * sin[:, None, :]
    rot = np.stack([ct.reshape(NCH, P, 256), st.reshape(NCH, P, 256)], 0)
    rot = np.ascontiguousarray(rot.transpose(2, 0, 1, 3)).astype(np.float32)
    head = np.arange(D) // DH
    hm = (head[:, None] == np.arange(HEADS)[None, :]).astype(np.float32)
    block = (head[:, None] == head[None, :]).astype(np.float32)
    causal = (np.arange(P)[:, None] <= np.arange(P)[None, :]).astype(np.float32)
    dec = np.repeat((gam[head] ** P)[:, None], NCH, 1)
    dec[:, NCH - 1] = 0.0
    eye = np.eye(P, dtype=np.float32)
    small = np.concatenate([eye, causal, block, hm, dec, routing_tables()], 1).astype(np.float32)
    return rot, np.ascontiguousarray(small)


def wait(eng, sem, value):
    if isinstance(value, int) and value <= 0:
        return
    eng.wait_ge(sem, value)


def spread(ap, axis, n):
    shape = list(ap.shape)
    shape[axis] = n
    return ap.broadcast_to(shape)


def build(nc, a, outs, upto=9):
    ctx = ExitStack()
    with ctx:
        def sb(name, shape, dt=F32):
            return ctx.enter_context(nc.sbuf_tensor(name, shape, dt))

        def sem(name):
            return ctx.enter_context(nc.semaphore(name))

        xin = sb("xin", [P, NCH, D])
        resid = sb("resid", [P, NCH, D])
        small = sb("small", [P, 5 * P + HEADS + NCH + EXPERTS + TILES + EXPERTS * NCH])
        eye, causal, block = small[:, 0:P], small[:, P:2 * P], small[:, 2 * P:3 * P]
        headmask = small[:, 3 * P:3 * P + HEADS]
        decay = small[:, 3 * P + HEADS:3 * P + HEADS + NCH]
        banks = ctx.enter_context(nc.psum_tensor("banks", [P, 8, 512], F32))

        at = 3 * P + HEADS + NCH
        route = {}
        for name, n in (("earlier", P), ("ones", P), ("rev", EXPERTS), ("tile_no", TILES),
                        ("restart", EXPERTS * NCH)):
            route[name] = small[:, at:at + n]
            at += n

        ffn_w = {
            "gate": sb("gate_sb", [P, EXPERTS]),
            "s_gu": sb("s_gu_sb", [P, 4, P]),
            "s_down": sb("s_down_sb", [P, 2, D]),
            "r_gu": sb("r_gu_sb", [P, EXPERTS, 2 * FE]),
            "r_down": sb("r_down_sb", [P, EXPERTS, 2, D]),
        }
        rows_in = nc.dram_tensor("rows_in", (TILES * P, D), F32).ap()
        rows_out = nc.dram_tensor("rows_out", (TILES * P, D), F32).ap()

        ffn_sems = ffn_semaphores(nc, ctx)
        loaded_x = sem("loaded_x")
        loaded_small = sem("loaded_small")
        loaded_ffn = sem("loaded_ffn")
        retention(nc, a, xin, resid, (eye, causal, block, headmask, decay), small, banks,
                  loaded_x, loaded_small, ffn_w, rows_in, loaded_ffn)
        if upto >= 1:
            ffn(nc, 0, xin, ffn_w, rows_in, rows_out, eye, route, banks, loaded_ffn, ffn_sems)
            clear_ffn_semaphores(nc, ffn_sems)
        if upto >= 2:
            tabs = {"cos": sb("cos_tab", [P, 2, T]), "dec": sb("dec_tab", [P, 2, T]),
                    "rdec": sb("rdec_tab", [P, 2, T]), "ready": sem("tables_ready")}
            power_rows = [nc.dram_tensor(f"power_rows{n}", (16, T), F32).ap() for n in range(3)]
            ow = {"qk": sb("qk_sb", [P, 256]), "v": sb("v_sb", [P, 2, P]), "g": sb("g_sb", [P, 2, P]),
                  "o": sb("o_sb", [P, 2, D]), "g_b": sb("g_b_sb", [P, 2]), "conv_w": sb("conv_w_sb", [P, 4]),
                  "conv_b": sb("conv_b_sb", [P, 1]), "ln_g": sb("ln_g_sb", [P, D]),
                  "ln_b": sb("ln_b_sb", [P, D]), "loaded": sem("loaded_osc"), "count": 9}
            with ExitStack() as tctx:
                sync, pool_part, vector_part, scalar_part = oscillator_tables(nc, a, tabs, power_rows, tctx)
                with nc.Block() as blk:
                    @blk.sync
                    def _(sp):
                        for n in ("qk", "v", "g", "o", "conv_w"):
                            sp.dma_start(ow[n][:], a["o_" + n]).then_inc(ow["loaded"], 16)
                        sp.dma_start(ow["g_b"][:], a["o_g_b"]) \
                          .then_inc(ow["loaded"], 16)
                        sp.dma_start(ow["conv_b"][:], a["o_conv_b"].rearrange("(p o) -> p o", o=1)) \
                          .then_inc(ow["loaded"], 16)
                        for n in ("ln_g", "ln_b"):
                            sp.dma_start(ow[n][:], a["o_" + n].partition_broadcast(P)) \
                              .then_inc(ow["loaded"], 16)
                        sync(sp)

                    blk.gpsimd(pool_part)
                    blk.vector(vector_part)
                    blk.scalar(scalar_part)
            oscillator(nc, a, xin, eye, banks, ow, tabs)
        if upto >= 3:
            ffn(nc, 1, xin, ffn_w, rows_in, rows_out, eye, route, banks, loaded_ffn, ffn_sems)
        store = sem("store")
        with nc.Block() as blk:
            @blk.sync
            def _(sp):
                sp.dma_start(outs.rearrange("b (c p) d -> p (b c) d", p=P), xin[:]).then_inc(store, 16)
                sp.wait_ge(store, 16)


def rsqrt_steps(eng, v, y, tmp, chain, count, done, out, between=()):
    between = list(between)
    n = [count]

    def link(ins):
        n[0] = n[0] + 1
        ins.then_inc(chain, 1)
        if between:
            between.pop(0)()
        eng.wait_ge(chain, n[0])

    link(eng.tensor_scalar(y.bitcast(I32), v.bitcast(I32), -0.5, MAGIC, ALU.mult, ALU.add))
    for shift in (3.0, 12.0, 768.0):
        link(eng.tensor_tensor(tmp, y, y, ALU.mult))
        link(eng.tensor_tensor(tmp, tmp, v, ALU.mult))
        link(eng.scalar_tensor_tensor(out=y, in0=tmp, scalar=shift, in1=y,
                                      op0=ALU.subtract, op1=ALU.mult))
    for work in between:
        work()
    eng.tensor_scalar(out, y, -1.0 / 8192.0, None, ALU.mult).then_inc(done, 1)


RS_LINKS = 10


def retention(nc, a, xin, resid, consts, small, banks, loaded_x, loaded_small, ffn_w, rows_in,
              loaded_ffn):
    eye, causal, block, headmask, decay = consts
    ctx = ExitStack()
    with ctx:
        def sb(name, shape, dt=F32):
            return ctx.enter_context(nc.sbuf_tensor(name, shape, dt))

        def sem(name):
            return ctx.enter_context(nc.semaphore(name))

        wqkvg = sb("wqkvg", [P, LAYERS, 4, D])
        wo = sb("wo", [P, LAYERS, D])
        w1 = sb("w1", [P, LAYERS, FA])
        w2 = sb("w2", [P, LAYERS, 2, D])
        rot = sb("rot", [P, 2, NCH, 256])
        lnsb = sb("lnsb", [P, 2])
        gns = sb("gns", [P, LAYERS, D])
        gnb = sb("gnb", [P, LAYERS, D])

        stats = sb("stats", [P, 4, 6])
        mv = sb("mv", [P, 4, 2])
        vv = sb("vv", [P, 20])
        vy = sb("vy", [P, 20])
        vt = sb("vt", [P, 20])
        rs = sb("rs", [P, 20])
        stats0 = sb("stats0", [P, NCH, 6])
        mv0 = sb("mv0", [P, NCH, 2])
        v0 = sb("v0", [P, NCH])
        y0 = sb("y0", [P, NCH])
        t0 = sb("t0", [P, NCH])
        rs0 = sb("rs0", [P, NCH])

        xz = sb("xz", [P, 4, D])
        xzT = sb("xzT", [P, 4, P])
        cosq = sb("cosq", [P, 2, 256])
        sinq = sb("sinq", [P, 2, 256])
        qk = sb("qk", [P, 2, 2, 2, D])
        qkT = sb("qkT", [P, 2, 2, 2, P])
        qexp = sb("qexp", [P, 2, 2, HEADS, P])
        ve = sb("ve", [P, 2, 2, 4, 2, 2, DH])
        th = sb("th", [P, 2, 2, D])
        gate = sb("gate", [P, 2, 2, D])
        gs = sb("gs", [P, 2, 2, D])
        gb = sb("gb", [P, 2, 2, D])
        att = sb("att", [P, 2, HEADS, P])
        state = sb("state", [P, D])
        kvm = sb("kvm", [P, D])
        yT = sb("yT", [P, 2, P])
        gsum = sb("gsum", [P, 16])
        yc = sb("yc", [P, 2, 2, D])
        sq = sb("sq", [P, 2, D])
        gyT = sb("gyT", [P, 2, P])
        h = sb("h", [P, 2, FA])
        hT = sb("hT", [P, 2, 4, P])
        zero_rows = sb("zero_rows", [P, TILES, D])

        b_qk, b_vg = banks[:, 0, :], banks[:, 1, :]
        b_att = banks[:, 2:4, :].rearrange("p b (h n) -> p (b h) n", n=P)
        b_y, b_sum, b_xz, b_t = banks[:, 4, :], banks[:, 5, :], banks[:, 6, :], banks[:, 7, :]

        s = {n: sem(n) for n in (
            "loaded_w", "zeroed", "halved", "start_chain", "start_rs", "resid_init",
            "yr_ready", "bn_stats_done", "bn_aggr_done", "x_next", "gn_sum", "yc_ready", "att_masked",
            "rot_ready", "kv_taken", "state_ready", "rs_chain", "var_ready", "rs_ready", "gate_ready",
            "xz_ready", "gy_chain", "gy_ready",
            "att_ready", "w2_ready", "y_ready", "kv_ready", "qkt_ready", "xzt_ready", "ytok_ready",
            "qk_ready", "vg_ready", "w1_ready", "gyt_ready", "wo_ready", "ht_ready",
            "hT_sb", "sq_ready", "qkT_sb", "yT_sb", "xzT_sb", "v_sb", "gyT_sb", "h_sb",
            "gsb_ready", "rot_sum", "qexp_ready")}
        N_W = 8

        def pair(t, g):
            p2 = (g & (GROUPS - 1)) * 2
            return t[:, bass.ds(p2, 2), :]

        def layer(g):
            return (g >> 3) & (LAYERS - 1)

        LAG = 5
        PRO = 8

        def run(step):
            def go(eng):
                for t in range(PRO):
                    step(t, t % 2, lambda lag: t - lag >= 0)
                with eng.Fori(PRO // 2, STEPS // 2, 1) as k:
                    for u in range(2):
                        step(k * 2 + u, u, lambda lag: True)
                for t in range(STEPS, STEPS + LAG):
                    step(t, t % 2, lambda lag: t - lag < STEPS)
            return go

        with nc.Block() as blk:
            @blk.sync
            def _(sp):
                sp.dma_start(xin[:], a["X"].rearrange("b (c p) d -> p (b c) d", p=P)).then_inc(loaded_x, 16)
                sp.dma_start(small[:], a["small"]).then_inc(loaded_small, 16)
                for n, name in enumerate(("Wq", "Wk", "Wv", "Wg")):
                    sp.dma_start(wqkvg[:, :, n, :], a[name].rearrange("l c d -> c l d")).then_inc(s["loaded_w"], 16)
                sp.dma_start(rot[:], a["rot"]).then_inc(s["loaded_w"], 16)
                sp.dma_start(wo[:], a["Wo"].rearrange("l c d -> c l d")).then_inc(s["loaded_w"], 16)
                sp.dma_start(w1[:], a["W1"].rearrange("l c f -> c l f")).then_inc(s["loaded_w"], 16)
                sp.dma_start(w2[:], a["W2"].rearrange("l (f c) d -> c l f d", c=P)).then_inc(s["loaded_w"], 16)
                sp.dma_start(ffn_w["gate"][:], a["gateT"]).then_inc(loaded_ffn, 16)
                sp.dma_start(ffn_w["s_gu"][:], a["s_gu"]).then_inc(loaded_ffn, 16)
                sp.dma_start(ffn_w["s_down"][:], a["s_down"]).then_inc(loaded_ffn, 16)
                sp.dma_start(ffn_w["r_gu"][:], a["r_gu"]).then_inc(loaded_ffn, 16)
                sp.dma_start(ffn_w["r_down"][:], a["r_down"]).then_inc(loaded_ffn, 16)
                sp.wait_ge(s["zeroed"], 3)
                sp.dma_start(rows_in.rearrange("(j p) d -> p j d", p=P), zero_rows[:]).then_inc(loaded_ffn, 16)

            @blk.scalar
            def _(act):
                for dst, name in ((gns, "gn_scale"), (gnb, "gn_bias")):
                    act.dma_start(dst[:], a[name].partition_broadcast(P)).then_inc(s["loaded_w"], 16)
                act.dma_start(lnsb[:, 0:1], a["ln_scale"].rearrange("(c o) -> c o", o=1)).then_inc(s["loaded_w"], 16)
                act.dma_start(lnsb[:, 1:2], a["ln_bias"].rearrange("(c o) -> c o", o=1)).then_inc(s["loaded_w"], 16)
                act.wait_ge(s["loaded_w"], 16 * (N_W + 4))

                def step(t, u, on):
                    if on(5):
                        g, v = t - 5, (u + 1) % 2
                        wait(act, s["ht_ready"], g + 1)
                        wait(act, s["w2_ready"], g - 1)
                        act.activation(hT[:, v].rearrange("p a b -> p (a b)"), b_t, ACT.Copy) \
                           .then_inc(s["hT_sb"], 1)
                    if on(3):
                        g, v = t - 3, (u + 1) % 2
                        wait(act, s["yc_ready"], g + 1)
                        wait(act, s["var_ready"], g)
                        act.activation(sq[:], yc[:, v], ACT.Square).then_inc(s["sq_ready"], 1)
                    if on(1):
                        g, v = t - 1, (u + 1) % 2
                        wait(act, s["qkt_ready"], g + 1)
                        wait(act, s["y_ready"], 2 * (g - 1))
                        act.activation(qkT[:, v].rearrange("p a b c -> p (a b c)"), b_t, ACT.Copy) \
                           .then_inc(s["qkT_sb"], 1)
                    if on(2):
                        g = t - 2
                        wait(act, s["y_ready"], 2 * g + 2)
                        wait(act, s["ytok_ready"], g)
                        act.activation(yT[:].rearrange("p a b -> p (a b)"), b_y[:, 0:256], ACT.Copy) \
                           .then_inc(s["yT_sb"], 1)
                    lo, hi = (0 if on(0) else 2), (4 if on(4) else 2)
                    if hi > lo:
                        wait(act, s["xzt_ready"], t + 1)
                        wait(act, s["w1_ready"], t - 4)
                        wait(act, s["vg_ready"], t if isinstance(t, int) and t <= STEPS else
                             (STEPS if isinstance(t, int) else t))
                        act.activation(xzT[:, lo:hi].rearrange("p a b -> p (a b)"),
                                       b_xz[:, lo * P:hi * P], ACT.Identity,
                                       scale=lnsb[:, 0:1], bias=lnsb[:, 1:2]).then_inc(s["xzT_sb"], 1)
                    if on(0):
                        g, v = t, u
                        wait(act, s["vg_ready"], g + 1)
                        wait(act, s["y_ready"], 2 * (g - 1))
                        wait(act, s["kv_ready"], 2 * (g - 1))
                        wait(act, s["gate_ready"], g - 1)
                        vg = b_vg.rearrange("p (c a j d) -> p c a j d", c=2, a=16, j=1)
                        for c in range(2):
                            src = b_vg[:, 256 * c:256 * c + D].rearrange("p (q j d) -> p q j d", q=4, j=2)
                            dst = ve[:, v, c].rearrange("p q e j d -> p q (e j) d")[:, :, 0:4:3, :]
                            act.activation(dst, src, ACT.Copy)
                        act.activation(th[:, v], b_vg.rearrange("p (c a d) -> p c a d", c=2, a=2)[:, :, 1, :],
                                       ACT.Tanh, scale=0.5).then_inc(s["v_sb"], 1)
                    if on(3):
                        g = t - 3
                        wait(act, s["gyt_ready"], g + 1)
                        wait(act, s["wo_ready"], g)
                        act.activation(gyT[:].rearrange("p a b -> p (a b)"), b_xz[:, 0:256], ACT.Copy) \
                           .then_inc(s["gyT_sb"], 1)
                    if on(4):
                        g = t - 4
                        wait(act, s["w1_ready"], g + 1)
                        wait(act, s["ht_ready"], g)
                        act.activation(h[:].rearrange("p a b -> p (a b)"), b_t, ACT.Gelu_apprx_tanh) \
                           .then_inc(s["h_sb"], 1)

                run(step)(act)

            @blk.gpsimd
            def _(pool):
                pool.memset(ve[:], 0.0).then_inc(s["zeroed"], 1)
                pool.memset(state[:], 0.0).then_inc(s["zeroed"], 1)
                pool.memset(zero_rows[:], 0.0).then_inc(s["zeroed"], 1)
                pool.wait_ge(s["loaded_w"], 16 * (N_W + 4))
                pool.wait_ge(loaded_small, 16)
                pool.tensor_scalar(gns[:], gns[:], 0.5, None, ALU.mult).then_inc(s["halved"], 1)
                pool.tensor_scalar(gnb[:], gnb[:], 0.5, None, ALU.mult).then_inc(s["halved"], 1)
                pool.wait_ge(s["halved"], 2)

                def step(t, u, on):
                    if on(2):
                        g, v = t - 2, u
                        wait(pool, s["gate_ready"], g + 1)
                        wait(pool, s["gy_ready"], g - 1)
                        for dst, tab in ((gs, gns), (gb, gnb)):
                            row = spread(tab[:, bass.ds(layer(g), 1), :], 1, 2)
                            ins = pool.tensor_tensor(dst[:, v], gate[:, v], row, ALU.mult)
                        ins.then_inc(s["gsb_ready"], 1)
                    if on(1):
                        g, v = t - 1, (u + 1) % 2
                        wait(pool, s["rot_ready"], g + 1)
                        wait(pool, s["kv_ready"], 2 * (g - 1))
                        wait(pool, s["qkt_ready"], g - 1)
                        pool.tensor_tensor(qk[:, v].rearrange("p a b c -> p (a b c)"),
                                           cosq[:].rearrange("p a b -> p (a b)"),
                                           sinq[:].rearrange("p a b -> p (a b)"), ALU.add) \
                            .then_inc(s["rot_sum"], 1)
                        wait(pool, s["qkT_sb"], g + 1)
                        wait(pool, s["att_ready"], 2 * (g - 1))
                        pool.tensor_tensor(qexp[:, v, :, 0, :], qkT[:, v, 0],
                                           spread(headmask[:, 0:1].unsqueeze(1), 1, 2).broadcast_to([P, 2, P]),
                                           ALU.mult)
                        for hd in range(1, HEADS):
                            ins = pool.tensor_scalar(qexp[:, v, :, hd, :], qkT[:, v, 0],
                                                     headmask[:, hd:hd + 1], None, ALU.mult)
                        ins.then_inc(s["qexp_ready"], 1)

                run(step)(pool)

            @blk.tensor
            def _(pe):
                pe.wait_ge(s["loaded_w"], 16 * (N_W + 4))
                pe.wait_ge(loaded_small, 16)
                pe.wait_ge(s["zeroed"], 2)

                def scores(g, v, c):
                    wait(pe, s["qexp_ready"], g + 1)
                    wait(pe, s["att_masked"], 2 * g + c)
                    for hh in range(2):
                        ins = pe.matmul(b_att[:, 4 * hh:4 * hh + 4, :], qkT[:, v, 1, c],
                                        qexp[:, v, c, 4 * hh:4 * hh + 4, :], start=True, stop=True)
                    ins.then_inc(s["att_ready"], 1)

                def outputs(g, v, c):
                    wait(pe, s["state_ready"], 2 * g + c)
                    wait(pe, s["att_masked"], 2 * g + c + 1)
                    if c == 0:
                        wait(pe, s["yc_ready"], g)
                        wait(pe, s["v_sb"], g + 1)
                    out = b_y[:, c * P:c * P + P]
                    pe.matmul(out, state[:], qkT[:, v, 0, c], start=True, stop=False, skip_group_check=True)
                    for e in range(2):
                        for q in range(4):
                            ins = pe.matmul(out[32 * q:32 * q + 32, :],
                                            ve[:, v, c, q, e].rearrange("p j d -> p (j d)"),
                                            att[:, c, 2 * q + e, :], start=False, stop=(e == 1),
                                            skip_group_check=True)
                    ins.then_inc(s["y_ready"], 1)

                def keys_values(g, v, c):
                    plain = ve[:, v, c].rearrange("p q e j d -> p q (e j) d")[:, :, 0:4:3, :]
                    pe.matmul(b_sum[:, 0:P], qk[:, v, c, 1], plain, start=True, stop=True) \
                      .then_inc(s["kv_ready"], 1)

                def step(t, u, on):
                    if on(2):
                        scores(t - 2, u, 0)
                    if on(5):
                        g, v = t - 5, (u + 1) % 2
                        wait(pe, s["hT_sb"], g + 1)
                        if on(4):
                            wait(pe, s["yr_ready"], t - 3)
                        for c in range(2):
                            for f in range(2):
                                ins = pe.matmul(b_sum[:, c * P:c * P + P], hT[:, v, 2 * c + f],
                                                w2[:, bass.ds(layer(g), 1), f, :], start=(f == 0),
                                                stop=(f == 1))
                        ins.then_inc(s["w2_ready"], 1)
                    if on(2):
                        g = t - 2
                        outputs(g, u, 0)
                        if on(5):
                            wait(pe, s["x_next"], t - 4)
                        keys_values(g, u, 0)
                        scores(g, u, 1)
                    if on(1):
                        g, v = t - 1, (u + 1) % 2
                        wait(pe, s["rot_sum"], g + 1)
                        if on(5):
                            wait(pe, s["hT_sb"], t - 4)
                        for n in range(4):
                            ins = pe.transpose(b_t[:, n * P:n * P + P], qk[:, v, n % 2, n // 2], eye)
                        ins.then_inc(s["qkt_ready"], 1)
                    if on(2):
                        g = t - 2
                        wait(pe, s["kv_taken"], 2 * g + 1)
                        keys_values(g, u, 1)
                        outputs(g, u, 1)
                    lo, hi = (0 if on(0) else 2), (4 if on(4) else 2)
                    if hi > lo:
                        wait(pe, s["xz_ready"], t + 1)
                        if on(4):
                            wait(pe, s["gyT_sb"], t - 3)
                        for n in range(lo, hi):
                            ins = pe.transpose(b_xz[:, n * P:n * P + P], xz[:, n], eye)
                        ins.then_inc(s["xzt_ready"], 1)
                    if on(2):
                        g = t - 2
                        wait(pe, s["yT_sb"], g + 1)
                        for c in range(2):
                            ins = pe.transpose(b_y[:, c * P:c * P + P], yT[:, c], eye)
                        ins.then_inc(s["ytok_ready"], 1)
                    if hi > lo:
                        wait(pe, s["xzT_sb"], t + 1)
                    if on(0):
                        g = t
                        wait(pe, s["rot_ready"], g)
                        wait(pe, s["gate_ready"], g)
                        for n, (bank, done) in enumerate(((b_qk, "qk_ready"), (b_vg, "vg_ready"))):
                            for c in range(2):
                                ins = pe.matmul(bank[:, 256 * c:256 * c + 256], xzT[:, c],
                                                wqkvg[:, bass.ds(layer(g), 1), 2 * n:2 * n + 2, :],
                                                start=True, stop=True)
                            ins.then_inc(s[done], 1)
                    if on(4):
                        g = t - 4
                        if on(1):
                            wait(pe, s["qkT_sb"], t)
                        for c in range(2):
                            ins = pe.matmul(b_t[:, 256 * c:256 * c + 256], xzT[:, 2 + c],
                                            w1[:, bass.ds(layer(g), 1), :], start=True, stop=True)
                        ins.then_inc(s["w1_ready"], 1)
                    if on(3):
                        g, v = t - 3, (u + 1) % 2
                        wait(pe, s["gy_ready"], g + 1)
                        for c in range(2):
                            ins = pe.transpose(b_xz[:, c * P:c * P + P], yc[:, v, c], eye)
                        ins.then_inc(s["gyt_ready"], 1)
                        wait(pe, s["gyT_sb"], g + 1)
                        if on(2):
                            wait(pe, s["kv_taken"], 2 * (t - 1))
                        for c in range(2):
                            ins = pe.matmul(b_sum[:, c * P:c * P + P], gyT[:, c],
                                            wo[:, bass.ds(layer(g), 1), :], start=True, stop=True)
                        ins.then_inc(s["wo_ready"], 1)
                    if on(4):
                        g = t - 4
                        wait(pe, s["h_sb"], g + 1)
                        for n in range(4):
                            ins = pe.transpose(b_t[:, n * P:n * P + P],
                                               h[:, n // 2, (n % 2) * P:(n % 2) * P + P], eye)
                        ins.then_inc(s["ht_ready"], 1)

                run(step)(pe)

            @blk.vector
            def _(dve):
                dve.memset(mv[:], 1.0).then_inc(s["start_chain"], 1)
                dve.memset(vv[:], 1.0).then_inc(s["start_chain"], 1)
                dve.wait_ge(loaded_x, 16)
                dve.wait_ge(loaded_small, 16)
                dve.wait_ge(s["start_chain"], 2)
                for c in range(NCH):
                    dve.bn_stats(stats0[:, c], xin[:, c]).then_inc(s["start_chain"], 1)
                for c in range(NCH):
                    dve.wait_ge(s["start_chain"], 3 + c)
                    dve.bn_aggr(mv0[:, c], stats0[:, c]).then_inc(s["start_rs"], 1)
                dve.wait_ge(s["start_rs"], NCH)
                dve.tensor_scalar(v0[:], mv0[:, :, 1], EPS, None, ALU.add).then_inc(s["start_rs"], 1)
                dve.wait_ge(s["start_rs"], NCH + 1)
                rsqrt_steps(dve, v0[:], y0[:], t0[:], s["start_chain"], NCH + 2, s["start_rs"], rs0[:])
                dve.wait_ge(s["start_rs"], NCH + 2)
                for c in range(NCH):
                    dve.tensor_scalar(resid[:, c], xin[:, c], mv0[:, c, 0:1], rs0[:, c:c + 1],
                                      ALU.subtract, ALU.mult).then_inc(s["resid_init"], 1)
                dve.wait_ge(s["loaded_w"], 16 * (N_W + 4))
                dve.wait_ge(s["resid_init"], NCH)
                dve.wait_ge(s["zeroed"], 2)

                def masked(g, c):
                    wait(dve, s["att_ready"], 2 * g + c + 1)
                    wait(dve, s["y_ready"], 2 * g + c - 1)
                    dve.tensor_tensor(att[:, c], b_att, spread(causal.unsqueeze(1), 1, HEADS),
                                      ALU.mult).then_inc(s["att_masked"], 1)

                def new_state(g, c):
                    wait(dve, s["kv_ready"], 2 * g + c + 1)
                    dec = decay[:, bass.ds((g & (GROUPS - 1)) * 2 + c, 1)]
                    dve.scalar_tensor_tensor(out=kvm[:], in0=b_sum[:, 0:P], scalar=dec, in1=block,
                                             op0=ALU.mult, op1=ALU.mult).then_inc(s["kv_taken"], 1)
                    wait(dve, s["kv_taken"], 2 * g + c + 1)
                    wait(dve, s["y_ready"], 2 * g + c + 1)
                    dve.scalar_tensor_tensor(out=state[:], in0=state[:], scalar=dec, in1=kvm[:],
                                             op0=ALU.mult, op1=ALU.add).then_inc(s["state_ready"], 1)

                def step(t, u, on):
                    lo, hi = (0 if on(0) else 2), (4 if on(4) else 2)
                    if on(0):
                        wait(dve, s["x_next"], t - 7)
                    if on(4):
                        g = t - 4
                        x2 = pair(resid, g)
                        wait(dve, s["wo_ready"], g + 1)
                        dve.tensor_tensor(x2, b_sum[:, 0:256].rearrange("p (c d) -> p c d", c=2), x2,
                                          ALU.add).then_inc(s["yr_ready"], 1)
                    if on(0):
                        for c in range(2):
                            ins = dve.bn_stats(stats[:, c], resid[:, bass.ds((t & 7) * 2 + c, 1), :])
                    if on(3):
                        wait(dve, s["ytok_ready"], t - 2)
                        if on(4):
                            wait(dve, s["yr_ready"], t - 3)
                        y = b_y[:, 0:256].rearrange("p (a d) -> p a d", d=DH)
                        dve.tensor_reduce(gsum[:], y, AX.X, ALU.add).then_inc(s["gn_sum"], 1)
                    if on(4):
                        if not on(3):
                            wait(dve, s["yr_ready"], t - 3)
                        for c in range(2):
                            ins = dve.bn_stats(stats[:, 2 + c],
                                               resid[:, bass.ds(((t - 4) & 7) * 2 + c, 1), :])
                    if hi > lo:
                        ins.then_inc(s["bn_stats_done"], 1)
                        wait(dve, s["bn_stats_done"], t + 1)
                    if on(3):
                        g, v = t - 3, (u + 1) % 2
                        wait(dve, s["gyt_ready"], g - 1)
                        wait(dve, s["gn_sum"], g + 1)
                        dve.scalar_tensor_tensor(
                            out=yc[:, v].rearrange("p c (a d) -> p (c a) d", d=DH),
                            in0=spread(gsum[:].unsqueeze(2), 2, DH),
                            scalar=-1.0 / DH, in1=y, op0=ALU.mult, op1=ALU.add).then_inc(s["yc_ready"], 1)
                    if hi > lo:
                        for n in range(lo, hi):
                            ins = dve.bn_aggr(mv[:, n], stats[:, n])
                        ins.then_inc(s["bn_aggr_done"], 1)
                    if on(2):
                        masked(t - 2, 0)
                    if on(5):
                        g = t - 5
                        wait(dve, s["w2_ready"], g + 1)
                        x0 = pair(resid, g)
                        dve.tensor_tensor(x0, b_sum[:, 0:256].rearrange("p (c d) -> p c d", c=2), x0,
                                          ALU.add).then_inc(s["x_next"], 1)
                    if on(1):
                        g, v = t - 1, (u + 1) % 2
                        wait(dve, s["qk_ready"], g + 1)
                        wait(dve, s["rot_sum"], g)
                        p2 = (g & (GROUPS - 1)) * 2
                        dve.tensor_tensor(cosq[:], b_qk.rearrange("p (c n) -> p c n", c=2),
                                          rot[:, 0, bass.ds(p2, 2), :], ALU.mult)
                        other = b_qk.rearrange("p (n e) -> p n e", e=2)[:, :, ::-1]
                        dve.tensor_tensor(
                            sinq[:].rearrange("p c (n e) -> p (c n) e", e=2), other,
                            rot[:, 1].rearrange("p c (n e) -> p (c n) e", e=2)[:, bass.ds(p2 * P, 256), :],
                            ALU.mult).then_inc(s["rot_ready"], 1)
                    wait(dve, s["bn_aggr_done"], t + 1 if hi > lo else t)
                    if on(3):
                        g = t - 3
                        wait(dve, s["sq_ready"], g + 1)
                        dve.tensor_reduce(vv[:, 4:20], sq[:].rearrange("p c (a d) -> p (c a) d", d=DH),
                                          AX.X, ALU.add).then_inc(s["var_ready"], 1)
                        wait(dve, s["var_ready"], g + 1)
                    chain = RS_LINKS + 2
                    dve.tensor_scalar(vv[:, 0:4], mv[:, :, 1], EPS, None, ALU.add) \
                       .then_inc(s["rs_chain"], 1)
                    dve.tensor_scalar(vv[:, 4:20], vv[:, 4:20], 1.0 / DH, EPS, ALU.mult, ALU.add) \
                       .then_inc(s["rs_chain"], 1)
                    dve.wait_ge(s["rs_chain"], chain * t + 2)
                    work = []
                    if on(2):
                        work.append(lambda: new_state(t - 2, 0))
                    if on(1):
                        def gates():
                            g, v = t - 1, (u + 1) % 2
                            wait(dve, s["v_sb"], g + 1)
                            wait(dve, s["gsb_ready"], g - 1)
                            dve.scalar_tensor_tensor(
                                out=gate[:, v], in0=th[:, v], scalar=1.0,
                                in1=b_vg.rearrange("p (c a d) -> p c a d", c=2, a=2)[:, :, 1, :],
                                op0=ALU.add, op1=ALU.mult).then_inc(s["gate_ready"], 1)
                        work.append(gates)
                    if on(2):
                        work.append(lambda: masked(t - 2, 1))
                    rsqrt_steps(dve, vv[:], vy[:], vt[:], s["rs_chain"], chain * t + 2,
                                s["rs_ready"], rs[:], work)
                    dve.wait_ge(s["rs_ready"], t + 1)
                    if hi > lo:
                        wait(dve, s["xzt_ready"], t)
                    norms = []
                    for n in range(lo, hi):
                        g = t if n < 2 else t - 4
                        norms.append((n, resid[:, bass.ds((g & 7) * 2 + n % 2, 1), :]))

                    def norm():
                        if norms:
                            n, src = norms.pop(0)
                            ins = dve.tensor_scalar(xz[:, n], src, mv[:, n, 0:1], rs[:, n:n + 1],
                                                    ALU.subtract, ALU.mult)
                            if not norms:
                                ins.then_inc(s["xz_ready"], 1)
                    norm()
                    norm()
                    if on(3):
                        g, v = t - 3, (u + 1) % 2
                        y = yc[:, v].rearrange("p c (a d) -> p (c a) d", d=DH)
                        dve.tensor_tensor(y, y, spread(rs[:, 4:20].unsqueeze(2), 2, DH), ALU.mult).then_inc(s["gy_chain"], 1)
                        norm()
                        norm()
                        wait(dve, s["gsb_ready"], g + 1)
                        wait(dve, s["gy_chain"], 2 * g + 1)
                        dve.tensor_tensor(yc[:, v], yc[:, v], gs[:, v], ALU.mult).then_inc(s["gy_chain"], 1)
                        wait(dve, s["gy_chain"], 2 * g + 2)
                        dve.tensor_tensor(yc[:, v], yc[:, v], gb[:, v], ALU.add).then_inc(s["gy_ready"], 1)
                    else:
                        norm()
                        norm()
                    if on(2):
                        new_state(t - 2, 1)

                run(step)(dve)

                dve.wait_ge(s["x_next"], STEPS)
                dve.tensor_tensor(xin[:], xin[:], resid[:], ALU.add)


RING = 4


def ffn_semaphores(nc, ctx):
    names = ("ones_set", "stats_done", "aggr_done", "rs_chain", "rs_ready", "xn_ready", "xnT_psum",
             "xnT_ready", "logits_ready", "route_chain", "hot_ready", "ranks_ready", "slot_ready",
             "expert_ready", "top_ready", "score_tanh", "xs_ready", "up_ready", "gate_silu", "hs_ready",
             "shared_ready", "shared_added", "scattered", "xt_psum", "xtT_ready",
             "gu_ready", "silr_ready", "hr_ready", "hrt_psum", "hrT_ready", "y_psum", "yt_ready",
             "gathered")
    one = {n: ctx.enter_context(nc.semaphore("ffn_" + n)) for n in names}
    ring = {n: [ctx.enter_context(nc.semaphore(f"ffn_{n}{r}")) for r in range(RING)]
            for n in ("x_loaded", "stored")}
    return {"one": one, **ring}


def clear_ffn_semaphores(nc, sems):
    with nc.Block() as blk:
        @blk.gpsimd
        def _(pool):
            for name, one in sems["one"].items():
                if name not in ("scattered", "gathered"):
                    pool.sem_clear(one)
            for one in sems["x_loaded"] + sems["stored"]:
                pool.sem_clear(one)


def ffn(nc, call, x, w, rows_in, rows_out, eye, route, banks, loaded_ffn, sems):
    BLK = 4
    ctx = ExitStack()
    with ctx:
        def sb(name, shape, dt=F32):
            return ctx.enter_context(nc.sbuf_tensor(f"ffn{call}_{name}", shape, dt))

        stats = sb("stats", [P, NCH, 6])
        mv = sb("mv", [P, NCH, 2])
        var, vy, vt, rs = (sb(n, [P, NCH]) for n in ("var", "vy", "vt", "rs"))
        xn = sb("xn", [P, NCH, D])
        xnT = sb("xnT", [P, NCH, P])
        top_logit = sb("top_logit", [P, NCH])
        tied = sb("tied", [P, NCH, EXPERTS])
        first = sb("first", [P, NCH])
        hot = sb("hot", [P, EXPERTS, NCH])
        upto = sb("upto", [P, EXPERTS, NCH])
        place = sb("place", [P, EXPERTS, NCH])
        ntiles, tiles_upto, tiles_before, all_one = (sb(n, [P, EXPERTS]) for n in
                                                     ("ntiles", "tiles_upto", "tiles_before", "all_one"))
        slot_f = sb("slot_f", [P, NCH])
        slot = sb("slot", [P, NCH], mybir.dt.uint32)
        past = sb("past", [P, TILES, EXPERTS])
        expert_f = sb("expert_f", [P, TILES])
        expert_of = sb("expert_of", [P, TILES], I32)
        score = sb("score", [P, NCH])
        xs = sb("xs", [P, NCH, D])
        sil = sb("sil", [P, 2, 512])
        hs = sb("hs", [P, 2, 2, 512])
        s, x_loaded, stored = sems["one"], sems["x_loaded"], sems["stored"]
        xt = sb("xt", [P, RING, D])
        xtT = sb("xtT", [P, 2, P])
        silr = sb("silr", [P, 2, FE])
        hr = sb("hr", [P, 2, FE])
        hrT = sb("hrT", [P, 2, 2, P])
        yt = sb("yt", [P, RING, D])
        yg = sb("yg", [P, NCH, D])

        LAG = 4
        PRO, UN = 8, 4

        def run(step):
            def go(eng):
                for t in range(PRO):
                    step(t, t % UN, t // UN, lambda lag: t - lag >= 0)
                with eng.Fori(PRO // UN, TILES // UN, 1) as k:
                    for u in range(UN):
                        step(k * UN + u, u, k, lambda lag: True)
                for t in range(TILES, TILES + LAG):
                    step(t, t % UN, t // UN, lambda lag: t - lag < TILES)
            return go

        with nc.Block() as blk:
            @blk.sync
            def _(sp):
                sp.wait_ge(s["scattered"], 16 * NCH * (call + 1))

                def step(t, u, k, on):
                    if on(0):
                        wait(sp, s["xt_psum"], t - RING + 1)
                        if isinstance(t, int):
                            row = t * P
                            src = rows_in[row:row + P, :]
                        else:
                            src = rows_in[bass.ds(t * P, P), :]
                        sp.dma_start(xt[:, u], src).then_inc(x_loaded[u], 16)
                run(step)(sp)

            @blk.gpsimd
            def _(pool):
                pool.memset(all_one[:], 1.0).then_inc(s["ones_set"], 1)
                pool.wait_ge(s["slot_ready"], 1)
                pool.wait_ge(s["xs_ready"], 1)
                pool.wait_ge(loaded_ffn, 16 * 6)
                for c in range(NCH):
                    pool.indirect_dma_start(
                        rows_in, bass.IndirectOffsetOnAxis(ap=slot[:, c:c + 1], axis=0),
                        xs[:, c], None).then_inc(s["scattered"], 16)
                for r in range(RING):
                    pool.wait_ge(stored[r], 16 * TILES // RING)
                for c in range(NCH):
                    pool.indirect_dma_start(
                        yg[:, c], None, rows_out,
                        bass.IndirectOffsetOnAxis(ap=slot[:, c:c + 1], axis=0)).then_inc(s["gathered"], 16)

            @blk.scalar
            def _(act):
                for b in range(NCH // 4):
                    act.wait_ge(s["xnT_psum"], b + 1)
                    act.activation(xnT[:, 4 * b:4 * b + 4].rearrange("p a b -> p (a b)"), banks[:, b, :],
                                   ACT.Copy).then_inc(s["xnT_ready"], 1)
                act.wait_ge(s["top_ready"], 1)
                act.activation(score[:], top_logit[:], ACT.Tanh, scale=0.5).then_inc(s["score_tanh"], 1)
                for b in range(NCH // BLK):
                    act.wait_ge(s["up_ready"], b + 1)
                    wait(act, s["hs_ready"], b)
                    act.activation(sil[:].rearrange("p a b -> p (a b)"),
                                   banks[:, 0:2, :].rearrange("p a b -> p (a b)"), ACT.Silu) \
                       .then_inc(s["gate_silu"], 1)

                def step(t, u, k, on):
                    if on(0):
                        v = u % 2
                        act.wait_ge(s["xt_psum"], t + 1)
                        wait(act, s["gu_ready"], t - 1)
                        act.activation(xtT[:, v], banks[:, v, 0:P], ACT.Copy).then_inc(s["xtT_ready"], 1)
                    if on(1):
                        j, v = t - 1, (u + 1) % 2
                        wait(act, s["gu_ready"], j + 1)
                        wait(act, s["hr_ready"], j - 1)
                        act.activation(silr[:, v], banks[:, 2 + v, 0:FE], ACT.Silu) \
                           .then_inc(s["silr_ready"], 1)
                    if on(2):
                        j, v = t - 2, u % 2
                        wait(act, s["hrt_psum"], j + 1)
                        wait(act, s["y_psum"], j - 1)
                        act.activation(hrT[:, v].rearrange("p a b -> p (a b)"), banks[:, 4 + v, 0:2 * P],
                                       ACT.Copy).then_inc(s["hrT_ready"], 1)
                    if on(4):
                        j = t - 4
                        wait(act, s["yt_ready"], j + 1)
                        dst = rows_out[j * P:j * P + P, :] if isinstance(j, int) else \
                            rows_out[bass.ds(j * P, P), :]
                        act.dma_start(dst, yt[:, u]).then_inc(stored[u], 16)
                run(step)(act)

            @blk.tensor
            def _(pe):
                pe.wait_ge(loaded_ffn, 16 * 6)
                for b in range(NCH // 4):
                    pe.wait_ge(s["xn_ready"], 4 * b + 4)
                    for c in range(4 * b, 4 * b + 4):
                        ins = pe.transpose(banks[:, b, (c % 4) * P:(c % 4) * P + P], xn[:, c], eye)
                    ins.then_inc(s["xnT_psum"], 1)
                for c in range(NCH):
                    pe.wait_ge(s["xnT_ready"], c // 4 + 1)
                    ins = pe.matmul(banks[:, 4, c * EXPERTS:(c + 1) * EXPERTS], xnT[:, c], w["gate"][:],
                                    start=True, stop=True)
                ins.then_inc(s["logits_ready"], 1)

                def shared_up(b):
                    pe.wait_ge(s["xnT_ready"], NCH // 4)
                    wait(pe, s["hs_ready"], b)
                    rhs = xnT[:, BLK * b:BLK * b + BLK].rearrange("p a b -> p (a b)")
                    for n in range(4):
                        ins = pe.matmul(banks[:, n, :], w["s_gu"][:, n], rhs, start=True, stop=True)
                    ins.then_inc(s["up_ready"], 1)

                def shared_down(b):
                    pe.wait_ge(s["hs_ready"], b + 1)
                    wait(pe, s["shared_added"], b)
                    for c in range(BLK):
                        for f in range(2):
                            ins = pe.matmul(banks[:, 6, c * P:c * P + P], hs[:, b % 2, f, c * P:c * P + P],
                                            w["s_down"][:, f], start=(f == 0), stop=(f == 1))
                    ins.then_inc(s["shared_ready"], 1)

                shared_up(0)
                pe.wait_ge(s["hot_ready"], 1)
                hot2 = hot[:].rearrange("p e c -> p (e c)")
                pe.matmul(banks[:, 5, 0:P], route["earlier"], hot2, start=True, stop=True)
                pe.matmul(banks[:, 5, P:2 * P], route["ones"], hot2, start=True, stop=True) \
                  .then_inc(s["ranks_ready"], 1)
                for b in range(NCH // BLK):
                    if b + 1 < NCH // BLK:
                        shared_up(b + 1)
                    shared_down(b)

                pe.wait_ge(s["expert_ready"], 1)
                pe.wait_ge(s["shared_added"], NCH // BLK)

                def expert(j):
                    at = expert_of[0:1, j:j + 1] if isinstance(j, int) else \
                        expert_of[0:1, bass.ds(j, 1)]
                    return pe.value_load(at, min_val=0, max_val=EXPERTS - 1)

                def step(t, u, k, on):
                    if on(0):
                        v = u % 2
                        wait(pe, x_loaded[u], k * 16 + 16)
                        wait(pe, s["xtT_ready"], t - 1)
                        pe.transpose(banks[:, v, 0:P], xt[:, u], eye).then_inc(s["xt_psum"], 1)
                    if on(1):
                        j, v = t - 1, (u + 1) % 2
                        e = expert(j)
                        wait(pe, s["xtT_ready"], j + 1)
                        wait(pe, s["hr_ready"], j - 1)
                        pe.matmul(banks[:, 2 + v, :], xtT[:, v], w["r_gu"][:, bass.ds(e, 1), :],
                                  start=True, stop=True).then_inc(s["gu_ready"], 1)
                    if on(2):
                        j, v = t - 2, u % 2
                        wait(pe, s["hr_ready"], j + 1)
                        wait(pe, s["hrT_ready"], j - 1)
                        for f in range(2):
                            ins = pe.transpose(banks[:, 4 + v, f * P:f * P + P], hr[:, v, f * P:f * P + P],
                                               eye)
                        ins.then_inc(s["hrt_psum"], 1)
                    if on(3):
                        j, v = t - 3, (u + 1) % 2
                        e = expert(j)
                        wait(pe, s["hrT_ready"], j + 1)
                        wait(pe, s["yt_ready"], j - 1)
                        for f in range(2):
                            ins = pe.matmul(banks[:, 6 + v, 0:P], hrT[:, v, f],
                                            w["r_down"][:, bass.ds(e, 1), f, :], start=(f == 0),
                                            stop=(f == 1))
                        ins.then_inc(s["y_psum"], 1)
                run(step)(pe)

            @blk.vector
            def _(dve):
                for c in range(NCH):
                    dve.bn_stats(stats[:, c], x[:, c]).then_inc(s["stats_done"], 1)
                for c in range(NCH):
                    dve.wait_ge(s["stats_done"], c + 1)
                    ins = dve.bn_aggr(mv[:, c], stats[:, c])
                ins.then_inc(s["aggr_done"], 1)
                dve.wait_ge(s["aggr_done"], 1)
                dve.tensor_scalar(var[:], mv[:, :, 1], EPS, None, ALU.add).then_inc(s["rs_chain"], 1)
                dve.wait_ge(s["rs_chain"], 1)
                rsqrt_steps(dve, var[:], vy[:], vt[:], s["rs_chain"], 1, s["rs_ready"], rs[:])
                dve.wait_ge(s["rs_ready"], 1)
                for c in range(NCH):
                    dve.tensor_scalar(xn[:, c], x[:, c], mv[:, c, 0:1], rs[:, c:c + 1],
                                      ALU.subtract, ALU.mult).then_inc(s["xn_ready"], 1)

                n = [0]

                def link(ins):
                    n[0] += 1
                    ins.then_inc(s["route_chain"], 1)
                    dve.wait_ge(s["route_chain"], n[0])

                rev = route["rev"]
                logits = banks[:, 4, 0:NCH * EXPERTS].rearrange("p (c e) -> p c e", e=EXPERTS)
                dve.wait_ge(s["logits_ready"], 1)
                dve.tensor_reduce(top_logit[:], logits, AX.X, ALU.max).then_inc(s["top_ready"], 1)
                dve.wait_ge(s["top_ready"], 1)
                link(dve.tensor_tensor(tied[:], logits, spread(top_logit[:].unsqueeze(2), 2, EXPERTS),
                                       ALU.is_equal))
                link(dve.tensor_tensor(tied[:], tied[:], spread(rev.unsqueeze(1), 1, NCH), ALU.mult))
                link(dve.tensor_reduce(first[:], tied[:], AX.X, ALU.max))
                dve.tensor_tensor(hot[:], spread(first[:].unsqueeze(1), 1, EXPERTS),
                                  spread(rev.unsqueeze(2), 2, NCH), ALU.is_equal).then_inc(s["hot_ready"], 1)

                def shared_hidden(b):
                    dve.wait_ge(s["gate_silu"], b + 1)
                    wait(dve, s["shared_ready"], b - 1)
                    dve.tensor_tensor(hs[:, b % 2], sil[:], banks[:, 2:4, :], ALU.mult) \
                       .then_inc(s["hs_ready"], 1)

                def shared_add(b):
                    dve.wait_ge(s["shared_ready"], b + 1)
                    part = x[:, BLK * b:BLK * b + BLK]
                    dve.tensor_tensor(part, part, banks[:, 6, :].rearrange("p (c d) -> p c d", c=BLK),
                                      ALU.add).then_inc(s["shared_added"], 1)

                dve.wait_ge(s["score_tanh"], 1)
                link(dve.tensor_scalar(score[:], score[:], 0.5, 0.5, ALU.mult, ALU.add))
                dve.tensor_tensor(xs[:], xn[:], spread(score[:].unsqueeze(2), 2, D), ALU.mult) \
                   .then_inc(s["xs_ready"], 1)
                shared_hidden(0)
                dve.wait_ge(s["ranks_ready"], 1)
                within, total = banks[:, 5, 0:P], banks[:, 5, P:2 * P]
                up2, pl2 = upto[:].rearrange("p e c -> p (e c)"), place[:].rearrange("p e c -> p (e c)")
                link(dve.tensor_tensor_scan(up2, route["restart"], total, 0.0, ALU.mult, ALU.add))
                link(dve.tensor_scalar(ntiles[:], upto[:, :, NCH - 1], 63.5, 1.0 / P, ALU.add, ALU.mult))
                link(dve.tensor_scalar(ntiles[:], ntiles[:], ROUND, None, ALU.add))
                link(dve.tensor_scalar(ntiles[:], ntiles[:], ROUND, None, ALU.subtract))
                dve.wait_ge(s["ones_set"], 1)
                link(dve.tensor_tensor_scan(tiles_upto[:], all_one[:], ntiles[:], 0.0, ALU.mult, ALU.add))
                link(dve.tensor_tensor(tiles_before[:], tiles_upto[:], ntiles[:], ALU.subtract))
                link(dve.tensor_tensor(pl2, up2, total, ALU.subtract))
                link(dve.tensor_tensor(pl2, pl2, within, ALU.add))
                link(dve.scalar_tensor_tensor(out=place[:], in0=spread(tiles_before[:].unsqueeze(2), 2, NCH),
                                              scalar=float(P), in1=place[:], op0=ALU.mult, op1=ALU.add))
                link(dve.tensor_tensor(place[:], place[:], hot[:], ALU.mult))
                link(dve.tensor_reduce(slot_f[:], place[:].rearrange("p e c -> p c e"), AX.X, ALU.add))
                dve.tensor_copy(slot[:], slot_f[:]).then_inc(s["slot_ready"], 1)
                link(dve.tensor_tensor(past[:], spread(route["tile_no"].unsqueeze(2), 2, EXPERTS),
                                       spread(tiles_upto[:].unsqueeze(1), 1, TILES), ALU.is_ge))
                link(dve.tensor_reduce(expert_f[:], past[:], AX.X, ALU.add))
                dve.tensor_scalar(expert_of[:], expert_f[:], float(EXPERTS - 1), None, ALU.min) \
                   .then_inc(s["expert_ready"], 1)
                for b in range(NCH // BLK):
                    if b + 1 < NCH // BLK:
                        shared_hidden(b + 1)
                    shared_add(b)

                def step(t, u, k, on):
                    if on(1):
                        j, v = t - 1, (u + 1) % 2
                        wait(dve, s["silr_ready"], j + 1)
                        wait(dve, s["hrt_psum"], j - 1)
                        dve.tensor_tensor(hr[:, v], silr[:, v], banks[:, 2 + v, FE:2 * FE], ALU.mult) \
                           .then_inc(s["hr_ready"], 1)
                    if on(3):
                        j, v, r = t - 3, (u + 1) % 2, (u + 1) % RING
                        wait(dve, s["y_psum"], j + 1)
                        wait(dve, stored[r], (k if u == UN - 1 else k - 1) * 16)
                        dve.tensor_copy(yt[:, r], banks[:, 6 + v, 0:P]).then_inc(s["yt_ready"], 1)
                run(step)(dve)
                dve.wait_ge(s["gathered"], 16 * NCH * (call + 1))
                dve.tensor_tensor(x[:], x[:], yg[:], ALU.add)


def oscillator(nc, a, x, eye, banks, w, tabs):
    NB, W = 4, T // 4
    HALF = 2
    ctx = ExitStack()
    with ctx:
        def sb(name, shape, dt=F32):
            return ctx.enter_context(nc.sbuf_tensor("osc_" + name, shape, dt))

        cos, dec, rdec = tabs["cos"], tabs["dec"], tabs["rdec"]
        stats = sb("stats", [P, NCH, 6])
        mv = sb("mv", [P, NCH, 2])
        var, vy, vt, rs = (sb(n, [P, NCH]) for n in ("var", "vy", "vt", "rs"))
        xn = sb("xn", [P, NCH, D])
        xT = sb("xT", [P, 3 + T])
        xc = sb("xc", [P, T])
        sq = sb("sq", [P, 4, 256])
        ss, sy, st, srs = (sb(n, [P, 64]) for n in ("ss", "sy", "st", "srs"))
        qn = sb("qn", [P, 4, 256])
        qT = sb("qT", [P, HALF, 1 + T])
        th = sb("th", [P, HALF, W])
        m = sb("m", [P, HALF, W])
        ak = sb("ak", [P, 2, HALF, W])
        mem = sb("mem", [P, 2, HALF, W])
        read = sb("read", [P, 2, HALF, W])
        one = sb("one", [P, W])
        ostats = sb("ostats", [P, 4, 6])
        omv = sb("omv", [P, 4, 2])
        ov, oy, ot, ors = (sb(n, [P, 4]) for n in ("ov", "oy", "ot", "ors"))
        on = sb("on", [P, 2, 4, D])

        s = {n: ctx.enter_context(nc.semaphore(f"osc_{n}")) for n in (
            "edges", "stats_done", "aggr_done", "rs_chain", "rs_ready", "xn_ready", "xt_psum", "xT_ready",
            "conv_chain", "xc_ready", "qk_ready", "sq_ready", "ss_ready", "q_chain", "q_rs", "qn_ready",
            "qt_psum", "qT_ready", "v_ready", "g_ready", "th_ready", "m_ready", "ak_ready", "kchain",
            "sum_chain", "mem_chain", "read_chain", "read_ready", "o_ready", "o_chain", "o_rs", "on_ready", "affine", "out_ready",
            "halved")}
        RL = RS_LINKS

        with nc.Block() as blk:
            @blk.gpsimd
            def _(pool):
                pool.memset(xT[:, 0:3], 0.0).then_inc(s["edges"], 1)
                pool.memset(qT[:, :, 0:1], 0.0).then_inc(s["edges"], 1)
                pool.memset(one[:], 1.0).then_inc(s["edges"], 1)
                pool.wait_ge(w["loaded"], 16 * w["count"])
                pool.tensor_scalar(w["g_b"][:], w["g_b"][:], 0.5, None, ALU.mult).then_inc(s["halved"], 1)
                pool.wait_ge(tabs["ready"], tabs["total"])

                def keys(b):
                    pool.wait_ge(s["qT_ready"], b + 1)
                    wait(pool, s["sum_chain"], b - 1)
                    blk_t = slice(W * b, W * b + W)
                    pool.tensor_tensor(ak[:, b % 2], cos[:, :, blk_t], qT[:, :, blk_t], ALU.add) \
                        .then_inc(s["kchain"], 1)
                    pool.wait_ge(s["kchain"], b + 1)
                    pool.tensor_tensor(ak[:, b % 2], ak[:, b % 2], dec[:, :, blk_t], ALU.mult) \
                        .then_inc(s["ak_ready"], 1)

                def affine(b):
                    pool.wait_ge(s["on_ready"], b + 1)
                    row = lambda n: spread(w[n][:].unsqueeze(1), 1, 4)
                    pool.tensor_tensor(on[:, b % 2], on[:, b % 2], row("ln_g"), ALU.mult) \
                        .then_inc(s["affine"], 1)
                    pool.wait_ge(s["affine"], 2 * b + 1)
                    pool.tensor_tensor(on[:, b % 2], on[:, b % 2], row("ln_b"), ALU.add) \
                        .then_inc(s["affine"], 1)
                for b in range(NB):
                    keys(b)
                    if b >= 1:
                        affine(b - 1)
                affine(NB - 1)

            @blk.scalar
            def _(act):
                act.wait_ge(s["edges"], 3)
                act.wait_ge(s["halved"], 1)
                for b in range(NB):
                    act.wait_ge(s["xt_psum"], b + 1)
                    act.activation(xT[:, 3 + W * b:3 + W * b + W], banks[:, b % 2, :], ACT.Copy) \
                       .then_inc(s["xT_ready"], 1)
                for b in range(NB):
                    act.wait_ge(s["qk_ready"], b + 1)
                    wait(act, s["ss_ready"], b)
                    act.activation(sq[:].rearrange("p a b -> p (a b)"),
                                   banks[:, 2:4, :].rearrange("p a b -> p (a b)"), ACT.Square) \
                       .then_inc(s["sq_ready"], 1)
                    act.wait_ge(s["g_ready"], b + 1)
                    wait(act, s["m_ready"], b)
                    for f in range(HALF):
                        ins = act.activation(th[:, f], banks[:, 6 + f, :], ACT.Tanh, scale=0.5,
                                             bias=w["g_b"][:, f:f + 1])
                    ins.then_inc(s["th_ready"], 1)
                    act.wait_ge(s["qt_psum"], b + 1)
                    for f in range(HALF):
                        ins = act.activation(qT[:, f, 1 + W * b:1 + W * b + W], banks[:, 2 + f, :], ACT.Copy)
                    ins.then_inc(s["qT_ready"], 1)

            @blk.tensor
            def _(pe):
                for b in range(NB):
                    pe.wait_ge(s["xn_ready"], 4 * b + 4)
                    wait(pe, s["xT_ready"], b - 1)
                    for c in range(4):
                        ins = pe.transpose(banks[:, b % 2, c * P:c * P + P], xn[:, 4 * b + c], eye)
                    ins.then_inc(s["xt_psum"], 1)
                pe.wait_ge(w["loaded"], 16 * w["count"])

                def out(b):
                    pe.wait_ge(s["read_ready"], b + 1)
                    if b == 0:
                        pe.wait_ge(s["xT_ready"], NB)
                    wait(pe, s["on_ready"], b)
                    for c in range(4):
                        for f in range(HALF):
                            ins = pe.matmul(banks[:, 1, c * P:c * P + P], read[:, b % 2, f, c * P:c * P + P],
                                            w["o"][:, f], start=(f == 0), stop=(f == 1))
                    ins.then_inc(s["o_ready"], 1)

                for b in range(NB):
                    pe.wait_ge(s["xc_ready"], b + 1)
                    wait(pe, s["qT_ready"], b)
                    for c in range(4):
                        at = W * b + c * P
                        ins = pe.matmul(banks[:, 2 + c // 2, (c % 2) * 256:(c % 2) * 256 + 256],
                                        xc[:, at:at + P], w["qk"][:], start=True, stop=True)
                    ins.then_inc(s["qk_ready"], 1)
                    rhs = xc[:, W * b:W * b + W]
                    wait(pe, s["th_ready"], b)
                    for f in range(HALF):
                        ins = pe.matmul(banks[:, 6 + f, :], w["g"][:, f], rhs, start=True, stop=True)
                    ins.then_inc(s["g_ready"], 1)
                    wait(pe, s["m_ready"], b)
                    for f in range(HALF):
                        ins = pe.matmul(banks[:, 4 + f, :], w["v"][:, f], rhs, start=True, stop=True)
                    ins.then_inc(s["v_ready"], 1)
                    pe.wait_ge(s["qn_ready"], b + 1)
                    for f in range(HALF):
                        for c in range(4):
                            ins = pe.transpose(banks[:, 2 + f, c * P:c * P + P],
                                               qn[:, c, f * P:f * P + P], eye)
                    ins.then_inc(s["qt_psum"], 1)
                    if b >= 1:
                        out(b - 1)
                out(NB - 1)

            @blk.vector
            def _(dve):
                for c in range(NCH):
                    dve.bn_stats(stats[:, c], x[:, c]).then_inc(s["stats_done"], 1)
                for c in range(NCH):
                    dve.wait_ge(s["stats_done"], c + 1)
                    ins = dve.bn_aggr(mv[:, c], stats[:, c])
                ins.then_inc(s["aggr_done"], 1)
                dve.wait_ge(s["aggr_done"], 1)
                dve.tensor_scalar(var[:], mv[:, :, 1], EPS, None, ALU.add).then_inc(s["rs_chain"], 1)
                dve.wait_ge(s["rs_chain"], 1)
                rsqrt_steps(dve, var[:], vy[:], vt[:], s["rs_chain"], 1, s["rs_ready"], rs[:])
                dve.wait_ge(s["rs_ready"], 1)
                for c in range(NCH):
                    dve.tensor_scalar(xn[:, c], x[:, c], mv[:, c, 0:1], rs[:, c:c + 1],
                                      ALU.subtract, ALU.mult).then_inc(s["xn_ready"], 1)
                dve.wait_ge(w["loaded"], 16 * w["count"])
                dve.wait_ge(tabs["ready"], tabs["total"])
                dve.wait_ge(s["edges"], 3)

                def conv(b):
                    dve.wait_ge(s["xT_ready"], b + 1)
                    dst = xc[:, W * b:W * b + W]
                    dve.tensor_scalar(dst, xT[:, 3 + W * b:3 + W * b + W], w["conv_w"][:, 3:4],
                                      w["conv_b"][:, 0:1], ALU.mult, ALU.add).then_inc(s["conv_chain"], 1)
                    for k in range(3):
                        dve.wait_ge(s["conv_chain"], 3 * b + k + 1)
                        dve.scalar_tensor_tensor(
                            out=dst, in0=xT[:, k + W * b:k + W * b + W], scalar=w["conv_w"][:, k:k + 1],
                            in1=dst, op0=ALU.mult, op1=ALU.add) \
                            .then_inc(s["conv_chain"] if k < 2 else s["xc_ready"], 1)

                def normalise(b):
                    dve.wait_ge(s["sq_ready"], b + 1)
                    dve.tensor_reduce(ss[:], sq[:].rearrange("p c (a d) -> p (c a) d", d=DH), AX.X,
                                      ALU.add).then_inc(s["ss_ready"], 1)
                    dve.wait_ge(s["ss_ready"], b + 1)
                    at = (RL + 1) * b
                    dve.tensor_scalar(ss[:], ss[:], 1e-24, None, ALU.max).then_inc(s["q_chain"], 1)
                    dve.wait_ge(s["q_chain"], at + 1)
                    rsqrt_steps(dve, ss[:], sy[:], st[:], s["q_chain"], at + 1, s["q_rs"], srs[:])
                    dve.wait_ge(s["q_rs"], b + 1)
                    wait(dve, s["qt_psum"], b)
                    for n in range(2):
                        ins = dve.tensor_tensor(
                            qn[:, 2 * n:2 * n + 2].rearrange("p c (a d) -> p (c a) d", d=DH),
                            banks[:, 2 + n, :].rearrange("p (a d) -> p a d", d=DH),
                            spread(srs[:, 32 * n:32 * n + 32].unsqueeze(2), 2, DH), ALU.mult)
                    ins.then_inc(s["qn_ready"], 1)

                def memory(b):
                    dve.wait_ge(s["th_ready"], b + 1)
                    dve.wait_ge(s["v_ready"], b + 1)
                    wait(dve, s["mem_chain"], 2 * b)
                    dve.scalar_tensor_tensor(out=m[:], in0=th[:], scalar=1.0, in1=banks[:, 4:6, :],
                                             op0=ALU.add, op1=ALU.mult).then_inc(s["m_ready"], 1)
                    dve.wait_ge(s["m_ready"], b + 1)
                    dve.wait_ge(s["ak_ready"], b + 1)
                    dve.tensor_tensor(m[:], m[:], ak[:, b % 2], ALU.mult).then_inc(s["sum_chain"], 1)
                    dve.wait_ge(s["sum_chain"], b + 1)
                    for f in range(HALF):
                        wait(dve, s["mem_chain"], 2 * b)
                        first = 0.0 if b == 0 else mem[:, (b - 1) % 2, f, W - 1:W]
                        dve.tensor_tensor_scan(mem[:, b % 2, f], one[:], m[:, f], first, ALU.mult,
                                               ALU.add).then_inc(s["mem_chain"], 1)
                    dve.wait_ge(s["mem_chain"], 2 * b + 2)
                    blk_t = slice(W * b, W * b + W)
                    wait(dve, s["o_ready"], b - 1)
                    dve.tensor_tensor(read[:, b % 2], mem[:, b % 2], rdec[:, :, blk_t], ALU.mult) \
                       .then_inc(s["read_chain"], 1)
                    dve.wait_ge(s["read_chain"], b + 1)
                    dve.tensor_tensor(read[:, b % 2], read[:, b % 2], qT[:, :, 1 + W * b:1 + W * b + W],
                                      ALU.mult).then_inc(s["read_ready"], 1)

                def norm_out(b):
                    dve.wait_ge(s["o_ready"], b + 1)
                    n = (RL + 9) * b
                    for c in range(4):
                        dve.bn_stats(ostats[:, c], banks[:, 1, c * P:c * P + P]).then_inc(s["o_chain"], 1)
                    for c in range(4):
                        dve.wait_ge(s["o_chain"], n + 1 + c)
                        dve.bn_aggr(omv[:, c], ostats[:, c]).then_inc(s["o_chain"], 1)
                    dve.wait_ge(s["o_chain"], n + 8)
                    dve.tensor_scalar(ov[:], omv[:, :, 1], EPS, None, ALU.add).then_inc(s["o_chain"], 1)
                    dve.wait_ge(s["o_chain"], n + 9)
                    rsqrt_steps(dve, ov[:], oy[:], ot[:], s["o_chain"], n + 9, s["o_rs"], ors[:])
                    dve.wait_ge(s["o_rs"], b + 1)
                    wait(dve, s["out_ready"], b - 1)
                    for c in range(4):
                        ins = dve.tensor_scalar(on[:, b % 2, c], banks[:, 1, c * P:c * P + P],
                                                omv[:, c, 0:1], ors[:, c:c + 1], ALU.subtract, ALU.mult)
                    ins.then_inc(s["on_ready"], 1)

                def add_out(b):
                    dve.wait_ge(s["affine"], 2 * b + 2)
                    part = x[:, 4 * b:4 * b + 4]
                    dve.tensor_tensor(part, part, on[:, b % 2], ALU.add).then_inc(s["out_ready"], 1)

                for b in range(NB):
                    conv(b)
                for b in range(NB):
                    normalise(b)
                    memory(b)
                    if b >= 1:
                        norm_out(b - 1)
                    if b >= 2:
                        add_out(b - 2)
                norm_out(NB - 1)
                add_out(NB - 2)
                add_out(NB - 1)


def oscillator_tables(nc, a, tabs, dram, ctx):
    def sb(name, shape, dt=F32):
        return ctx.enter_context(nc.sbuf_tensor("tab_" + name, shape, dt))

    times = sb("times", [P, T])
    freqs = sb("freqs", [P, 2])
    turns = sb("turns", [P, 2, T])
    gam = sb("gam", [16, 12])
    powers = sb("powers", [16, T])
    flat = sb("flat", [P, 256])
    rflat = sb("rflat", [P, 256])
    s = {n: ctx.enter_context(nc.semaphore("tab_" + n)) for n in (
        "loaded", "chain", "angles", "gamma", "powers_done", "powers_out", "powers_in", "inverse", "out",
        "angle_ready")}
    cos, dec, rdec = tabs["cos"], tabs["dec"], tabs["rdec"]
    two_pi = 2 * np.pi
    c1 = 6.28125
    c2 = float(np.float32(np.floor((two_pi - c1) * 2.0 ** 16) / 2.0 ** 16))
    c3 = float(np.float32(two_pi - c1 - c2))

    def sync(sp):
        sp.dma_start(times[:], a["times"].partition_broadcast(P)).then_inc(s["loaded"], 16)
        sp.dma_start(freqs[:], a["freqs"]).then_inc(s["loaded"], 16)
        sp.dma_start(gam[:, 0:1], a["gamma"].rearrange("h a b -> h (a b)")).then_inc(s["loaded"], 16)
        sp.wait_ge(s["powers_done"], 12)
        sp.dma_start(dram[0], powers[:]).then_inc(s["powers_out"], 16)
        sp.wait_ge(s["powers_out"], 16)
        sp.dma_start(flat[:], dram[0].rearrange("h (b t) -> (h b) t", t=256)).then_inc(s["powers_in"], 16)
        sp.wait_ge(s["inverse"], 3)
        sp.dma_start(dram[1].rearrange("h (b t) -> (h b) t", t=256), flat[:]).then_inc(s["out"], 16)
        sp.dma_start(dram[2].rearrange("h (b t) -> (h b) t", t=256), rflat[:]).then_inc(s["out"], 16)
        sp.wait_ge(s["out"], 32)
        for n, tab in ((1, dec), (2, rdec)):
            for f in range(2):
                for h in range(8):
                    sp.dma_start(tab[16 * h:16 * h + 16, f, :],
                                 dram[n][8 * f + h, :].partition_broadcast(16)).then_inc(tabs["ready"], 16)

    def pool_part(pool):
        pool.memset(powers[:, 0:1], 1.0).then_inc(s["powers_done"], 1)
        pool.wait_ge(s["loaded"], 48)
        for k in range(11):
            pool.wait_ge(s["powers_done"], k + 1)
            n = 1 << k
            pool.tensor_scalar(powers[:, n:2 * n], powers[:, 0:n], gam[:, k:k + 1], None, ALU.mult) \
                .then_inc(s["powers_done"], 1)
            pool.tensor_tensor(gam[:, k + 1:k + 2], gam[:, k:k + 1], gam[:, k:k + 1], ALU.mult) \
                .then_inc(s["gamma"], 1)
            pool.wait_ge(s["gamma"], k + 1)

    def vector_part(dve):
        n = [0]

        def link(ins):
            n[0] += 1
            ins.then_inc(s["chain"], 1)
            dve.wait_ge(s["chain"], n[0])

        dve.wait_ge(s["loaded"], 48)
        for f in range(2):
            link(dve.tensor_scalar(cos[:, f], times[:], freqs[:, f:f + 1], None, ALU.mult))
        link(dve.tensor_scalar(turns[:], cos[:], float(np.pi / 2), 1 / two_pi, ALU.add, ALU.mult))
        link(dve.tensor_scalar(turns[:], turns[:], ROUND, None, ALU.add))
        link(dve.tensor_scalar(turns[:], turns[:], ROUND, None, ALU.subtract))
        for c in (c1, c2, c3):
            link(dve.scalar_tensor_tensor(out=cos[:], in0=turns[:], scalar=-c, in1=cos[:], op0=ALU.mult,
                                          op1=ALU.add))
        link(dve.tensor_scalar(cos[:], cos[:], float(np.pi / 2), float(np.float32(3.1415925)), ALU.add,
                               ALU.min))
        dve.tensor_scalar(cos[:], cos[:], -float(np.float32(3.1415925)), None, ALU.max) \
           .then_inc(s["angle_ready"], 1)
        dve.wait_ge(s["powers_in"], 16)
        dve.tensor_scalar(rflat[:], flat[:], 1e-6, None, ALU.add).then_inc(s["inverse"], 1)
        dve.wait_ge(s["inverse"], 1)
        dve.reciprocal(rflat[:], rflat[:]).then_inc(s["inverse"], 1)
        dve.tensor_scalar(flat[:], flat[:], 0.5, None, ALU.mult).then_inc(s["inverse"], 1)

    def scalar_part(act):
        act.wait_ge(s["angle_ready"], 1)
        act.activation(cos[:], cos[:], ACT.Sin).then_inc(tabs["ready"], 16)

    tabs["total"] = 16 * 33
    return sync, pool_part, vector_part, scalar_part


UPTO = 9
NAMES = ("X", "Wq", "Wk", "Wv", "Wg", "Wo", "W1", "W2", "ln_scale", "ln_bias", "gn_scale", "gn_bias")


def kernel(**inputs):
    import concourse.bacc as bacc
    from concourse.bass_utils import run_bass_kernel_spmd

    nc = bacc.Bacc("TRN2", target_bir_lowering=False, num_devices=1)
    inputs = {n: np.asarray(v) for n, v in inputs.items()}
    arrays = {n: np.ascontiguousarray(inputs["L0_attn_a_" + n]) for n in NAMES}
    arrays["rot"], arrays["small"] = retention_tables()
    arrays["gateT"] = np.ascontiguousarray(inputs["L0_ffn_gate_w"].T)
    sh = [np.asarray(inputs["L0_ffn_shared_" + n]) for n in ("gate", "up", "down")]
    ro = [np.asarray(inputs["L0_ffn_r_" + n]) for n in ("gate", "up", "down")]
    arrays["s_gu"] = np.ascontiguousarray(np.concatenate([sh[0], sh[1]], 0).T).reshape(D, 4, P)
    arrays["s_down"] = np.ascontiguousarray(sh[2].T.reshape(2, P, D).transpose(1, 0, 2))
    arrays["r_gu"] = np.ascontiguousarray(np.concatenate([ro[0], ro[1]], 1).transpose(2, 0, 1))
    arrays["r_down"] = np.ascontiguousarray(ro[2].transpose(0, 2, 1).reshape(EXPERTS, 2, P, D)
                                            .transpose(2, 0, 1, 3))
    b = {n: inputs["L0_attn_b_" + n] for n in ("qk_w", "v_w", "g_w", "g_b", "o_w", "conv_w", "conv_b",
                                               "ln_g", "ln_b", "freqs", "gamma")}
    arrays["o_qk"] = np.ascontiguousarray(b["qk_w"].T)
    arrays["o_v"] = np.ascontiguousarray(b["v_w"].T).reshape(D, 2, P)
    arrays["o_g"] = np.ascontiguousarray(b["g_w"].T).reshape(D, 2, P)
    arrays["o_o"] = np.ascontiguousarray(b["o_w"].T.reshape(2, P, D).transpose(1, 0, 2))
    arrays["o_conv_w"] = np.ascontiguousarray(b["conv_w"].reshape(D, 4))
    arrays["o_g_b"] = np.ascontiguousarray(b["g_b"].reshape(2, P).T)
    for n in ("conv_b", "ln_g", "ln_b"):
        arrays["o_" + n] = b[n]
    arrays["freqs"] = np.ascontiguousarray(b["freqs"].reshape(2, P).T)
    arrays["gamma"] = b["gamma"]
    arrays["times"] = np.arange(T, dtype=np.float32)
    aps = {n: nc.dram_tensor("in_" + n, v.shape, mybir.dt.from_np(v.dtype), kind="ExternalInput").ap()
           for n, v in arrays.items()}
    out = nc.dram_tensor("out", (1, T, D), F32, kind="ExternalOutput").ap()
    build(nc, aps, out, UPTO)
    r = run_bass_kernel_spmd(nc, [{"in_" + n: v for n, v in arrays.items()}], core_ids=[0])
    return r.results[0]["out"]
```

```python
from contextlib import ExitStack

import numpy as np

import concourse.bass as bass
from concourse import mybir

ALU = mybir.AluOpType
ACT = mybir.ActivationFunctionType
AX = mybir.AxisListType
F32 = mybir.dt.float32
I32 = mybir.dt.int32

P = 128
T = 2048
NCH = T // P
D = 128
LAYERS, HEADS, DH, FA = 4, 8, 16, 256
GROUPS = NCH // 2
STEPS = LAYERS * GROUPS
EPS = 1e-5
RING = 4
EXPERTS, FE = 8, 256
TILES = NCH + EXPERTS
ROUND = 12582912.0
MAGIC = float(0x5F3759DF)


def routing_tables():
    earlier = (np.arange(P)[:, None] < np.arange(P)[None, :]).astype(np.float32)
    ones = np.ones((P, P), np.float32)
    rows = [EXPERTS - np.arange(EXPERTS), np.arange(TILES),
            (np.arange(EXPERTS * NCH) % NCH != 0)]
    return np.concatenate([earlier, ones] + [np.tile(r.astype(np.float32)[None], (P, 1)) for r in rows], 1)


def retention_tables():
    gam = (np.float32(1.0) - np.exp(np.linspace(np.log(1 / 32), np.log(1 / 64), HEADS))
           .astype(np.float32)).astype(np.float64)
    inv = (np.float32(1.0) / np.power(np.float32(10000.0), np.arange(0, DH, 2, dtype=np.float32)
                                      / np.float32(DH))).astype(np.float32)
    ang = (np.arange(T, dtype=np.float32)[:, None] * inv[None, :]).astype(np.float64)
    cos, sin = np.cos(ang), np.sin(ang)
    i = np.arange(T) % P
    up = gam[None, :] ** i[:, None]
    down = gam[None, :] ** (-i[:, None].astype(np.float64))
    ct = np.zeros((T, 2, HEADS, DH // 2, 2))
    st = np.zeros((T, 2, HEADS, DH // 2, 2))
    for a, (dec, sg) in enumerate(((up, 1.0), (down, -1.0))):
        ct[:, a] = (dec[:, :, None] * cos[:, None, :])[..., None]
        st[:, a, :, :, 0] = -sg * dec[:, :, None] * sin[:, None, :]
        st[:, a, :, :, 1] = sg * dec[:, :, None] * sin[:, None, :]
    rot = np.stack([ct.reshape(NCH, P, 256), st.reshape(NCH, P, 256)], 0)
    rot = np.ascontiguousarray(rot.transpose(2, 0, 1, 3)).astype(np.float32)
    head = np.arange(D) // DH
    hm = (head[:, None] == np.arange(HEADS)[None, :]).astype(np.float32)
    block = (head[:, None] == head[None, :]).astype(np.float32)
    causal = (np.arange(P)[:, None] <= np.arange(P)[None, :]).astype(np.float32)
    dec = np.repeat((gam[head] ** P)[:, None], NCH, 1)
    dec[:, NCH - 1] = 0.0
    eye = np.eye(P, dtype=np.float32)
    small = np.concatenate([eye, causal, block, hm, dec, routing_tables()], 1).astype(np.float32)
    return rot, np.ascontiguousarray(small)


def wait(eng, sem, value):
    if isinstance(value, int) and value <= 0:
        return
    eng.wait_ge(sem, value)


def spread(ap, axis, n):
    shape = list(ap.shape)
    shape[axis] = n
    return ap.broadcast_to(shape)


def build(nc, a, outs, upto=9):
    ctx = ExitStack()
    with ctx:
        def sb(name, shape, dt=F32):
            return ctx.enter_context(nc.sbuf_tensor(name, shape, dt))

        def sem(name):
            return ctx.enter_context(nc.semaphore(name))

        xin = sb("xin", [P, NCH, D])
        resid = sb("resid", [P, NCH, D])
        small = sb("small", [P, 5 * P + HEADS + NCH + EXPERTS + TILES + EXPERTS * NCH])
        eye, causal, block = small[:, 0:P], small[:, P:2 * P], small[:, 2 * P:3 * P]
        headmask = small[:, 3 * P:3 * P + HEADS]
        decay = small[:, 3 * P + HEADS:3 * P + HEADS + NCH]
        banks = ctx.enter_context(nc.psum_tensor("banks", [P, 8, 512], F32))

        at = 3 * P + HEADS + NCH
        route = {}
        for name, n in (("earlier", P), ("ones", P), ("rev", EXPERTS), ("tile_no", TILES),
                        ("restart", EXPERTS * NCH)):
            route[name] = small[:, at:at + n]
            at += n

        ffn_w = {
            "gate": sb("gate_sb", [P, EXPERTS]),
            "s_gu": sb("s_gu_sb", [P, 4, P]),
            "s_down": sb("s_down_sb", [P, 2, D]),
            "r_gu": sb("r_gu_sb", [P, EXPERTS, 2 * FE]),
            "r_down": sb("r_down_sb", [P, EXPERTS, 2, D]),
        }
        rows_in = nc.dram_tensor("rows_in", (TILES * P, D), F32).ap()
        rows_out = nc.dram_tensor("rows_out", (TILES * P, D), F32).ap()

        ffn_sems = ffn_semaphores(nc, ctx)
        loaded_x = sem("loaded_x")
        loaded_small = sem("loaded_small")
        loaded_ffn = sem("loaded_ffn")
        retention(nc, a, xin, resid, (eye, causal, block, headmask, decay), small, banks,
                  loaded_x, loaded_small, ffn_w, rows_in, loaded_ffn)
        if upto >= 1:
            ffn(nc, 0, xin, ffn_w, rows_in, rows_out, eye, route, banks, loaded_ffn, ffn_sems)
            clear_ffn_semaphores(nc, ffn_sems)
        if upto >= 2:
            tabs = {"cos": sb("cos_tab", [P, 2, T]), "dec": sb("dec_tab", [P, 2, T]),
                    "rdec": sb("rdec_tab", [P, 2, T]), "ready": sem("tables_ready")}
            power_rows = [nc.dram_tensor(f"power_rows{n}", (16, T), F32).ap() for n in range(3)]
            ow = {"qk": sb("qk_sb", [P, 256]), "v": sb("v_sb", [P, 2, P]), "g": sb("g_sb", [P, 2, P]),
                  "o": sb("o_sb", [P, 2, D]), "g_b": sb("g_b_sb", [P, 2]), "conv_w": sb("conv_w_sb", [P, 4]),
                  "conv_b": sb("conv_b_sb", [P, 1]), "ln_g": sb("ln_g_sb", [P, D]),
                  "ln_b": sb("ln_b_sb", [P, D]), "loaded": sem("loaded_osc"), "count": 9}
            with ExitStack() as tctx:
                sync, pool_part, vector_part, scalar_part = oscillator_tables(nc, a, tabs, power_rows, tctx)
                with nc.Block() as blk:
                    @blk.sync
                    def _(sp):
                        for n in ("qk", "v", "g", "o", "conv_w"):
                            sp.dma_start(ow[n][:], a["o_" + n]).then_inc(ow["loaded"], 16)
                        sp.dma_start(ow["g_b"][:], a["o_g_b"]) \
                          .then_inc(ow["loaded"], 16)
                        sp.dma_start(ow["conv_b"][:], a["o_conv_b"].rearrange("(p o) -> p o", o=1)) \
                          .then_inc(ow["loaded"], 16)
                        for n in ("ln_g", "ln_b"):
                            sp.dma_start(ow[n][:], a["o_" + n].partition_broadcast(P)) \
                              .then_inc(ow["loaded"], 16)
                        sync(sp)

                    blk.gpsimd(pool_part)
                    blk.vector(vector_part)
                    blk.scalar(scalar_part)
            oscillator(nc, a, xin, eye, banks, ow, tabs)
        if upto >= 3:
            ffn(nc, 1, xin, ffn_w, rows_in, rows_out, eye, route, banks, loaded_ffn, ffn_sems)
        store = sem("store")
        with nc.Block() as blk:
            @blk.sync
            def _(sp):
                sp.dma_start(outs.rearrange("b (c p) d -> p (b c) d", p=P), xin[:]).then_inc(store, 16)
                sp.wait_ge(store, 16)


def rsqrt_steps(eng, v, y, tmp, chain, count, done, out, between=()):
    between = list(between)
    n = [count]

    def link(ins):
        n[0] = n[0] + 1
        ins.then_inc(chain, 1)
        if between:
            between.pop(0)()
        eng.wait_ge(chain, n[0])

    link(eng.tensor_scalar(y.bitcast(I32), v.bitcast(I32), -0.5, MAGIC, ALU.mult, ALU.add))
    for shift in (3.0, 12.0, 768.0):
        link(eng.tensor_tensor(tmp, y, y, ALU.mult))
        link(eng.tensor_tensor(tmp, tmp, v, ALU.mult))
        link(eng.scalar_tensor_tensor(out=y, in0=tmp, scalar=shift, in1=y,
                                      op0=ALU.subtract, op1=ALU.mult))
    for work in between:
        work()
    eng.tensor_scalar(out, y, -1.0 / 8192.0, None, ALU.mult).then_inc(done, 1)


RS_LINKS = 10


def retention(nc, a, xin, resid, consts, small, banks, loaded_x, loaded_small, ffn_w, rows_in,
              loaded_ffn):
    eye, causal, block, headmask, decay = consts
    ctx = ExitStack()
    with ctx:
        def sb(name, shape, dt=F32):
            return ctx.enter_context(nc.sbuf_tensor(name, shape, dt))

        def sem(name):
            return ctx.enter_context(nc.semaphore(name))

        wqkvg = sb("wqkvg", [P, LAYERS, 4, D])
        wo = sb("wo", [P, LAYERS, D])
        w1 = sb("w1", [P, LAYERS, FA])
        w2 = sb("w2", [P, LAYERS, 2, D])
        rot = sb("rot", [P, 2, NCH, 256])
        lnsb = sb("lnsb", [P, 2])
        gns = sb("gns", [P, LAYERS, D])
        gnb = sb("gnb", [P, LAYERS, D])

        stats = sb("stats", [P, 4, 6])
        mv = sb("mv", [P, 4, 2])
        vv = sb("vv", [P, 20])
        vy = sb("vy", [P, 20])
        vt = sb("vt", [P, 20])
        rs = sb("rs", [P, 20])
        stats0 = sb("stats0", [P, NCH, 6])
        mv0 = sb("mv0", [P, NCH, 2])
        v0 = sb("v0", [P, NCH])
        y0 = sb("y0", [P, NCH])
        t0 = sb("t0", [P, NCH])
        rs0 = sb("rs0", [P, NCH])

        xz = sb("xz", [P, 4, D])
        xzT = sb("xzT", [P, 4, P])
        cosq = sb("cosq", [P, 2, 256])
        sinq = sb("sinq", [P, 2, 256])
        qk = sb("qk", [P, RING, 2, 2, D])
        qkT = sb("qkT", [P, RING, 2, 2, P])
        qexp = sb("qexp", [P, 2, 2, HEADS, P])
        ve = sb("ve", [P, RING, 2, 4, 2, 2, DH])
        th = sb("th", [P, RING, 2, D])
        gate = sb("gate", [P, RING, 2, D])
        gs = sb("gs", [P, RING, 2, D])
        gb = sb("gb", [P, RING, 2, D])
        att = sb("att", [P, 2, HEADS, P])
        state = sb("state", [P, 2, D])
        kvm = sb("kvm", [P, 2, D])
        yT = sb("yT", [P, 2, P])
        gsum = sb("gsum", [P, 16])
        yc = sb("yc", [P, RING, 2, D])
        sq = sb("sq", [P, 2, D])
        gyT = sb("gyT", [P, 2, P])
        h = sb("h", [P, 2, FA])
        hT = sb("hT", [P, 4, P])
        ytok = sb("ytok", [P, 2, 2 * D])
        zero_rows = sb("zero_rows", [P, TILES, D])

        b_qk, b_vg = banks[:, 0, :], banks[:, 1, :]
        b_att = banks[:, 2:4, :].rearrange("p b (h n) -> p (b h) n", n=P)
        b_y, b_sum, b_xz, b_t = banks[:, 4, :], banks[:, 5, :], banks[:, 6, :], banks[:, 7, :]

        s = {n: sem(n) for n in (
            "loaded_w", "zeroed", "halved", "start_chain", "start_rs", "resid_init",
            "yr_ready", "bn_stats_done", "bn_aggr_done", "x_next", "gn_sum", "yc_ready", "att_masked",
            "rot_ready", "kv_taken", "state_ready", "rs_chain", "var_ready", "rs_ready", "gate_ready",
            "xz_ready", "gy_chain", "gy_ready",
            "att_ready", "w2_ready", "y_ready", "kv_ready", "qkt_ready", "xzt_ready", "ytok_ready",
            "qk_ready", "vg_ready", "w1_ready", "gyt_ready", "wo_ready", "ht_ready",
            "hT_sb", "sq_ready", "qkT_sb", "yT_sb", "xzT_sb", "v_sb", "gyT_sb", "h_sb",
            "gsb_ready", "rot_sum", "att_raw", "att_masked2", "ytok_sb", "qexp_ready", "qexp_act")}
        N_W = 8
        HALF = HEADS // 2
        ACT_HEADS = 5

        def pair(t, g):
            p2 = (g & (GROUPS - 1)) * 2
            return t[:, bass.ds(p2, 2), :]

        def layer(g):
            return (g >> 3) & (LAYERS - 1)

        LAG, PRO, UN = 7, 8, RING

        def run(step):
            def go(eng):
                for t in range(PRO):
                    step(t, t % UN, lambda n: t - n >= 0)
                with eng.Fori(PRO // UN, STEPS // UN, 1) as k:
                    for u in range(UN):
                        step(k * UN + u, u, lambda n: True)
                for t in range(STEPS, STEPS + LAG):
                    step(t, t % UN, lambda n: t - n < STEPS)
            return go

        with nc.Block() as blk:
            @blk.sync
            def _(sp):
                sp.dma_start(xin[:], a["X"].rearrange("b (c p) d -> p (b c) d", p=P)).then_inc(loaded_x, 16)
                sp.dma_start(small[:], a["small"]).then_inc(loaded_small, 16)
                for n, name in enumerate(("Wq", "Wk", "Wv", "Wg")):
                    sp.dma_start(wqkvg[:, :, n, :], a[name].rearrange("l c d -> c l d")).then_inc(s["loaded_w"], 16)
                sp.dma_start(rot[:], a["rot"]).then_inc(s["loaded_w"], 16)
                sp.dma_start(wo[:], a["Wo"].rearrange("l c d -> c l d")).then_inc(s["loaded_w"], 16)
                sp.dma_start(w1[:], a["W1"].rearrange("l c f -> c l f")).then_inc(s["loaded_w"], 16)
                sp.dma_start(w2[:], a["W2"].rearrange("l (f c) d -> c l f d", c=P)).then_inc(s["loaded_w"], 16)
                sp.dma_start(ffn_w["gate"][:], a["gateT"]).then_inc(loaded_ffn, 16)
                sp.dma_start(ffn_w["s_gu"][:], a["s_gu"]).then_inc(loaded_ffn, 16)
                sp.dma_start(ffn_w["s_down"][:], a["s_down"]).then_inc(loaded_ffn, 16)
                sp.dma_start(ffn_w["r_gu"][:], a["r_gu"]).then_inc(loaded_ffn, 16)
                sp.dma_start(ffn_w["r_down"][:], a["r_down"]).then_inc(loaded_ffn, 16)
                sp.wait_ge(s["zeroed"], 3)
                sp.dma_start(rows_in.rearrange("(j p) d -> p j d", p=P), zero_rows[:]).then_inc(loaded_ffn, 16)

            @blk.scalar
            def _(act):
                for dst, name in ((gns, "gn_scale"), (gnb, "gn_bias")):
                    act.dma_start(dst[:], a[name].partition_broadcast(P)).then_inc(s["loaded_w"], 16)
                act.dma_start(lnsb[:, 0:1], a["ln_scale"].rearrange("(c o) -> c o", o=1)).then_inc(s["loaded_w"], 16)
                act.dma_start(lnsb[:, 1:2], a["ln_bias"].rearrange("(c o) -> c o", o=1)).then_inc(s["loaded_w"], 16)
                act.wait_ge(s["loaded_w"], 16 * (N_W + 4))

                def raw_scores(g, c):
                    wait(act, s["y_ready"], 2 * g + c - 1)
                    wait(act, s["att_ready"], 2 * g + c + 1)
                    act.activation(att[:, c, HALF:HEADS], b_att[:, HALF:HEADS], ACT.Copy) \
                       .then_inc(s["att_raw"], 1)

                def step(t, u, on):
                    if on(4):
                        g, v = t - 4, u % 2
                        wait(act, s["yc_ready"], g - 1)
                        wait(act, s["ytok_ready"], g + 1)
                        act.activation(ytok[:, v], b_y[:, 0:256], ACT.Copy).then_inc(s["ytok_sb"], 1)
                    if on(2):
                        g, v = t - 2, (u - 2) % RING
                        wait(act, s["qkt_ready"], g + 1)
                        wait(act, s["y_ready"], 2 * g - 6)
                        act.activation(qkT[:, v].rearrange("p a b c -> p (a b c)"), b_t, ACT.Copy) \
                           .then_inc(s["qkT_sb"], 1)
                    if on(2):
                        g, v = t - 2, (u - 2) % RING
                        wait(act, s["qkT_sb"], g + 1)
                        wait(act, s["att_ready"], 2 * g - 2)
                        for hd in range(ACT_HEADS):
                            ins = act.activation(qexp[:, v % 2, :, hd, :], qkT[:, v, 0], ACT.Copy,
                                                 scale=headmask[:, hd:hd + 1])
                        ins.then_inc(s["qexp_act"], 1)
                    if on(7):
                        g = t - 7
                        wait(act, s["ht_ready"], g + 1)
                        wait(act, s["w2_ready"], g)
                        act.activation(hT[:].rearrange("p a b -> p (a b)"), b_t, ACT.Copy) \
                           .then_inc(s["hT_sb"], 1)
                    if on(3):
                        raw_scores(t - 3, 1)
                    lo, hi = (0 if on(0) else 2), (4 if on(6) else 2)
                    if hi > lo:
                        wait(act, s["xzt_ready"], t + 1)
                        if on(7):
                            wait(act, s["w1_ready"], t - 6)
                        if on(1):
                            wait(act, s["qk_ready"], t)
                        act.activation(xzT[:, lo:hi].rearrange("p a b -> p (a b)"),
                                       b_xz[:, lo * P:hi * P], ACT.Identity,
                                       scale=lnsb[:, 0:1], bias=lnsb[:, 1:2]).then_inc(s["xzT_sb"], 1)
                    if on(3):
                        g = t - 3
                        wait(act, s["y_ready"], 2 * g + 2)
                        wait(act, s["ytok_ready"], g)
                        act.activation(yT[:].rearrange("p a b -> p (a b)"), b_y[:, 0:256], ACT.Copy) \
                           .then_inc(s["yT_sb"], 1)
                    if on(5):
                        g = t - 5
                        wait(act, s["gyt_ready"], g + 1)
                        wait(act, s["wo_ready"], g)
                        act.activation(gyT[:].rearrange("p a b -> p (a b)"), b_xz[:, 0:256], ACT.Copy) \
                           .then_inc(s["gyT_sb"], 1)
                    if on(4):
                        g, v = t - 4, (u - 4) % RING
                        wait(act, s["yc_ready"], g + 1)
                        wait(act, s["var_ready"], g)
                        act.activation(sq[:], yc[:, v], ACT.Square).then_inc(s["sq_ready"], 1)
                    if on(0):
                        g, v = t, u
                        wait(act, s["vg_ready"], g + 1)
                        wait(act, s["y_ready"], 2 * g - 6)
                        wait(act, s["gate_ready"], g - 3)
                        for c in range(2):
                            src = b_vg[:, 256 * c:256 * c + D].rearrange("p (q j d) -> p q j d", q=4, j=2)
                            dst = ve[:, v, c].rearrange("p q e j d -> p q (e j) d")[:, :, 0:4:3, :]
                            act.activation(dst, src, ACT.Copy)
                        act.activation(th[:, v], b_vg.rearrange("p (c a d) -> p c a d", c=2, a=2)[:, :, 1, :],
                                       ACT.Tanh, scale=0.5).then_inc(s["v_sb"], 1)
                    if on(2):
                        raw_scores(t - 2, 0)
                    if on(6):
                        g = t - 6
                        wait(act, s["w1_ready"], g + 1)
                        wait(act, s["ht_ready"], g)
                        act.activation(h[:].rearrange("p a b -> p (a b)"), b_t, ACT.Gelu_apprx_tanh) \
                           .then_inc(s["h_sb"], 1)

                run(step)(act)

            @blk.gpsimd
            def _(pool):
                pool.memset(ve[:], 0.0).then_inc(s["zeroed"], 1)
                pool.memset(state[:], 0.0).then_inc(s["zeroed"], 1)
                pool.memset(zero_rows[:], 0.0).then_inc(s["zeroed"], 1)
                pool.wait_ge(s["loaded_w"], 16 * (N_W + 4))
                pool.wait_ge(loaded_small, 16)
                pool.tensor_scalar(gns[:], gns[:], 0.5, None, ALU.mult).then_inc(s["halved"], 1)
                pool.tensor_scalar(gnb[:], gnb[:], 0.5, None, ALU.mult).then_inc(s["halved"], 1)
                pool.wait_ge(s["halved"], 2)

                def masked(g, c):
                    wait(pool, s["att_raw"], 2 * g + c + 1)
                    pool.tensor_tensor(att[:, c, HALF:HEADS], att[:, c, HALF:HEADS],
                                       spread(causal.unsqueeze(1), 1, HALF), ALU.mult) \
                        .then_inc(s["att_masked2"], 1)

                def step(t, u, on):
                    if on(2):
                        g, v = t - 2, (u - 2) % RING
                        wait(pool, s["qkT_sb"], g + 1)
                        wait(pool, s["att_ready"], 2 * g - 2)
                        pool.tensor_tensor(qexp[:, v % 2, :, ACT_HEADS, :], qkT[:, v, 0],
                                           headmask[:, ACT_HEADS:ACT_HEADS + 1].unsqueeze(1)
                                           .broadcast_to([P, 2, P]), ALU.mult)
                        for hd in range(ACT_HEADS + 1, HEADS):
                            ins = pool.tensor_scalar(qexp[:, v % 2, :, hd, :], qkT[:, v, 0],
                                                     headmask[:, hd:hd + 1], None, ALU.mult)
                        ins.then_inc(s["qexp_ready"], 1)
                    if on(3):
                        masked(t - 3, 1)
                    if on(2):
                        wait(pool, s["gate_ready"], g + 1)
                        wait(pool, s["gy_ready"], g - 3)
                        for dst, tab in ((gs, gns), (gb, gnb)):
                            row = spread(tab[:, bass.ds(layer(g), 1), :], 1, 2)
                            ins = pool.tensor_tensor(dst[:, v], gate[:, v], row, ALU.mult)
                        ins.then_inc(s["gsb_ready"], 1)
                    if on(1):
                        g, v = t - 1, (u - 1) % RING
                        wait(pool, s["rot_ready"], g + 1)
                        wait(pool, s["kv_ready"], g - 3)
                        wait(pool, s["qkt_ready"], g - 3)
                        pool.tensor_tensor(qk[:, v].rearrange("p a b c -> p (a b c)"),
                                           cosq[:].rearrange("p a b -> p (a b)"),
                                           sinq[:].rearrange("p a b -> p (a b)"), ALU.add) \
                            .then_inc(s["rot_sum"], 1)
                    if on(2):
                        masked(t - 2, 0)

                run(step)(pool)

            @blk.tensor
            def _(pe):
                pe.wait_ge(s["loaded_w"], 16 * (N_W + 4))
                pe.wait_ge(loaded_small, 16)
                pe.wait_ge(s["zeroed"], 2)

                def scores(g, v, c):
                    wait(pe, s["qexp_ready"], g + 1)
                    wait(pe, s["qexp_act"], g + 1)
                    wait(pe, s["att_raw"], 2 * g + c)
                    wait(pe, s["att_masked"], 2 * g + c)
                    for hh in range(2):
                        ins = pe.matmul(b_att[:, 4 * hh:4 * hh + 4, :], qkT[:, v, 1, c],
                                        qexp[:, v % 2, c, 4 * hh:4 * hh + 4, :], start=True, stop=True)
                    ins.then_inc(s["att_ready"], 1)

                def outputs(g, v, c):
                    wait(pe, s["state_ready"], 2 * g + c)
                    if c == 0:
                        wait(pe, s["ytok_sb"], g)
                    wait(pe, s["att_masked2"], 2 * g + c + 1)
                    wait(pe, s["att_masked"], 2 * g + c + 1)
                    out = b_y[:, c * P:c * P + P]
                    pe.matmul(out, state[:, c], qkT[:, v, 0, c], start=True, stop=False,
                              skip_group_check=True)
                    for e in range(2):
                        for q in range(4):
                            ins = pe.matmul(out[32 * q:32 * q + 32, :],
                                            ve[:, v, c, q, e].rearrange("p j d -> p (j d)"),
                                            att[:, c, 2 * q + e, :], start=False, stop=(e == 1),
                                            skip_group_check=True)
                    ins.then_inc(s["y_ready"], 1)

                def step(t, u, on):
                    w = (u - 3) % RING
                    if on(3):
                        g = t - 3
                        wait(pe, s["v_sb"], g + 1)
                        if on(6):
                            wait(pe, s["yr_ready"], t - 5)
                        for c in range(2):
                            plain = ve[:, w, c].rearrange("p q e j d -> p q (e j) d")[:, :, 0:4:3, :]
                            ins = pe.matmul(b_sum[:, c * P:c * P + P], qk[:, w, c, 1], plain,
                                            start=True, stop=True)
                        ins.then_inc(s["kv_ready"], 1)
                    if on(7):
                        if on(2):
                            wait(pe, s["qkT_sb"], t - 1)
                        wait(pe, s["h_sb"], t - 6)
                        for n in range(4):
                            ins = pe.transpose(b_t[:, n * P:n * P + P],
                                               h[:, n // 2, (n % 2) * P:(n % 2) * P + P], eye)
                        ins.then_inc(s["ht_ready"], 1)
                    if on(3):
                        scores(t - 3, w, 1)
                        outputs(t - 3, w, 0)
                    if on(7):
                        g = t - 7
                        if on(3):
                            wait(pe, s["kv_taken"], 2 * t - 4)
                        else:
                            wait(pe, s["yr_ready"], min(t - 5, STEPS))
                            wait(pe, s["x_next"], g)
                        wait(pe, s["hT_sb"], g + 1)
                        for c in range(2):
                            for f in range(2):
                                ins = pe.matmul(b_sum[:, c * P:c * P + P], hT[:, 2 * c + f],
                                                w2[:, bass.ds(layer(g), 1), f, :], start=(f == 0),
                                                stop=(f == 1))
                        ins.then_inc(s["w2_ready"], 1)
                    lo, hi = (0 if on(0) else 2), (4 if on(6) else 2)
                    if hi > lo:
                        if on(6):
                            wait(pe, s["gyT_sb"], t - 5)
                        wait(pe, s["xz_ready"], t + 1)
                        for n in range(lo, hi):
                            ins = pe.transpose(b_xz[:, n * P:n * P + P], xz[:, n], eye)
                        ins.then_inc(s["xzt_ready"], 1)
                    if on(3):
                        outputs(t - 3, w, 1)
                    if on(2):
                        scores(t - 2, (u - 2) % RING, 0)
                    if on(5):
                        g, v = t - 5, (u - 5) % RING
                        if hi > lo:
                            wait(pe, s["xzT_sb"], t + 1)
                        wait(pe, s["gy_ready"], g + 1)
                        for c in range(2):
                            ins = pe.transpose(b_xz[:, c * P:c * P + P], yc[:, v, c], eye)
                        ins.then_inc(s["gyt_ready"], 1)

                    def projections(bank, n, done):
                        for c in range(2):
                            ins = pe.matmul(bank[:, 256 * c:256 * c + 256], xzT[:, c],
                                            wqkvg[:, bass.ds(layer(t), 1), 2 * n:2 * n + 2, :],
                                            start=True, stop=True)
                        ins.then_inc(s[done], 1)

                    if on(0):
                        if not on(5):
                            wait(pe, s["xzT_sb"], t + 1)
                        wait(pe, s["gate_ready"], t)
                        projections(b_vg, 1, "vg_ready")
                    if on(5):
                        g = t - 5
                        if on(7):
                            wait(pe, s["x_next"], t - 6)
                        elif on(3):
                            wait(pe, s["kv_taken"], 2 * t - 4)
                        wait(pe, s["gyT_sb"], g + 1)
                        for c in range(2):
                            ins = pe.matmul(b_sum[:, c * P:c * P + P], gyT[:, c],
                                            wo[:, bass.ds(layer(g), 1), :], start=True, stop=True)
                        ins.then_inc(s["wo_ready"], 1)
                    if on(6):
                        if on(7):
                            wait(pe, s["hT_sb"], t - 6)
                        wait(pe, s["xzT_sb"], t + 1)
                        for c in range(2):
                            ins = pe.matmul(b_t[:, 256 * c:256 * c + 256], xzT[:, 2 + c],
                                            w1[:, bass.ds(layer(t - 6), 1), :], start=True, stop=True)
                        ins.then_inc(s["w1_ready"], 1)
                    if on(0):
                        wait(pe, s["rot_ready"], t)
                        projections(b_qk, 0, "qk_ready")
                    if on(3):
                        wait(pe, s["yT_sb"], t - 2)
                        for c in range(2):
                            ins = pe.transpose(b_y[:, c * P:c * P + P], yT[:, c], eye)
                        ins.then_inc(s["ytok_ready"], 1)
                    if on(1):
                        g, v = t - 1, (u - 1) % RING
                        if on(6):
                            wait(pe, s["h_sb"], t - 5)
                        elif on(2):
                            wait(pe, s["qkT_sb"], t - 1)
                        wait(pe, s["rot_sum"], g + 1)
                        for n in range(4):
                            ins = pe.transpose(b_t[:, n * P:n * P + P], qk[:, v, n % 2, n // 2], eye)
                        ins.then_inc(s["qkt_ready"], 1)

                run(step)(pe)

            @blk.vector
            def _(dve):
                dve.memset(mv[:], 1.0).then_inc(s["start_chain"], 1)
                dve.memset(vv[:], 1.0).then_inc(s["start_chain"], 1)
                dve.wait_ge(loaded_x, 16)
                dve.wait_ge(loaded_small, 16)
                dve.wait_ge(s["start_chain"], 2)
                for c in range(NCH):
                    dve.bn_stats(stats0[:, c], xin[:, c]).then_inc(s["start_chain"], 1)
                for c in range(NCH):
                    dve.wait_ge(s["start_chain"], 3 + c)
                    dve.bn_aggr(mv0[:, c], stats0[:, c]).then_inc(s["start_rs"], 1)
                dve.wait_ge(s["start_rs"], NCH)
                dve.tensor_scalar(v0[:], mv0[:, :, 1], EPS, None, ALU.add).then_inc(s["start_rs"], 1)
                dve.wait_ge(s["start_rs"], NCH + 1)
                rsqrt_steps(dve, v0[:], y0[:], t0[:], s["start_chain"], NCH + 2, s["start_rs"], rs0[:])
                dve.wait_ge(s["start_rs"], NCH + 2)
                for c in range(NCH):
                    dve.tensor_scalar(resid[:, c], xin[:, c], mv0[:, c, 0:1], rs0[:, c:c + 1],
                                      ALU.subtract, ALU.mult).then_inc(s["resid_init"], 1)
                dve.wait_ge(s["loaded_w"], 16 * (N_W + 4))
                dve.wait_ge(s["resid_init"], NCH)
                dve.wait_ge(s["zeroed"], 2)

                def masked(g, c):
                    wait(dve, s["y_ready"], 2 * g + c - 1)
                    wait(dve, s["att_ready"], 2 * g + c + 1)
                    dve.tensor_tensor(att[:, c, 0:HALF], b_att[:, 0:HALF],
                                      spread(causal.unsqueeze(1), 1, HALF), ALU.mult).then_inc(s["att_masked"], 1)

                def chunk_decay(g, c):
                    return decay[:, bass.ds((g & (GROUPS - 1)) * 2 + c, 1)]

                def keys_values(g, c):
                    wait(dve, s["state_ready"], 2 * g + c - 1)
                    wait(dve, s["kv_ready"], g + 1)
                    dve.scalar_tensor_tensor(out=kvm[:, c], in0=b_sum[:, c * P:c * P + P],
                                             scalar=chunk_decay(g, c), in1=block,
                                             op0=ALU.mult, op1=ALU.mult).then_inc(s["kv_taken"], 1)

                def new_state(g, c):
                    wait(dve, s["kv_taken"], 2 * g + c + 1)
                    wait(dve, s["state_ready"], 2 * g + c)
                    wait(dve, s["y_ready"], 2 * g + c)
                    dve.scalar_tensor_tensor(out=state[:, 1 - c], in0=state[:, c],
                                             scalar=chunk_decay(g, c), in1=kvm[:, c],
                                             op0=ALU.mult, op1=ALU.add).then_inc(s["state_ready"], 1)

                def gates(g, v):
                    wait(dve, s["gsb_ready"], g - 3)
                    wait(dve, s["v_sb"], g + 1)
                    dve.scalar_tensor_tensor(
                        out=gate[:, v], in0=th[:, v], scalar=1.0,
                        in1=b_vg.rearrange("p (c a d) -> p c a d", c=2, a=2)[:, :, 1, :],
                        op0=ALU.add, op1=ALU.mult).then_inc(s["gate_ready"], 1)

                def mlp_added(g):
                    wait(dve, s["w2_ready"], g + 1)
                    x0 = pair(resid, g)
                    dve.tensor_tensor(x0, b_sum[:, 0:256].rearrange("p (c d) -> p c d", c=2), x0,
                                      ALU.add).then_inc(s["x_next"], 1)

                def rotate_cos(g):
                    wait(dve, s["rot_sum"], g)
                    wait(dve, s["qk_ready"], g + 1)
                    p2 = (g & (GROUPS - 1)) * 2
                    dve.tensor_tensor(cosq[:], b_qk.rearrange("p (c n) -> p c n", c=2),
                                      rot[:, 0, bass.ds(p2, 2), :], ALU.mult)

                def rotate_sin(g):
                    p2 = (g & (GROUPS - 1)) * 2
                    other = b_qk.rearrange("p (n e) -> p n e", e=2)[:, :, ::-1]
                    dve.tensor_tensor(
                        sinq[:].rearrange("p c (n e) -> p (c n) e", e=2), other,
                        rot[:, 1].rearrange("p c (n e) -> p (c n) e", e=2)[:, bass.ds(p2 * P, 256), :],
                        ALU.mult).then_inc(s["rot_ready"], 1)

                def step(t, u, on):
                    lo, hi = (0 if on(0) else 2), (4 if on(6) else 2)
                    v4, v5 = (u - 4) % RING, (u - 5) % RING
                    if on(0):
                        wait(dve, s["x_next"], t - 7)
                    if on(3):
                        masked(t - 3, 0)
                    if on(0):
                        for c in range(2):
                            ins = dve.bn_stats(stats[:, c], resid[:, bass.ds((t & 7) * 2 + c, 1), :])
                    if on(6):
                        g = t - 6
                        x2 = pair(resid, g)
                        wait(dve, s["wo_ready"], g + 1)
                        dve.tensor_tensor(x2, b_sum[:, 0:256].rearrange("p (c d) -> p c d", c=2), x2,
                                          ALU.add).then_inc(s["yr_ready"], 1)
                    if on(6):
                        wait(dve, s["yr_ready"], t - 5)
                    if on(5):
                        wait(dve, s["sq_ready"], t - 4)
                        dve.tensor_reduce(vv[:, 4:20], sq[:].rearrange("p c (a d) -> p (c a) d", d=DH),
                                          AX.X, ALU.add).then_inc(s["var_ready"], 1)
                    if on(6):
                        for c in range(2):
                            ins = dve.bn_stats(stats[:, 2 + c],
                                               resid[:, bass.ds(((t - 6) & 7) * 2 + c, 1), :])
                    if hi > lo:
                        ins.then_inc(s["bn_stats_done"], 1)
                        wait(dve, s["bn_stats_done"], t + 1)
                    chain = RS_LINKS + 2
                    if on(5):
                        wait(dve, s["var_ready"], t - 4)
                    dve.tensor_scalar(vv[:, 4:20], vv[:, 4:20], 1.0 / DH, EPS, ALU.mult, ALU.add) \
                       .then_inc(s["rs_chain"], 1)
                    if hi > lo:
                        for n in range(lo, hi):
                            ins = dve.bn_aggr(mv[:, n], stats[:, n])
                        ins.then_inc(s["bn_aggr_done"], 1)
                        wait(dve, s["bn_aggr_done"], t + 1)
                    dve.tensor_scalar(vv[:, 0:4], mv[:, :, 1], EPS, None, ALU.add) \
                       .then_inc(s["rs_chain"], 1)
                    dve.wait_ge(s["rs_chain"], chain * t + 2)
                    work = []
                    if on(3):
                        work += [lambda: keys_values(t - 3, 0),
                                 lambda: keys_values(t - 3, 1), lambda: new_state(t - 3, 0)]
                    if on(1):
                        work.append(lambda: gates(t - 1, (u - 1) % RING))
                    rsqrt_steps(dve, vv[:], vy[:], vt[:], s["rs_chain"], chain * t + 2,
                                s["rs_ready"], rs[:], work)
                    dve.wait_ge(s["rs_ready"], t + 1)
                    if hi > lo:
                        wait(dve, s["xzt_ready"], t)
                        for n in range(lo, hi):
                            g = t if n < 2 else t - 6
                            ins = dve.tensor_scalar(xz[:, n], resid[:, bass.ds((g & 7) * 2 + n % 2, 1), :],
                                                    mv[:, n, 0:1], rs[:, n:n + 1],
                                                    ALU.subtract, ALU.mult)
                        ins.then_inc(s["xz_ready"], 1)
                    if on(3):
                        masked(t - 3, 1)
                    if on(5):
                        g, yv = t - 5, yc[:, v5].rearrange("p c (a d) -> p (c a) d", d=DH)
                        dve.tensor_tensor(yv, yv, spread(rs[:, 4:20].unsqueeze(2), 2, DH), ALU.mult) \
                           .then_inc(s["gy_chain"], 1)
                    if on(1):
                        rotate_cos(t - 1)
                    if on(5):
                        wait(dve, s["gsb_ready"], g + 1)
                        wait(dve, s["gy_chain"], 2 * g + 1)
                        dve.tensor_tensor(yc[:, v5], yc[:, v5], gs[:, v5], ALU.mult) \
                           .then_inc(s["gy_chain"], 1)
                    if on(1):
                        rotate_sin(t - 1)
                    if on(5):
                        wait(dve, s["gy_chain"], 2 * g + 2)
                        dve.tensor_tensor(yc[:, v5], yc[:, v5], gb[:, v5], ALU.add).then_inc(s["gy_ready"], 1)
                    y = ytok[:, u % 2].rearrange("p (a d) -> p a d", d=DH)
                    if on(4):
                        wait(dve, s["ytok_sb"], t - 3)
                        dve.tensor_reduce(gsum[:], y, AX.X, ALU.add).then_inc(s["gn_sum"], 1)
                    if on(7):
                        mlp_added(t - 7)
                    if on(4):
                        wait(dve, s["gyt_ready"], t - 7)
                        wait(dve, s["gn_sum"], t - 3)
                        dve.scalar_tensor_tensor(
                            out=yc[:, v4].rearrange("p c (a d) -> p (c a) d", d=DH),
                            in0=spread(gsum[:].unsqueeze(2), 2, DH),
                            scalar=-1.0 / DH, in1=y, op0=ALU.mult, op1=ALU.add).then_inc(s["yc_ready"], 1)
                    if on(3):
                        new_state(t - 3, 1)

                run(step)(dve)

                dve.wait_ge(s["x_next"], STEPS)
                dve.tensor_tensor(xin[:], xin[:], resid[:], ALU.add)


def ffn_semaphores(nc, ctx):
    names = ("ones_set", "stats_done", "aggr_done", "rs_chain", "rs_ready", "xn_ready", "xnT_psum",
             "xnT_ready", "logits_ready", "route_chain", "hot_ready", "ranks_ready", "slot_ready",
             "expert_ready", "top_ready", "score_tanh", "xs_ready", "up_ready", "gate_silu", "hs_ready",
             "shared_ready", "shared_added", "scattered", "xt_psum", "xtT_ready",
             "gu_ready", "silr_ready", "hr_ready", "hrt_psum", "hrT_ready", "y_psum", "yt_ready",
             "gathered")
    one = {n: ctx.enter_context(nc.semaphore("ffn_" + n)) for n in names}
    ring = {n: [ctx.enter_context(nc.semaphore(f"ffn_{n}{r}")) for r in range(RING)]
            for n in ("x_loaded", "stored")}
    return {"one": one, **ring}


def clear_ffn_semaphores(nc, sems):
    with nc.Block() as blk:
        @blk.gpsimd
        def _(pool):
            for name, one in sems["one"].items():
                if name not in ("scattered", "gathered"):
                    pool.sem_clear(one)
            for one in sems["x_loaded"] + sems["stored"]:
                pool.sem_clear(one)


def ffn(nc, call, x, w, rows_in, rows_out, eye, route, banks, loaded_ffn, sems):
    BLK = 4
    ctx = ExitStack()
    with ctx:
        def sb(name, shape, dt=F32):
            return ctx.enter_context(nc.sbuf_tensor(f"ffn{call}_{name}", shape, dt))

        stats = sb("stats", [P, NCH, 6])
        mv = sb("mv", [P, NCH, 2])
        var, vy, vt, rs = (sb(n, [P, NCH]) for n in ("var", "vy", "vt", "rs"))
        xn = sb("xn", [P, NCH, D])
        xnT = sb("xnT", [P, NCH, P])
        top_logit = sb("top_logit", [P, NCH])
        tied = sb("tied", [P, NCH, EXPERTS])
        first = sb("first", [P, NCH])
        hot = sb("hot", [P, EXPERTS, NCH])
        upto = sb("upto", [P, EXPERTS, NCH])
        place = sb("place", [P, EXPERTS, NCH])
        ntiles, tiles_upto, tiles_before, all_one = (sb(n, [P, EXPERTS]) for n in
                                                     ("ntiles", "tiles_upto", "tiles_before", "all_one"))
        slot_f = sb("slot_f", [P, NCH])
        slot = sb("slot", [P, NCH], mybir.dt.uint32)
        past = sb("past", [P, TILES, EXPERTS])
        expert_f = sb("expert_f", [P, TILES])
        expert_of = sb("expert_of", [P, TILES], I32)
        score = sb("score", [P, NCH])
        xs = sb("xs", [P, NCH, D])
        sil = sb("sil", [P, 2, 512])
        hs = sb("hs", [P, 2, 2, 512])
        s, x_loaded, stored = sems["one"], sems["x_loaded"], sems["stored"]
        xt = sb("xt", [P, RING, D])
        xtT = sb("xtT", [P, 2, P])
        silr = sb("silr", [P, 2, FE])
        hr = sb("hr", [P, 2, FE])
        hrT = sb("hrT", [P, 2, 2, P])
        yt = sb("yt", [P, RING, D])
        yg = sb("yg", [P, NCH, D])

        LAG = 4
        PRO, UN = 8, 4

        def run(step):
            def go(eng):
                for t in range(PRO):
                    step(t, t % UN, t // UN, lambda lag: t - lag >= 0)
                with eng.Fori(PRO // UN, TILES // UN, 1) as k:
                    for u in range(UN):
                        step(k * UN + u, u, k, lambda lag: True)
                for t in range(TILES, TILES + LAG):
                    step(t, t % UN, t // UN, lambda lag: t - lag < TILES)
            return go

        with nc.Block() as blk:
            @blk.sync
            def _(sp):
                sp.wait_ge(s["scattered"], 16 * NCH * (call + 1))

                def step(t, u, k, on):
                    if on(0):
                        wait(sp, s["xt_psum"], t - RING + 1)
                        if isinstance(t, int):
                            row = t * P
                            src = rows_in[row:row + P, :]
                        else:
                            src = rows_in[bass.ds(t * P, P), :]
                        sp.dma_start(xt[:, u], src).then_inc(x_loaded[u], 16)
                run(step)(sp)

            @blk.gpsimd
            def _(pool):
                pool.memset(all_one[:], 1.0).then_inc(s["ones_set"], 1)
                pool.wait_ge(s["slot_ready"], 1)
                pool.wait_ge(s["xs_ready"], 1)
                pool.wait_ge(loaded_ffn, 16 * 6)
                for c in range(NCH):
                    pool.indirect_dma_start(
                        rows_in, bass.IndirectOffsetOnAxis(ap=slot[:, c:c + 1], axis=0),
                        xs[:, c], None).then_inc(s["scattered"], 16)
                for r in range(RING):
                    pool.wait_ge(stored[r], 16 * TILES // RING)
                for c in range(NCH):
                    pool.indirect_dma_start(
                        yg[:, c], None, rows_out,
                        bass.IndirectOffsetOnAxis(ap=slot[:, c:c + 1], axis=0)).then_inc(s["gathered"], 16)

            @blk.scalar
            def _(act):
                for b in range(NCH // 4):
                    act.wait_ge(s["xnT_psum"], b + 1)
                    act.activation(xnT[:, 4 * b:4 * b + 4].rearrange("p a b -> p (a b)"), banks[:, b, :],
                                   ACT.Copy).then_inc(s["xnT_ready"], 1)
                act.wait_ge(s["top_ready"], 1)
                act.activation(score[:], top_logit[:], ACT.Tanh, scale=0.5).then_inc(s["score_tanh"], 1)
                for b in range(NCH // BLK):
                    act.wait_ge(s["up_ready"], b + 1)
                    wait(act, s["hs_ready"], b)
                    act.activation(sil[:].rearrange("p a b -> p (a b)"),
                                   banks[:, 0:2, :].rearrange("p a b -> p (a b)"), ACT.Silu) \
                       .then_inc(s["gate_silu"], 1)

                def step(t, u, k, on):
                    if on(0):
                        v = u % 2
                        act.wait_ge(s["xt_psum"], t + 1)
                        wait(act, s["gu_ready"], t - 1)
                        act.activation(xtT[:, v], banks[:, v, 0:P], ACT.Copy).then_inc(s["xtT_ready"], 1)
                    if on(1):
                        j, v = t - 1, (u + 1) % 2
                        wait(act, s["gu_ready"], j + 1)
                        wait(act, s["hr_ready"], j - 1)
                        act.activation(silr[:, v], banks[:, 2 + v, 0:FE], ACT.Silu) \
                           .then_inc(s["silr_ready"], 1)
                    if on(2):
                        j, v = t - 2, u % 2
                        wait(act, s["hrt_psum"], j + 1)
                        wait(act, s["y_psum"], j - 1)
                        act.activation(hrT[:, v].rearrange("p a b -> p (a b)"), banks[:, 4 + v, 0:2 * P],
                                       ACT.Copy).then_inc(s["hrT_ready"], 1)
                    if on(4):
                        j = t - 4
                        wait(act, s["yt_ready"], j + 1)
                        dst = rows_out[j * P:j * P + P, :] if isinstance(j, int) else \
                            rows_out[bass.ds(j * P, P), :]
                        act.dma_start(dst, yt[:, u]).then_inc(stored[u], 16)
                run(step)(act)

            @blk.tensor
            def _(pe):
                pe.wait_ge(loaded_ffn, 16 * 6)
                for b in range(NCH // 4):
                    pe.wait_ge(s["xn_ready"], 4 * b + 4)
                    for c in range(4 * b, 4 * b + 4):
                        ins = pe.transpose(banks[:, b, (c % 4) * P:(c % 4) * P + P], xn[:, c], eye)
                    ins.then_inc(s["xnT_psum"], 1)
                for c in range(NCH):
                    pe.wait_ge(s["xnT_ready"], c // 4 + 1)
                    ins = pe.matmul(banks[:, 4, c * EXPERTS:(c + 1) * EXPERTS], xnT[:, c], w["gate"][:],
                                    start=True, stop=True)
                ins.then_inc(s["logits_ready"], 1)

                def shared_up(b):
                    pe.wait_ge(s["xnT_ready"], NCH // 4)
                    wait(pe, s["hs_ready"], b)
                    rhs = xnT[:, BLK * b:BLK * b + BLK].rearrange("p a b -> p (a b)")
                    for n in range(4):
                        ins = pe.matmul(banks[:, n, :], w["s_gu"][:, n], rhs, start=True, stop=True)
                    ins.then_inc(s["up_ready"], 1)

                def shared_down(b):
                    pe.wait_ge(s["hs_ready"], b + 1)
                    wait(pe, s["shared_added"], b)
                    for c in range(BLK):
                        for f in range(2):
                            ins = pe.matmul(banks[:, 6, c * P:c * P + P], hs[:, b % 2, f, c * P:c * P + P],
                                            w["s_down"][:, f], start=(f == 0), stop=(f == 1))
                    ins.then_inc(s["shared_ready"], 1)

                shared_up(0)
                pe.wait_ge(s["hot_ready"], 1)
                hot2 = hot[:].rearrange("p e c -> p (e c)")
                pe.matmul(banks[:, 5, 0:P], route["earlier"], hot2, start=True, stop=True)
                pe.matmul(banks[:, 5, P:2 * P], route["ones"], hot2, start=True, stop=True) \
                  .then_inc(s["ranks_ready"], 1)
                for b in range(NCH // BLK):
                    if b + 1 < NCH // BLK:
                        shared_up(b + 1)
                    shared_down(b)

                pe.wait_ge(s["expert_ready"], 1)
                pe.wait_ge(s["shared_added"], NCH // BLK)

                def expert(j):
                    at = expert_of[0:1, j:j + 1] if isinstance(j, int) else \
                        expert_of[0:1, bass.ds(j, 1)]
                    return pe.value_load(at, min_val=0, max_val=EXPERTS - 1)

                def step(t, u, k, on):
                    if on(0):
                        v = u % 2
                        wait(pe, x_loaded[u], k * 16 + 16)
                        wait(pe, s["xtT_ready"], t - 1)
                        pe.transpose(banks[:, v, 0:P], xt[:, u], eye).then_inc(s["xt_psum"], 1)
                    if on(1):
                        j, v = t - 1, (u + 1) % 2
                        e = expert(j)
                        wait(pe, s["xtT_ready"], j + 1)
                        wait(pe, s["hr_ready"], j - 1)
                        pe.matmul(banks[:, 2 + v, :], xtT[:, v], w["r_gu"][:, bass.ds(e, 1), :],
                                  start=True, stop=True).then_inc(s["gu_ready"], 1)
                    if on(2):
                        j, v = t - 2, u % 2
                        wait(pe, s["hr_ready"], j + 1)
                        wait(pe, s["hrT_ready"], j - 1)
                        for f in range(2):
                            ins = pe.transpose(banks[:, 4 + v, f * P:f * P + P], hr[:, v, f * P:f * P + P],
                                               eye)
                        ins.then_inc(s["hrt_psum"], 1)
                    if on(3):
                        j, v = t - 3, (u + 1) % 2
                        e = expert(j)
                        wait(pe, s["hrT_ready"], j + 1)
                        wait(pe, s["yt_ready"], j - 1)
                        for f in range(2):
                            ins = pe.matmul(banks[:, 6 + v, 0:P], hrT[:, v, f],
                                            w["r_down"][:, bass.ds(e, 1), f, :], start=(f == 0),
                                            stop=(f == 1))
                        ins.then_inc(s["y_psum"], 1)
                run(step)(pe)

            @blk.vector
            def _(dve):
                for c in range(NCH):
                    dve.bn_stats(stats[:, c], x[:, c]).then_inc(s["stats_done"], 1)
                for c in range(NCH):
                    dve.wait_ge(s["stats_done"], c + 1)
                    ins = dve.bn_aggr(mv[:, c], stats[:, c])
                ins.then_inc(s["aggr_done"], 1)
                dve.wait_ge(s["aggr_done"], 1)
                dve.tensor_scalar(var[:], mv[:, :, 1], EPS, None, ALU.add).then_inc(s["rs_chain"], 1)
                dve.wait_ge(s["rs_chain"], 1)
                rsqrt_steps(dve, var[:], vy[:], vt[:], s["rs_chain"], 1, s["rs_ready"], rs[:])
                dve.wait_ge(s["rs_ready"], 1)
                for c in range(NCH):
                    dve.tensor_scalar(xn[:, c], x[:, c], mv[:, c, 0:1], rs[:, c:c + 1],
                                      ALU.subtract, ALU.mult).then_inc(s["xn_ready"], 1)

                n = [0]

                def link(ins):
                    n[0] += 1
                    ins.then_inc(s["route_chain"], 1)
                    dve.wait_ge(s["route_chain"], n[0])

                rev = route["rev"]
                logits = banks[:, 4, 0:NCH * EXPERTS].rearrange("p (c e) -> p c e", e=EXPERTS)
                dve.wait_ge(s["logits_ready"], 1)
                dve.tensor_reduce(top_logit[:], logits, AX.X, ALU.max).then_inc(s["top_ready"], 1)
                dve.wait_ge(s["top_ready"], 1)
                link(dve.tensor_tensor(tied[:], logits, spread(top_logit[:].unsqueeze(2), 2, EXPERTS),
                                       ALU.is_equal))
                link(dve.tensor_tensor(tied[:], tied[:], spread(rev.unsqueeze(1), 1, NCH), ALU.mult))
                link(dve.tensor_reduce(first[:], tied[:], AX.X, ALU.max))
                dve.tensor_tensor(hot[:], spread(first[:].unsqueeze(1), 1, EXPERTS),
                                  spread(rev.unsqueeze(2), 2, NCH), ALU.is_equal).then_inc(s["hot_ready"], 1)

                def shared_hidden(b):
                    dve.wait_ge(s["gate_silu"], b + 1)
                    wait(dve, s["shared_ready"], b - 1)
                    dve.tensor_tensor(hs[:, b % 2], sil[:], banks[:, 2:4, :], ALU.mult) \
                       .then_inc(s["hs_ready"], 1)

                def shared_add(b):
                    dve.wait_ge(s["shared_ready"], b + 1)
                    part = x[:, BLK * b:BLK * b + BLK]
                    dve.tensor_tensor(part, part, banks[:, 6, :].rearrange("p (c d) -> p c d", c=BLK),
                                      ALU.add).then_inc(s["shared_added"], 1)

                dve.wait_ge(s["score_tanh"], 1)
                link(dve.tensor_scalar(score[:], score[:], 0.5, 0.5, ALU.mult, ALU.add))
                dve.tensor_tensor(xs[:], xn[:], spread(score[:].unsqueeze(2), 2, D), ALU.mult) \
                   .then_inc(s["xs_ready"], 1)
                shared_hidden(0)
                dve.wait_ge(s["ranks_ready"], 1)
                within, total = banks[:, 5, 0:P], banks[:, 5, P:2 * P]
                up2, pl2 = upto[:].rearrange("p e c -> p (e c)"), place[:].rearrange("p e c -> p (e c)")
                link(dve.tensor_tensor_scan(up2, route["restart"], total, 0.0, ALU.mult, ALU.add))
                link(dve.tensor_scalar(ntiles[:], upto[:, :, NCH - 1], 63.5, 1.0 / P, ALU.add, ALU.mult))
                link(dve.tensor_scalar(ntiles[:], ntiles[:], ROUND, None, ALU.add))
                link(dve.tensor_scalar(ntiles[:], ntiles[:], ROUND, None, ALU.subtract))
                dve.wait_ge(s["ones_set"], 1)
                link(dve.tensor_tensor_scan(tiles_upto[:], all_one[:], ntiles[:], 0.0, ALU.mult, ALU.add))
                link(dve.tensor_tensor(tiles_before[:], tiles_upto[:], ntiles[:], ALU.subtract))
                link(dve.tensor_tensor(pl2, up2, total, ALU.subtract))
                link(dve.tensor_tensor(pl2, pl2, within, ALU.add))
                link(dve.scalar_tensor_tensor(out=place[:], in0=spread(tiles_before[:].unsqueeze(2), 2, NCH),
                                              scalar=float(P), in1=place[:], op0=ALU.mult, op1=ALU.add))
                link(dve.tensor_tensor(place[:], place[:], hot[:], ALU.mult))
                link(dve.tensor_reduce(slot_f[:], place[:].rearrange("p e c -> p c e"), AX.X, ALU.add))
                dve.tensor_copy(slot[:], slot_f[:]).then_inc(s["slot_ready"], 1)
                link(dve.tensor_tensor(past[:], spread(route["tile_no"].unsqueeze(2), 2, EXPERTS),
                                       spread(tiles_upto[:].unsqueeze(1), 1, TILES), ALU.is_ge))
                link(dve.tensor_reduce(expert_f[:], past[:], AX.X, ALU.add))
                dve.tensor_scalar(expert_of[:], expert_f[:], float(EXPERTS - 1), None, ALU.min) \
                   .then_inc(s["expert_ready"], 1)
                for b in range(NCH // BLK):
                    if b + 1 < NCH // BLK:
                        shared_hidden(b + 1)
                    shared_add(b)

                def step(t, u, k, on):
                    if on(1):
                        j, v = t - 1, (u + 1) % 2
                        wait(dve, s["silr_ready"], j + 1)
                        wait(dve, s["hrt_psum"], j - 1)
                        dve.tensor_tensor(hr[:, v], silr[:, v], banks[:, 2 + v, FE:2 * FE], ALU.mult) \
                           .then_inc(s["hr_ready"], 1)
                    if on(3):
                        j, v, r = t - 3, (u + 1) % 2, (u + 1) % RING
                        wait(dve, s["y_psum"], j + 1)
                        wait(dve, stored[r], (k if u == UN - 1 else k - 1) * 16)
                        dve.tensor_copy(yt[:, r], banks[:, 6 + v, 0:P]).then_inc(s["yt_ready"], 1)
                run(step)(dve)
                dve.wait_ge(s["gathered"], 16 * NCH * (call + 1))
                dve.tensor_tensor(x[:], x[:], yg[:], ALU.add)


def oscillator(nc, a, x, eye, banks, w, tabs):
    NB, W = 4, T // 4
    HALF = 2
    ctx = ExitStack()
    with ctx:
        def sb(name, shape, dt=F32):
            return ctx.enter_context(nc.sbuf_tensor("osc_" + name, shape, dt))

        cos, dec, rdec = tabs["cos"], tabs["dec"], tabs["rdec"]
        stats = sb("stats", [P, NCH, 6])
        mv = sb("mv", [P, NCH, 2])
        var, vy, vt, rs = (sb(n, [P, NCH]) for n in ("var", "vy", "vt", "rs"))
        xn = sb("xn", [P, NCH, D])
        xT = sb("xT", [P, 3 + T])
        xc = sb("xc", [P, T])
        sq = sb("sq", [P, 4, 256])
        ss, sy, st, srs = (sb(n, [P, 64]) for n in ("ss", "sy", "st", "srs"))
        qn = sb("qn", [P, 4, 256])
        qT = sb("qT", [P, HALF, 1 + T])
        th = sb("th", [P, HALF, W])
        m = sb("m", [P, HALF, W])
        ak = sb("ak", [P, 2, HALF, W])
        mem = sb("mem", [P, 2, HALF, W])
        read = sb("read", [P, 2, HALF, W])
        one = sb("one", [P, W])
        ostats = sb("ostats", [P, 4, 6])
        omv = sb("omv", [P, 4, 2])
        ov, oy, ot, ors = (sb(n, [P, 4]) for n in ("ov", "oy", "ot", "ors"))
        on = sb("on", [P, 2, 4, D])

        s = {n: ctx.enter_context(nc.semaphore(f"osc_{n}")) for n in (
            "edges", "stats_done", "aggr_done", "rs_chain", "rs_ready", "xn_ready", "xt_psum", "xT_ready",
            "conv_chain", "xc_ready", "qk_ready", "sq_ready", "ss_ready", "q_chain", "q_rs", "qn_ready",
            "qt_psum", "qT_ready", "v_ready", "g_ready", "th_ready", "m_ready", "ak_ready", "kchain",
            "sum_chain", "mem_chain", "read_chain", "read_ready", "o_ready", "o_chain", "o_rs", "on_ready", "affine", "out_ready",
            "halved")}
        RL = RS_LINKS

        with nc.Block() as blk:
            @blk.gpsimd
            def _(pool):
                pool.memset(xT[:, 0:3], 0.0).then_inc(s["edges"], 1)
                pool.memset(qT[:, :, 0:1], 0.0).then_inc(s["edges"], 1)
                pool.memset(one[:], 1.0).then_inc(s["edges"], 1)
                pool.wait_ge(w["loaded"], 16 * w["count"])
                pool.tensor_scalar(w["g_b"][:], w["g_b"][:], 0.5, None, ALU.mult).then_inc(s["halved"], 1)
                pool.wait_ge(tabs["ready"], tabs["total"])

                def keys(b):
                    pool.wait_ge(s["qT_ready"], b + 1)
                    wait(pool, s["sum_chain"], b - 1)
                    blk_t = slice(W * b, W * b + W)
                    pool.tensor_tensor(ak[:, b % 2], cos[:, :, blk_t], qT[:, :, blk_t], ALU.add) \
                        .then_inc(s["kchain"], 1)
                    pool.wait_ge(s["kchain"], b + 1)
                    pool.tensor_tensor(ak[:, b % 2], ak[:, b % 2], dec[:, :, blk_t], ALU.mult) \
                        .then_inc(s["ak_ready"], 1)

                def affine(b):
                    pool.wait_ge(s["on_ready"], b + 1)
                    row = lambda n: spread(w[n][:].unsqueeze(1), 1, 4)
                    pool.tensor_tensor(on[:, b % 2], on[:, b % 2], row("ln_g"), ALU.mult) \
                        .then_inc(s["affine"], 1)
                    pool.wait_ge(s["affine"], 2 * b + 1)
                    pool.tensor_tensor(on[:, b % 2], on[:, b % 2], row("ln_b"), ALU.add) \
                        .then_inc(s["affine"], 1)
                for b in range(NB):
                    keys(b)
                    if b >= 1:
                        affine(b - 1)
                affine(NB - 1)

            @blk.scalar
            def _(act):
                act.wait_ge(s["edges"], 3)
                act.wait_ge(s["halved"], 1)
                for b in range(NB):
                    act.wait_ge(s["xt_psum"], b + 1)
                    act.activation(xT[:, 3 + W * b:3 + W * b + W], banks[:, b % 2, :], ACT.Copy) \
                       .then_inc(s["xT_ready"], 1)
                for b in range(NB):
                    act.wait_ge(s["qk_ready"], b + 1)
                    wait(act, s["ss_ready"], b)
                    act.activation(sq[:].rearrange("p a b -> p (a b)"),
                                   banks[:, 2:4, :].rearrange("p a b -> p (a b)"), ACT.Square) \
                       .then_inc(s["sq_ready"], 1)
                    act.wait_ge(s["g_ready"], b + 1)
                    wait(act, s["m_ready"], b)
                    for f in range(HALF):
                        ins = act.activation(th[:, f], banks[:, 6 + f, :], ACT.Tanh, scale=0.5,
                                             bias=w["g_b"][:, f:f + 1])
                    ins.then_inc(s["th_ready"], 1)
                    act.wait_ge(s["qt_psum"], b + 1)
                    for f in range(HALF):
                        ins = act.activation(qT[:, f, 1 + W * b:1 + W * b + W], banks[:, 2 + f, :], ACT.Copy)
                    ins.then_inc(s["qT_ready"], 1)

            @blk.tensor
            def _(pe):
                for b in range(NB):
                    pe.wait_ge(s["xn_ready"], 4 * b + 4)
                    wait(pe, s["xT_ready"], b - 1)
                    for c in range(4):
                        ins = pe.transpose(banks[:, b % 2, c * P:c * P + P], xn[:, 4 * b + c], eye)
                    ins.then_inc(s["xt_psum"], 1)
                pe.wait_ge(w["loaded"], 16 * w["count"])

                def out(b):
                    pe.wait_ge(s["read_ready"], b + 1)
                    if b == 0:
                        pe.wait_ge(s["xT_ready"], NB)
                    wait(pe, s["on_ready"], b)
                    for c in range(4):
                        for f in range(HALF):
                            ins = pe.matmul(banks[:, 1, c * P:c * P + P], read[:, b % 2, f, c * P:c * P + P],
                                            w["o"][:, f], start=(f == 0), stop=(f == 1))
                    ins.then_inc(s["o_ready"], 1)

                for b in range(NB):
                    pe.wait_ge(s["xc_ready"], b + 1)
                    wait(pe, s["qT_ready"], b)
                    for c in range(4):
                        at = W * b + c * P
                        ins = pe.matmul(banks[:, 2 + c // 2, (c % 2) * 256:(c % 2) * 256 + 256],
                                        xc[:, at:at + P], w["qk"][:], start=True, stop=True)
                    ins.then_inc(s["qk_ready"], 1)
                    rhs = xc[:, W * b:W * b + W]
                    wait(pe, s["th_ready"], b)
                    for f in range(HALF):
                        ins = pe.matmul(banks[:, 6 + f, :], w["g"][:, f], rhs, start=True, stop=True)
                    ins.then_inc(s["g_ready"], 1)
                    wait(pe, s["m_ready"], b)
                    for f in range(HALF):
                        ins = pe.matmul(banks[:, 4 + f, :], w["v"][:, f], rhs, start=True, stop=True)
                    ins.then_inc(s["v_ready"], 1)
                    pe.wait_ge(s["qn_ready"], b + 1)
                    for f in range(HALF):
                        for c in range(4):
                            ins = pe.transpose(banks[:, 2 + f, c * P:c * P + P],
                                               qn[:, c, f * P:f * P + P], eye)
                    ins.then_inc(s["qt_psum"], 1)
                    if b >= 1:
                        out(b - 1)
                out(NB - 1)

            @blk.vector
            def _(dve):
                for c in range(NCH):
                    dve.bn_stats(stats[:, c], x[:, c]).then_inc(s["stats_done"], 1)
                for c in range(NCH):
                    dve.wait_ge(s["stats_done"], c + 1)
                    ins = dve.bn_aggr(mv[:, c], stats[:, c])
                ins.then_inc(s["aggr_done"], 1)
                dve.wait_ge(s["aggr_done"], 1)
                dve.tensor_scalar(var[:], mv[:, :, 1], EPS, None, ALU.add).then_inc(s["rs_chain"], 1)
                dve.wait_ge(s["rs_chain"], 1)
                rsqrt_steps(dve, var[:], vy[:], vt[:], s["rs_chain"], 1, s["rs_ready"], rs[:])
                dve.wait_ge(s["rs_ready"], 1)
                for c in range(NCH):
                    dve.tensor_scalar(xn[:, c], x[:, c], mv[:, c, 0:1], rs[:, c:c + 1],
                                      ALU.subtract, ALU.mult).then_inc(s["xn_ready"], 1)
                dve.wait_ge(w["loaded"], 16 * w["count"])
                dve.wait_ge(tabs["ready"], tabs["total"])
                dve.wait_ge(s["edges"], 3)

                def conv(b):
                    dve.wait_ge(s["xT_ready"], b + 1)
                    dst = xc[:, W * b:W * b + W]
                    dve.tensor_scalar(dst, xT[:, 3 + W * b:3 + W * b + W], w["conv_w"][:, 3:4],
                                      w["conv_b"][:, 0:1], ALU.mult, ALU.add).then_inc(s["conv_chain"], 1)
                    for k in range(3):
                        dve.wait_ge(s["conv_chain"], 3 * b + k + 1)
                        dve.scalar_tensor_tensor(
                            out=dst, in0=xT[:, k + W * b:k + W * b + W], scalar=w["conv_w"][:, k:k + 1],
                            in1=dst, op0=ALU.mult, op1=ALU.add) \
                            .then_inc(s["conv_chain"] if k < 2 else s["xc_ready"], 1)

                def normalise(b):
                    dve.wait_ge(s["sq_ready"], b + 1)
                    dve.tensor_reduce(ss[:], sq[:].rearrange("p c (a d) -> p (c a) d", d=DH), AX.X,
                                      ALU.add).then_inc(s["ss_ready"], 1)
                    dve.wait_ge(s["ss_ready"], b + 1)
                    at = (RL + 1) * b
                    dve.tensor_scalar(ss[:], ss[:], 1e-24, None, ALU.max).then_inc(s["q_chain"], 1)
                    dve.wait_ge(s["q_chain"], at + 1)
                    rsqrt_steps(dve, ss[:], sy[:], st[:], s["q_chain"], at + 1, s["q_rs"], srs[:])
                    dve.wait_ge(s["q_rs"], b + 1)
                    wait(dve, s["qt_psum"], b)
                    for n in range(2):
                        ins = dve.tensor_tensor(
                            qn[:, 2 * n:2 * n + 2].rearrange("p c (a d) -> p (c a) d", d=DH),
                            banks[:, 2 + n, :].rearrange("p (a d) -> p a d", d=DH),
                            spread(srs[:, 32 * n:32 * n + 32].unsqueeze(2), 2, DH), ALU.mult)
                    ins.then_inc(s["qn_ready"], 1)

                def memory(b):
                    dve.wait_ge(s["th_ready"], b + 1)
                    dve.wait_ge(s["v_ready"], b + 1)
                    wait(dve, s["mem_chain"], 2 * b)
                    dve.scalar_tensor_tensor(out=m[:], in0=th[:], scalar=1.0, in1=banks[:, 4:6, :],
                                             op0=ALU.add, op1=ALU.mult).then_inc(s["m_ready"], 1)
                    dve.wait_ge(s["m_ready"], b + 1)
                    dve.wait_ge(s["ak_ready"], b + 1)
                    dve.tensor_tensor(m[:], m[:], ak[:, b % 2], ALU.mult).then_inc(s["sum_chain"], 1)
                    dve.wait_ge(s["sum_chain"], b + 1)
                    for f in range(HALF):
                        wait(dve, s["mem_chain"], 2 * b)
                        first = 0.0 if b == 0 else mem[:, (b - 1) % 2, f, W - 1:W]
                        dve.tensor_tensor_scan(mem[:, b % 2, f], one[:], m[:, f], first, ALU.mult,
                                               ALU.add).then_inc(s["mem_chain"], 1)
                    dve.wait_ge(s["mem_chain"], 2 * b + 2)
                    blk_t = slice(W * b, W * b + W)
                    wait(dve, s["o_ready"], b - 1)
                    dve.tensor_tensor(read[:, b % 2], mem[:, b % 2], rdec[:, :, blk_t], ALU.mult) \
                       .then_inc(s["read_chain"], 1)
                    dve.wait_ge(s["read_chain"], b + 1)
                    dve.tensor_tensor(read[:, b % 2], read[:, b % 2], qT[:, :, 1 + W * b:1 + W * b + W],
                                      ALU.mult).then_inc(s["read_ready"], 1)

                def norm_out(b):
                    dve.wait_ge(s["o_ready"], b + 1)
                    n = (RL + 9) * b
                    for c in range(4):
                        dve.bn_stats(ostats[:, c], banks[:, 1, c * P:c * P + P]).then_inc(s["o_chain"], 1)
                    for c in range(4):
                        dve.wait_ge(s["o_chain"], n + 1 + c)
                        dve.bn_aggr(omv[:, c], ostats[:, c]).then_inc(s["o_chain"], 1)
                    dve.wait_ge(s["o_chain"], n + 8)
                    dve.tensor_scalar(ov[:], omv[:, :, 1], EPS, None, ALU.add).then_inc(s["o_chain"], 1)
                    dve.wait_ge(s["o_chain"], n + 9)
                    rsqrt_steps(dve, ov[:], oy[:], ot[:], s["o_chain"], n + 9, s["o_rs"], ors[:])
                    dve.wait_ge(s["o_rs"], b + 1)
                    wait(dve, s["out_ready"], b - 1)
                    for c in range(4):
                        ins = dve.tensor_scalar(on[:, b % 2, c], banks[:, 1, c * P:c * P + P],
                                                omv[:, c, 0:1], ors[:, c:c + 1], ALU.subtract, ALU.mult)
                    ins.then_inc(s["on_ready"], 1)

                def add_out(b):
                    dve.wait_ge(s["affine"], 2 * b + 2)
                    part = x[:, 4 * b:4 * b + 4]
                    dve.tensor_tensor(part, part, on[:, b % 2], ALU.add).then_inc(s["out_ready"], 1)

                for b in range(NB):
                    conv(b)
                for b in range(NB):
                    normalise(b)
                    memory(b)
                    if b >= 1:
                        norm_out(b - 1)
                    if b >= 2:
                        add_out(b - 2)
                norm_out(NB - 1)
                add_out(NB - 2)
                add_out(NB - 1)


def oscillator_tables(nc, a, tabs, dram, ctx):
    def sb(name, shape, dt=F32):
        return ctx.enter_context(nc.sbuf_tensor("tab_" + name, shape, dt))

    times = sb("times", [P, T])
    freqs = sb("freqs", [P, 2])
    turns = sb("turns", [P, 2, T])
    gam = sb("gam", [16, 12])
    powers = sb("powers", [16, T])
    flat = sb("flat", [P, 256])
    rflat = sb("rflat", [P, 256])
    s = {n: ctx.enter_context(nc.semaphore("tab_" + n)) for n in (
        "loaded", "chain", "angles", "gamma", "powers_done", "powers_out", "powers_in", "inverse", "out",
        "angle_ready")}
    cos, dec, rdec = tabs["cos"], tabs["dec"], tabs["rdec"]
    two_pi = 2 * np.pi
    c1 = 6.28125
    c2 = float(np.float32(np.floor((two_pi - c1) * 2.0 ** 16) / 2.0 ** 16))
    c3 = float(np.float32(two_pi - c1 - c2))

    def sync(sp):
        sp.dma_start(times[:], a["times"].partition_broadcast(P)).then_inc(s["loaded"], 16)
        sp.dma_start(freqs[:], a["freqs"]).then_inc(s["loaded"], 16)
        sp.dma_start(gam[:, 0:1], a["gamma"].rearrange("h a b -> h (a b)")).then_inc(s["loaded"], 16)
        sp.wait_ge(s["powers_done"], 12)
        sp.dma_start(dram[0], powers[:]).then_inc(s["powers_out"], 16)
        sp.wait_ge(s["powers_out"], 16)
        sp.dma_start(flat[:], dram[0].rearrange("h (b t) -> (h b) t", t=256)).then_inc(s["powers_in"], 16)
        sp.wait_ge(s["inverse"], 3)
        sp.dma_start(dram[1].rearrange("h (b t) -> (h b) t", t=256), flat[:]).then_inc(s["out"], 16)
        sp.dma_start(dram[2].rearrange("h (b t) -> (h b) t", t=256), rflat[:]).then_inc(s["out"], 16)
        sp.wait_ge(s["out"], 32)
        for n, tab in ((1, dec), (2, rdec)):
            for f in range(2):
                for h in range(8):
                    sp.dma_start(tab[16 * h:16 * h + 16, f, :],
                                 dram[n][8 * f + h, :].partition_broadcast(16)).then_inc(tabs["ready"], 16)

    def pool_part(pool):
        pool.memset(powers[:, 0:1], 1.0).then_inc(s["powers_done"], 1)
        pool.wait_ge(s["loaded"], 48)
        for k in range(11):
            pool.wait_ge(s["powers_done"], k + 1)
            n = 1 << k
            pool.tensor_scalar(powers[:, n:2 * n], powers[:, 0:n], gam[:, k:k + 1], None, ALU.mult) \
                .then_inc(s["powers_done"], 1)
            pool.tensor_tensor(gam[:, k + 1:k + 2], gam[:, k:k + 1], gam[:, k:k + 1], ALU.mult) \
                .then_inc(s["gamma"], 1)
            pool.wait_ge(s["gamma"], k + 1)

    def vector_part(dve):
        n = [0]

        def link(ins):
            n[0] += 1
            ins.then_inc(s["chain"], 1)
            dve.wait_ge(s["chain"], n[0])

        dve.wait_ge(s["loaded"], 48)
        for f in range(2):
            link(dve.tensor_scalar(cos[:, f], times[:], freqs[:, f:f + 1], None, ALU.mult))
        link(dve.tensor_scalar(turns[:], cos[:], float(np.pi / 2), 1 / two_pi, ALU.add, ALU.mult))
        link(dve.tensor_scalar(turns[:], turns[:], ROUND, None, ALU.add))
        link(dve.tensor_scalar(turns[:], turns[:], ROUND, None, ALU.subtract))
        for c in (c1, c2, c3):
            link(dve.scalar_tensor_tensor(out=cos[:], in0=turns[:], scalar=-c, in1=cos[:], op0=ALU.mult,
                                          op1=ALU.add))
        link(dve.tensor_scalar(cos[:], cos[:], float(np.pi / 2), float(np.float32(3.1415925)), ALU.add,
                               ALU.min))
        dve.tensor_scalar(cos[:], cos[:], -float(np.float32(3.1415925)), None, ALU.max) \
           .then_inc(s["angle_ready"], 1)
        dve.wait_ge(s["powers_in"], 16)
        dve.tensor_scalar(rflat[:], flat[:], 1e-6, None, ALU.add).then_inc(s["inverse"], 1)
        dve.wait_ge(s["inverse"], 1)
        dve.reciprocal(rflat[:], rflat[:]).then_inc(s["inverse"], 1)
        dve.tensor_scalar(flat[:], flat[:], 0.5, None, ALU.mult).then_inc(s["inverse"], 1)

    def scalar_part(act):
        act.wait_ge(s["angle_ready"], 1)
        act.activation(cos[:], cos[:], ACT.Sin).then_inc(tabs["ready"], 16)

    tabs["total"] = 16 * 33
    return sync, pool_part, vector_part, scalar_part


UPTO = 9
NAMES = ("X", "Wq", "Wk", "Wv", "Wg", "Wo", "W1", "W2", "ln_scale", "ln_bias", "gn_scale", "gn_bias")


def kernel(**inputs):
    import concourse.bacc as bacc
    from concourse.bass_utils import run_bass_kernel_spmd

    nc = bacc.Bacc("TRN2", target_bir_lowering=False, num_devices=1)
    inputs = {n: np.asarray(v) for n, v in inputs.items()}
    arrays = {n: np.ascontiguousarray(inputs["L0_attn_a_" + n]) for n in NAMES}
    arrays["rot"], arrays["small"] = retention_tables()
    arrays["gateT"] = np.ascontiguousarray(inputs["L0_ffn_gate_w"].T)
    sh = [np.asarray(inputs["L0_ffn_shared_" + n]) for n in ("gate", "up", "down")]
    ro = [np.asarray(inputs["L0_ffn_r_" + n]) for n in ("gate", "up", "down")]
    arrays["s_gu"] = np.ascontiguousarray(np.concatenate([sh[0], sh[1]], 0).T).reshape(D, 4, P)
    arrays["s_down"] = np.ascontiguousarray(sh[2].T.reshape(2, P, D).transpose(1, 0, 2))
    arrays["r_gu"] = np.ascontiguousarray(np.concatenate([ro[0], ro[1]], 1).transpose(2, 0, 1))
    arrays["r_down"] = np.ascontiguousarray(ro[2].transpose(0, 2, 1).reshape(EXPERTS, 2, P, D)
                                            .transpose(2, 0, 1, 3))
    b = {n: inputs["L0_attn_b_" + n] for n in ("qk_w", "v_w", "g_w", "g_b", "o_w", "conv_w", "conv_b",
                                               "ln_g", "ln_b", "freqs", "gamma")}
    arrays["o_qk"] = np.ascontiguousarray(b["qk_w"].T)
    arrays["o_v"] = np.ascontiguousarray(b["v_w"].T).reshape(D, 2, P)
    arrays["o_g"] = np.ascontiguousarray(b["g_w"].T).reshape(D, 2, P)
    arrays["o_o"] = np.ascontiguousarray(b["o_w"].T.reshape(2, P, D).transpose(1, 0, 2))
    arrays["o_conv_w"] = np.ascontiguousarray(b["conv_w"].reshape(D, 4))
    arrays["o_g_b"] = np.ascontiguousarray(b["g_b"].reshape(2, P).T)
    for n in ("conv_b", "ln_g", "ln_b"):
        arrays["o_" + n] = b[n]
    arrays["freqs"] = np.ascontiguousarray(b["freqs"].reshape(2, P).T)
    arrays["gamma"] = b["gamma"]
    arrays["times"] = np.arange(T, dtype=np.float32)
    aps = {n: nc.dram_tensor("in_" + n, v.shape, mybir.dt.from_np(v.dtype), kind="ExternalInput").ap()
           for n, v in arrays.items()}
    out = nc.dram_tensor("out", (1, T, D), F32, kind="ExternalOutput").ap()
    build(nc, aps, out, UPTO)
    r = run_bass_kernel_spmd(nc, [{"in_" + n: v for n, v in arrays.items()}], core_ids=[0])
    return r.results[0]["out"]
```

```python
from contextlib import ExitStack

import numpy as np

import concourse.bass as bass
from concourse import mybir

ALU = mybir.AluOpType
ACT = mybir.ActivationFunctionType
AX = mybir.AxisListType
F32 = mybir.dt.float32
I32 = mybir.dt.int32

P = 128
T = 2048
NCH = T // P
D = 128
LAYERS, HEADS, DH, FA = 4, 8, 16, 256
GROUPS = NCH // 2
STEPS = LAYERS * GROUPS
EPS = 1e-5
RING = 4
EXPERTS, FE = 8, 256
TILES = NCH + EXPERTS
ROUND = 12582912.0
MAGIC = float(0x5F3759DF)


def routing_tables():
    earlier = (np.arange(P)[:, None] < np.arange(P)[None, :]).astype(np.float32)
    ones = np.ones((P, P), np.float32)
    rows = [EXPERTS - np.arange(EXPERTS), np.arange(TILES),
            (np.arange(EXPERTS * NCH) % NCH != 0)]
    return np.concatenate([earlier, ones] + [np.tile(r.astype(np.float32)[None], (P, 1)) for r in rows], 1)


def retention_tables():
    gam = (np.float32(1.0) - np.exp(np.linspace(np.log(1 / 32), np.log(1 / 64), HEADS))
           .astype(np.float32)).astype(np.float64)
    inv = (np.float32(1.0) / np.power(np.float32(10000.0), np.arange(0, DH, 2, dtype=np.float32)
                                      / np.float32(DH))).astype(np.float32)
    ang = (np.arange(T, dtype=np.float32)[:, None] * inv[None, :]).astype(np.float64)
    cos, sin = np.cos(ang), np.sin(ang)
    i = np.arange(T) % P
    up = gam[None, :] ** i[:, None]
    down = gam[None, :] ** (-i[:, None].astype(np.float64))
    ct = np.zeros((T, 2, HEADS, DH // 2, 2))
    st = np.zeros((T, 2, HEADS, DH // 2, 2))
    for a, (dec, sg) in enumerate(((up, 1.0), (down, -1.0))):
        ct[:, a] = (dec[:, :, None] * cos[:, None, :])[..., None]
        st[:, a, :, :, 0] = -sg * dec[:, :, None] * sin[:, None, :]
        st[:, a, :, :, 1] = sg * dec[:, :, None] * sin[:, None, :]
    rot = np.stack([ct.reshape(NCH, P, 256), st.reshape(NCH, P, 256)], 0)
    rot = np.ascontiguousarray(rot.transpose(2, 0, 1, 3)).astype(np.float32)
    head = np.arange(D) // DH
    hm = (head[:, None] == np.arange(HEADS)[None, :]).astype(np.float32)
    block = (head[:, None] == head[None, :]).astype(np.float32)
    causal = (np.arange(P)[:, None] <= np.arange(P)[None, :]).astype(np.float32)
    dec = np.repeat((gam[head] ** P)[:, None], NCH, 1)
    dec[:, NCH - 1] = 0.0
    eye = np.eye(P, dtype=np.float32)
    small = np.concatenate([eye, causal, block, hm, dec, routing_tables()], 1).astype(np.float32)
    return rot, np.ascontiguousarray(small)


def wait(eng, sem, value):
    if isinstance(value, int) and value <= 0:
        return
    eng.wait_ge(sem, value)


def spread(ap, axis, n):
    shape = list(ap.shape)
    shape[axis] = n
    return ap.broadcast_to(shape)


def build(nc, a, outs):
    ctx = ExitStack()
    with ctx:
        def sb(name, shape, dt=F32):
            return ctx.enter_context(nc.sbuf_tensor(name, shape, dt))

        def sem(name):
            return ctx.enter_context(nc.semaphore(name))

        xin = sb("xin", [P, NCH, D])
        resid = sb("resid", [P, NCH, D])
        stats = sb("next_stats", [P, NCH, 6])
        small = sb("small", [P, 5 * P + HEADS + NCH + EXPERTS + TILES + EXPERTS * NCH])
        eye, causal, block = small[:, 0:P], small[:, P:2 * P], small[:, 2 * P:3 * P]
        headmask = small[:, 3 * P:3 * P + HEADS]
        decay = small[:, 3 * P + HEADS:3 * P + HEADS + NCH]
        banks = ctx.enter_context(nc.psum_tensor("banks", [P, 8, 512], F32))

        at = 3 * P + HEADS + NCH
        route = {}
        for name, n in (("earlier", P), ("ones", P), ("rev", EXPERTS), ("tile_no", TILES),
                        ("restart", EXPERTS * NCH)):
            route[name] = small[:, at:at + n]
            at += n

        ffn_w = {
            "gate": sb("gate_sb", [P, EXPERTS]),
            "s_gu": sb("s_gu_sb", [P, 4, P]),
            "s_down": sb("s_down_sb", [P, 2, D]),
            "routed": sb("routed_sb", [P, EXPERTS, 2 * FE + 2 * D]),
        }
        rows_in = nc.dram_tensor("rows_in", (TILES * P, D), F32).ap()
        rows_out = nc.dram_tensor("rows_out", (TILES * P, D), F32).ap()

        ffn_sems = ffn_semaphores(nc, ctx)
        loaded_x = sem("loaded_x")
        loaded_small = sem("loaded_small")
        loaded_ffn = sem("loaded_ffn")
        retention(nc, a, xin, resid, stats, (eye, causal, block, headmask, decay), small, banks,
                  loaded_x, loaded_small, ffn_w, rows_in, loaded_ffn)
        tabs = {"cos": sb("cos_tab", [P, 2, T]), "dec": sb("dec_tab", [P, 2, T]),
                "rdec": sb("rdec_tab", [P, 2, T])}
        ow = {"qk": sb("qk_sb", [P, 256]), "v": sb("v_sb", [P, 2, P]), "g": sb("g_sb", [P, 2, P]),
              "o": sb("o_sb", [P, 2, D]), "g_b": sb("g_b_sb", [P, 2]), "conv_w": sb("conv_w_sb", [P, 4]),
              "conv_b": sb("conv_b_sb", [P, 1]), "ln_g": sb("ln_g_sb", [P, D]),
              "ln_b": sb("ln_b_sb", [P, D])}
        with ExitStack() as scratch:
            tables = OscillatorTables(nc, a, tabs, ow, sem, scratch)
            ffn(nc, 0, xin, stats, ffn_w, rows_in, rows_out, eye, route, banks, loaded_ffn, ffn_sems,
                tables, None)
        oscillator(nc, a, xin, stats, eye, banks, ow, tabs, ffn_sems)
        ffn(nc, 1, xin, stats, ffn_w, rows_in, rows_out, eye, route, banks, loaded_ffn, ffn_sems,
            None, outs)


def rsqrt_steps(eng, v, y, tmp, chain, count, done, out):
    n = count + 1
    eng.tensor_scalar(y.bitcast(I32), v.bitcast(I32), -0.5, MAGIC, ALU.mult, ALU.add).then_inc(chain, 1)
    yield
    eng.wait_ge(chain, n)
    for shift in (3.0, 12.0, 768.0):
        eng.tensor_tensor(tmp, y, y, ALU.mult).then_inc(chain, 1)
        yield
        eng.wait_ge(chain, n + 1)
        eng.tensor_tensor(tmp, tmp, v, ALU.mult).then_inc(chain, 1)
        yield
        eng.wait_ge(chain, n + 2)
        eng.scalar_tensor_tensor(out=y, in0=tmp, scalar=shift, in1=y, op0=ALU.subtract, op1=ALU.mult) \
           .then_inc(chain, 1)
        yield
        eng.wait_ge(chain, n + 3)
        n = n + 3
    eng.tensor_scalar(out, y, -1.0 / 8192.0, None, ALU.mult).then_inc(done, 1)


def rsqrt(*args):
    for _ in rsqrt_steps(*args):
        pass


RS_LINKS = 10


def retention(nc, a, xin, resid, out_stats, consts, small, banks, loaded_x, loaded_small, ffn_w, rows_in,
              loaded_ffn):
    eye, causal, block, headmask, decay = consts
    ctx = ExitStack()
    with ctx:
        def sb(name, shape, dt=F32):
            return ctx.enter_context(nc.sbuf_tensor(name, shape, dt))

        def sem(name):
            return ctx.enter_context(nc.semaphore(name))

        wqkvg = sb("wqkvg", [P, LAYERS, 4, D])
        wo = sb("wo", [P, LAYERS, D])
        w1 = sb("w1", [P, LAYERS, FA])
        w2 = sb("w2", [P, LAYERS, 2, D])
        rot = sb("rot", [P, 2, NCH, 256])
        lnsb = sb("lnsb", [P, 2])
        gns = sb("gns", [P, LAYERS, D])
        gnb = sb("gnb", [P, LAYERS, D])

        stats = sb("stats", [P, 4, 6])
        mv = sb("mv", [P, 4, 2])
        vv = sb("vv", [P, 20])
        vy = sb("vy", [P, 20])
        vt = sb("vt", [P, 20])
        rs = sb("rs", [P, 20])
        stats0 = sb("stats0", [P, NCH, 6])
        mv0 = sb("mv0", [P, NCH, 2])
        v0 = sb("v0", [P, NCH])
        y0 = sb("y0", [P, NCH])
        t0 = sb("t0", [P, NCH])
        rs0 = sb("rs0", [P, NCH])

        xz = sb("xz", [P, 4, D])
        xzT = sb("xzT", [P, 4, P])
        cosq = sb("cosq", [P, 2, 256])
        sinq = sb("sinq", [P, 2, 256])
        qk = sb("qk", [P, RING, 2, 2, D])
        qkT = sb("qkT", [P, RING, 2, 2, P])
        qexp = sb("qexp", [P, 2, 2, HEADS, P])
        ve = sb("ve", [P, RING, 2, 4, 2, 2, DH])
        th = sb("th", [P, RING, 2, D])
        gate = sb("gate", [P, RING, 2, D])
        gs = sb("gs", [P, RING, 2, D])
        gb = sb("gb", [P, RING, 2, D])
        att = sb("att", [P, 2, HEADS, P])
        state = sb("state", [P, 2, D])
        kvm = sb("kvm", [P, 2, D])
        yT = sb("yT", [P, 2, P])
        gsum = sb("gsum", [P, 16])
        yc = sb("yc", [P, RING, 2, D])
        sq = sb("sq", [P, 2, D])
        gyT = sb("gyT", [P, 2, P])
        h = sb("h", [P, 2, FA])
        hT = sb("hT", [P, 4, P])
        ytok = sb("ytok", [P, 2, 2 * D])
        zero_rows = sb("zero_rows", [P, TILES, D])

        b_qk, b_vg = banks[:, 0, :], banks[:, 1, :]
        b_att = banks[:, 2:4, :].rearrange("p b (h n) -> p (b h) n", n=P)
        b_y, b_sum, b_xz, b_t = banks[:, 4, :], banks[:, 5, :], banks[:, 6, :], banks[:, 7, :]

        s = {n: sem(n) for n in (
            "loaded_early_x", "loaded_early_rot", "loaded_first", "loaded_w", "zeroed", "halved",
            "start_chain", "start_rs", "resid_init",
            "qk_ready", "vg_ready", "qkt_ready", "att_ready", "kv_ready", "y_ready", "ytok_ready",
            "gyt_ready", "wo_ready", "xzt_ready", "w1_ready", "ht_ready", "w2_ready",
            "qkT_sb", "qexp_act", "att_raw", "yT_sb", "ytok_sb", "sq_ready", "gyT_sb", "xzT_sb", "v_sb",
            "h_sb", "hT_sb",
            "rot_sum", "qexp_ready", "att_masked_rest", "gsb_ready",
            "rot_ready", "gate_ready", "att_masked", "kv_taken", "state_ready", "gn_sum", "yc_ready",
            "var_ready", "bn_stats_done", "bn_aggr_done", "rs_chain", "rs_ready", "xz_ready",
            "gy_chain", "gy_ready", "yr_ready", "x_next", "joined")}
        EARLY = 4
        N_FIRST, N_W = 6, 12
        HALF = HEADS // 2
        ACT_HEADS = 5

        def pair(t, g):
            p2 = (g & (GROUPS - 1)) * 2
            return t[:, bass.ds(p2, 2), :]

        def layer(g):
            return (g >> 3) & (LAYERS - 1)

        LAG, PRO, UN = 7, 8, RING

        def run(step):
            def go(eng):
                for t in range(PRO):
                    step(t, t % UN, lambda n: t - n >= 0)
                with eng.Fori(PRO // UN, STEPS // UN, 1) as k:
                    for u in range(UN):
                        step(k * UN + u, u, lambda n: True)
                for t in range(STEPS, STEPS + LAG):
                    step(t, t % UN, lambda n: t - n < STEPS)
            return go

        with nc.Block() as blk:
            @blk.sync
            def _(sp):
                x_by_chunk = a["X"].rearrange("b (c p) d -> p (b c) d", p=P)
                sp.dma_start(xin[:, 0:EARLY], x_by_chunk[:, 0:EARLY]).then_inc(s["loaded_early_x"], 16)
                sp.dma_start(small[:], a["small"]).then_inc(loaded_small, 16)
                for n, name in enumerate(("Wq", "Wk", "Wv", "Wg")):
                    sp.dma_start(wqkvg[:, 0, n, :], a[name][0]).then_inc(s["loaded_first"], 16)
                for at in range(EARLY, NCH, 4):
                    sp.dma_start(rot[:, :, at:at + 4], a["rot"][:, :, at:at + 4]).then_inc(s["loaded_w"], 16)
                for n, name in enumerate(("Wq", "Wk", "Wv", "Wg")):
                    sp.dma_start(wqkvg[:, 1:, n, :], a[name][1:].rearrange("l c d -> c l d")) \
                      .then_inc(s["loaded_w"], 16)
                sp.dma_start(wo[:], a["Wo"].rearrange("l c d -> c l d")).then_inc(s["loaded_w"], 16)
                sp.dma_start(w1[:], a["W1"].rearrange("l c f -> c l f")).then_inc(s["loaded_w"], 16)
                sp.dma_start(w2[:], a["W2"].rearrange("l (f c) d -> c l f d", c=P)).then_inc(s["loaded_w"], 16)
                sp.dma_start(ffn_w["gate"][:], a["gateT"]).then_inc(loaded_ffn, 16)
                sp.dma_start(ffn_w["s_gu"][:], a["s_gu"]).then_inc(loaded_ffn, 16)
                sp.dma_start(ffn_w["s_down"][:], a["s_down"]).then_inc(loaded_ffn, 16)
                sp.dma_start(ffn_w["routed"][:], a["routed"]).then_inc(loaded_ffn, 16)
                sp.wait_ge(s["zeroed"], 3)
                sp.dma_start(rows_in.rearrange("(j p) d -> p j d", p=P), zero_rows[:]).then_inc(loaded_ffn, 16)

            @blk.scalar
            def _(act):
                act.dma_start(lnsb[:, 0:1], a["ln_scale"].rearrange("(c o) -> c o", o=1)) \
                   .then_inc(s["loaded_first"], 16)
                act.dma_start(lnsb[:, 1:2], a["ln_bias"].rearrange("(c o) -> c o", o=1)) \
                   .then_inc(s["loaded_first"], 16)
                act.dma_start(xin[:, EARLY:], a["X"].rearrange("b (c p) d -> p (b c) d", p=P)[:, EARLY:]) \
                   .then_inc(loaded_x, 16)
                act.dma_start(rot[:, :, 0:EARLY], a["rot"][:, :, 0:EARLY]).then_inc(s["loaded_early_rot"], 16)
                for dst, name in ((gns, "gn_scale"), (gnb, "gn_bias")):
                    act.dma_start(dst[:], a[name].partition_broadcast(P)).then_inc(s["loaded_w"], 16)
                act.wait_ge(s["loaded_first"], 16 * N_FIRST)

                def raw_scores(g, c):
                    wait(act, s["y_ready"], 2 * g + c - 1)
                    wait(act, s["att_ready"], 2 * g + c + 1)
                    act.activation(att[:, c, HALF:HEADS], b_att[:, HALF:HEADS], ACT.Copy) \
                       .then_inc(s["att_raw"], 1)

                def step(t, u, on):
                    if on(4):
                        g, v = t - 4, u % 2
                        wait(act, s["yc_ready"], g - 1)
                        wait(act, s["ytok_ready"], g + 1)
                        act.activation(ytok[:, v], b_y[:, 0:256], ACT.Copy).then_inc(s["ytok_sb"], 1)
                    if on(2):
                        g, v = t - 2, (u - 2) % RING
                        wait(act, s["qkt_ready"], g + 1)
                        wait(act, s["y_ready"], 2 * g - 6)
                        act.activation(qkT[:, v].rearrange("p a b c -> p (a b c)"), b_t, ACT.Copy) \
                           .then_inc(s["qkT_sb"], 1)
                    if on(2):
                        g, v = t - 2, (u - 2) % RING
                        wait(act, s["qkT_sb"], g + 1)
                        wait(act, s["att_ready"], 2 * g - 2)
                        for hd in range(ACT_HEADS):
                            ins = act.activation(qexp[:, v % 2, :, hd, :], qkT[:, v, 0], ACT.Copy,
                                                 scale=headmask[:, hd:hd + 1])
                        ins.then_inc(s["qexp_act"], 1)
                    if on(7):
                        g = t - 7
                        wait(act, s["ht_ready"], g + 1)
                        wait(act, s["w2_ready"], g)
                        act.activation(hT[:].rearrange("p a b -> p (a b)"), b_t, ACT.Copy) \
                           .then_inc(s["hT_sb"], 1)
                    if on(3):
                        raw_scores(t - 3, 1)
                    lo, hi = (0 if on(0) else 2), (4 if on(6) else 2)
                    if hi > lo:
                        wait(act, s["xzt_ready"], t + 1)
                        if on(7):
                            wait(act, s["w1_ready"], t - 6)
                        if on(1):
                            wait(act, s["qk_ready"], t)
                        act.activation(xzT[:, lo:hi].rearrange("p a b -> p (a b)"),
                                       b_xz[:, lo * P:hi * P], ACT.Identity,
                                       scale=lnsb[:, 0:1], bias=lnsb[:, 1:2]).then_inc(s["xzT_sb"], 1)
                    if on(3):
                        g = t - 3
                        wait(act, s["y_ready"], 2 * g + 2)
                        wait(act, s["ytok_ready"], g)
                        act.activation(yT[:].rearrange("p a b -> p (a b)"), b_y[:, 0:256], ACT.Copy) \
                           .then_inc(s["yT_sb"], 1)
                    if on(5):
                        g = t - 5
                        wait(act, s["gyt_ready"], g + 1)
                        wait(act, s["wo_ready"], g)
                        act.activation(gyT[:].rearrange("p a b -> p (a b)"), b_xz[:, 0:256], ACT.Copy) \
                           .then_inc(s["gyT_sb"], 1)
                    if on(4):
                        g, v = t - 4, (u - 4) % RING
                        wait(act, s["yc_ready"], g + 1)
                        wait(act, s["var_ready"], g)
                        act.activation(sq[:], yc[:, v], ACT.Square).then_inc(s["sq_ready"], 1)
                    if on(0):
                        g, v = t, u
                        wait(act, s["vg_ready"], g + 1)
                        wait(act, s["y_ready"], 2 * g - 6)
                        wait(act, s["gate_ready"], g - 3)
                        for c in range(2):
                            src = b_vg[:, 256 * c:256 * c + D].rearrange("p (q j d) -> p q j d", q=4, j=2)
                            dst = ve[:, v, c].rearrange("p q e j d -> p q (e j) d")[:, :, 0:4:3, :]
                            act.activation(dst, src, ACT.Copy)
                        act.activation(th[:, v], b_vg.rearrange("p (c a d) -> p c a d", c=2, a=2)[:, :, 1, :],
                                       ACT.Tanh, scale=0.5).then_inc(s["v_sb"], 1)
                    if on(2):
                        raw_scores(t - 2, 0)
                    if on(6):
                        g = t - 6
                        wait(act, s["w1_ready"], g + 1)
                        wait(act, s["ht_ready"], g)
                        act.activation(h[:].rearrange("p a b -> p (a b)"), b_t, ACT.Gelu_apprx_tanh) \
                           .then_inc(s["h_sb"], 1)

                run(step)(act)

            @blk.gpsimd
            def _(pool):
                pool.memset(ve[:], 0.0).then_inc(s["zeroed"], 1)
                pool.memset(state[:], 0.0).then_inc(s["zeroed"], 1)
                pool.memset(zero_rows[:], 0.0).then_inc(s["zeroed"], 1)
                pool.wait_ge(loaded_small, 16)

                def masked(g, c):
                    wait(pool, s["att_raw"], 2 * g + c + 1)
                    pool.tensor_tensor(att[:, c, HALF:HEADS], att[:, c, HALF:HEADS],
                                       spread(causal.unsqueeze(1), 1, HALF), ALU.mult) \
                        .then_inc(s["att_masked_rest"], 1)

                def step(t, u, on):
                    if on(2):
                        g, v = t - 2, (u - 2) % RING
                        wait(pool, s["qkT_sb"], g + 1)
                        wait(pool, s["att_ready"], 2 * g - 2)
                        pool.tensor_tensor(qexp[:, v % 2, :, ACT_HEADS, :], qkT[:, v, 0],
                                           headmask[:, ACT_HEADS:ACT_HEADS + 1].unsqueeze(1)
                                           .broadcast_to([P, 2, P]), ALU.mult)
                        for hd in range(ACT_HEADS + 1, HEADS):
                            ins = pool.tensor_scalar(qexp[:, v % 2, :, hd, :], qkT[:, v, 0],
                                                     headmask[:, hd:hd + 1], None, ALU.mult)
                        ins.then_inc(s["qexp_ready"], 1)
                    if on(3):
                        masked(t - 3, 1)
                    if isinstance(t, int) and t == 2:
                        pool.wait_ge(s["loaded_w"], 16 * N_W)
                        pool.tensor_scalar(gns[:], gns[:], 0.5, None, ALU.mult).then_inc(s["halved"], 1)
                        pool.tensor_scalar(gnb[:], gnb[:], 0.5, None, ALU.mult).then_inc(s["halved"], 1)
                        pool.wait_ge(s["halved"], 2)
                    if on(2):
                        wait(pool, s["gate_ready"], g + 1)
                        wait(pool, s["gy_ready"], g - 3)
                        for dst, tab in ((gs, gns), (gb, gnb)):
                            row = spread(tab[:, bass.ds(layer(g), 1), :], 1, 2)
                            ins = pool.tensor_tensor(dst[:, v], gate[:, v], row, ALU.mult)
                        ins.then_inc(s["gsb_ready"], 1)
                    if on(1):
                        g, v = t - 1, (u - 1) % RING
                        wait(pool, s["rot_ready"], g + 1)
                        wait(pool, s["kv_ready"], g - 3)
                        wait(pool, s["qkt_ready"], g - 3)
                        pool.tensor_tensor(qk[:, v].rearrange("p a b c -> p (a b c)"),
                                           cosq[:].rearrange("p a b -> p (a b)"),
                                           sinq[:].rearrange("p a b -> p (a b)"), ALU.add) \
                            .then_inc(s["rot_sum"], 1)
                    if on(2):
                        masked(t - 2, 0)

                run(step)(pool)

            @blk.tensor
            def _(pe):
                pe.wait_ge(s["loaded_first"], 16 * N_FIRST)
                pe.wait_ge(loaded_small, 16)
                pe.wait_ge(s["zeroed"], 2)

                def scores(g, v, c):
                    wait(pe, s["qexp_ready"], g + 1)
                    wait(pe, s["qexp_act"], g + 1)
                    wait(pe, s["att_raw"], 2 * g + c)
                    wait(pe, s["att_masked"], 2 * g + c)
                    for hh in range(2):
                        ins = pe.matmul(b_att[:, 4 * hh:4 * hh + 4, :], qkT[:, v, 1, c],
                                        qexp[:, v % 2, c, 4 * hh:4 * hh + 4, :], start=True, stop=True)
                    ins.then_inc(s["att_ready"], 1)

                def outputs(g, v, c):
                    wait(pe, s["state_ready"], 2 * g + c)
                    if c == 0:
                        wait(pe, s["ytok_sb"], g)
                    wait(pe, s["att_masked_rest"], 2 * g + c + 1)
                    wait(pe, s["att_masked"], 2 * g + c + 1)
                    out = b_y[:, c * P:c * P + P]
                    pe.matmul(out, state[:, c], qkT[:, v, 0, c], start=True, stop=False,
                              skip_group_check=True)
                    for e in range(2):
                        for q in range(4):
                            ins = pe.matmul(out[32 * q:32 * q + 32, :],
                                            ve[:, v, c, q, e].rearrange("p j d -> p (j d)"),
                                            att[:, c, 2 * q + e, :], start=False, stop=(e == 1),
                                            skip_group_check=True)
                    ins.then_inc(s["y_ready"], 1)

                def step(t, u, on):
                    w = (u - 3) % RING
                    if isinstance(t, int) and t == 5:
                        pe.wait_ge(s["loaded_w"], 16 * N_W)
                    if on(3):
                        g = t - 3
                        wait(pe, s["v_sb"], g + 1)
                        if on(6):
                            wait(pe, s["yr_ready"], t - 5)
                        for c in range(2):
                            plain = ve[:, w, c].rearrange("p q e j d -> p q (e j) d")[:, :, 0:4:3, :]
                            ins = pe.matmul(b_sum[:, c * P:c * P + P], qk[:, w, c, 1], plain,
                                            start=True, stop=True)
                        ins.then_inc(s["kv_ready"], 1)
                    if on(7):
                        if on(2):
                            wait(pe, s["qkT_sb"], t - 1)
                        wait(pe, s["h_sb"], t - 6)
                        for n in range(4):
                            ins = pe.transpose(b_t[:, n * P:n * P + P],
                                               h[:, n // 2, (n % 2) * P:(n % 2) * P + P], eye)
                        ins.then_inc(s["ht_ready"], 1)
                    if on(3):
                        scores(t - 3, w, 1)
                        outputs(t - 3, w, 0)
                    if on(7):
                        g = t - 7
                        if on(3):
                            wait(pe, s["kv_taken"], 2 * t - 4)
                        else:
                            wait(pe, s["yr_ready"], min(t - 5, STEPS))
                            wait(pe, s["x_next"], g)
                        wait(pe, s["hT_sb"], g + 1)
                        for c in range(2):
                            for f in range(2):
                                ins = pe.matmul(b_sum[:, c * P:c * P + P], hT[:, 2 * c + f],
                                                w2[:, bass.ds(layer(g), 1), f, :], start=(f == 0),
                                                stop=(f == 1))
                        ins.then_inc(s["w2_ready"], 1)
                    lo, hi = (0 if on(0) else 2), (4 if on(6) else 2)
                    if hi > lo:
                        if on(6):
                            wait(pe, s["gyT_sb"], t - 5)
                        wait(pe, s["xz_ready"], t + 1)
                        for n in range(lo, hi):
                            ins = pe.transpose(b_xz[:, n * P:n * P + P], xz[:, n], eye)
                        ins.then_inc(s["xzt_ready"], 1)
                    if on(3):
                        outputs(t - 3, w, 1)
                    if on(2):
                        scores(t - 2, (u - 2) % RING, 0)
                    if on(5):
                        g, v = t - 5, (u - 5) % RING
                        if hi > lo:
                            wait(pe, s["xzT_sb"], t + 1)
                        wait(pe, s["gy_ready"], g + 1)
                        for c in range(2):
                            ins = pe.transpose(b_xz[:, c * P:c * P + P], yc[:, v, c], eye)
                        ins.then_inc(s["gyt_ready"], 1)

                    def projections(bank, n, done):
                        for c in range(2):
                            ins = pe.matmul(bank[:, 256 * c:256 * c + 256], xzT[:, c],
                                            wqkvg[:, bass.ds(layer(t), 1), 2 * n:2 * n + 2, :],
                                            start=True, stop=True)
                        ins.then_inc(s[done], 1)

                    if on(0):
                        if not on(5):
                            wait(pe, s["xzT_sb"], t + 1)
                        wait(pe, s["gate_ready"], t)
                        projections(b_vg, 1, "vg_ready")
                    if on(5):
                        g = t - 5
                        if on(7):
                            wait(pe, s["x_next"], t - 6)
                        elif on(3):
                            wait(pe, s["kv_taken"], 2 * t - 4)
                        wait(pe, s["gyT_sb"], g + 1)
                        for c in range(2):
                            ins = pe.matmul(b_sum[:, c * P:c * P + P], gyT[:, c],
                                            wo[:, bass.ds(layer(g), 1), :], start=True, stop=True)
                        ins.then_inc(s["wo_ready"], 1)
                    if on(6):
                        if on(7):
                            wait(pe, s["hT_sb"], t - 6)
                        wait(pe, s["xzT_sb"], t + 1)
                        for c in range(2):
                            ins = pe.matmul(b_t[:, 256 * c:256 * c + 256], xzT[:, 2 + c],
                                            w1[:, bass.ds(layer(t - 6), 1), :], start=True, stop=True)
                        ins.then_inc(s["w1_ready"], 1)
                    if on(0):
                        wait(pe, s["rot_ready"], t)
                        projections(b_qk, 0, "qk_ready")
                    if on(3):
                        wait(pe, s["yT_sb"], t - 2)
                        for c in range(2):
                            ins = pe.transpose(b_y[:, c * P:c * P + P], yT[:, c], eye)
                        ins.then_inc(s["ytok_ready"], 1)
                    if on(1):
                        g, v = t - 1, (u - 1) % RING
                        if on(6):
                            wait(pe, s["h_sb"], t - 5)
                        elif on(2):
                            wait(pe, s["qkT_sb"], t - 1)
                        wait(pe, s["rot_sum"], g + 1)
                        for n in range(4):
                            ins = pe.transpose(b_t[:, n * P:n * P + P], qk[:, v, n % 2, n // 2], eye)
                        ins.then_inc(s["qkt_ready"], 1)

                run(step)(pe)

            @blk.vector
            def _(dve):
                dve.memset(mv[:], 1.0).then_inc(s["start_chain"], 1)
                dve.memset(vv[:], 1.0).then_inc(s["start_chain"], 1)
                dve.wait_ge(s["start_chain"], 2)

                def input_statistics(part, lo, hi, links):
                    for c in range(lo, hi):
                        ins = dve.bn_stats(stats0[:, c], xin[:, c])
                    ins.then_inc(s["start_chain"], 1)
                    dve.wait_ge(s["start_chain"], links + 1)
                    for c in range(lo, hi):
                        ins = dve.bn_aggr(mv0[:, c], stats0[:, c])
                    ins.then_inc(s["start_chain"], 1)
                    dve.wait_ge(s["start_chain"], links + 2)
                    dve.tensor_scalar(v0[:, lo:hi], mv0[:, lo:hi, 1], EPS, None, ALU.add) \
                       .then_inc(s["start_chain"], 1)
                    dve.wait_ge(s["start_chain"], links + 3)
                    rsqrt(dve, v0[:, lo:hi], y0[:, lo:hi], t0[:, lo:hi], s["start_chain"], links + 3,
                          s["start_rs"], rs0[:, lo:hi])

                def normalise_input(part, lo, hi):
                    dve.wait_ge(s["start_rs"], part + 1)
                    for c in range(lo, hi):
                        ins = dve.tensor_scalar(resid[:, c], xin[:, c], mv0[:, c, 0:1], rs0[:, c:c + 1],
                                                ALU.subtract, ALU.mult)
                    ins.then_inc(s["resid_init"], 1)
                    dve.wait_ge(s["resid_init"], part + 1)

                dve.wait_ge(s["loaded_early_x"], 16)
                input_statistics(0, 0, EARLY, 2)
                normalise_input(0, 0, EARLY)
                dve.wait_ge(s["zeroed"], 2)

                def masked(g, c):
                    wait(dve, s["y_ready"], 2 * g + c - 1)
                    wait(dve, s["att_ready"], 2 * g + c + 1)
                    dve.tensor_tensor(att[:, c, 0:HALF], b_att[:, 0:HALF],
                                      spread(causal.unsqueeze(1), 1, HALF), ALU.mult).then_inc(s["att_masked"], 1)

                def chunk_decay(g, c):
                    return decay[:, bass.ds((g & (GROUPS - 1)) * 2 + c, 1)]

                def keys_values(g, c):
                    wait(dve, s["state_ready"], 2 * g + c - 1)
                    wait(dve, s["kv_ready"], g + 1)
                    dve.scalar_tensor_tensor(out=kvm[:, c], in0=b_sum[:, c * P:c * P + P],
                                             scalar=chunk_decay(g, c), in1=block,
                                             op0=ALU.mult, op1=ALU.mult).then_inc(s["kv_taken"], 1)

                def new_state(g, c):
                    wait(dve, s["kv_taken"], 2 * g + c + 1)
                    wait(dve, s["state_ready"], 2 * g + c)
                    wait(dve, s["y_ready"], 2 * g + c)
                    dve.scalar_tensor_tensor(out=state[:, 1 - c], in0=state[:, c],
                                             scalar=chunk_decay(g, c), in1=kvm[:, c],
                                             op0=ALU.mult, op1=ALU.add).then_inc(s["state_ready"], 1)

                def gates(g, v):
                    wait(dve, s["gsb_ready"], g - 3)
                    wait(dve, s["v_sb"], g + 1)
                    dve.scalar_tensor_tensor(
                        out=gate[:, v], in0=th[:, v], scalar=1.0,
                        in1=b_vg.rearrange("p (c a d) -> p c a d", c=2, a=2)[:, :, 1, :],
                        op0=ALU.add, op1=ALU.mult).then_inc(s["gate_ready"], 1)

                def mlp_added(g):
                    wait(dve, s["w2_ready"], g + 1)
                    x0 = pair(resid, g)
                    dve.tensor_tensor(x0, b_sum[:, 0:256].rearrange("p (c d) -> p c d", c=2), x0,
                                      ALU.add).then_inc(s["x_next"], 1)

                def rotate_cos(g):
                    wait(dve, s["rot_sum"], g)
                    wait(dve, s["qk_ready"], g + 1)
                    p2 = (g & (GROUPS - 1)) * 2
                    dve.tensor_tensor(cosq[:], b_qk.rearrange("p (c n) -> p c n", c=2),
                                      rot[:, 0, bass.ds(p2, 2), :], ALU.mult)

                def rotate_sin(g):
                    p2 = (g & (GROUPS - 1)) * 2
                    other = b_qk.rearrange("p (n e) -> p n e", e=2)[:, :, ::-1]
                    dve.tensor_tensor(
                        sinq[:].rearrange("p c (n e) -> p (c n) e", e=2), other,
                        rot[:, 1].rearrange("p c (n e) -> p (c n) e", e=2)[:, bass.ds(p2 * P, 256), :],
                        ALU.mult).then_inc(s["rot_ready"], 1)

                def step(t, u, on):
                    if isinstance(t, int) and t == 1:
                        dve.wait_ge(loaded_x, 16)
                        input_statistics(1, EARLY, NCH, 2 + 3 + RS_LINKS)
                        dve.wait_ge(loaded_small, 16)
                        dve.wait_ge(s["loaded_early_rot"], 16)
                    if isinstance(t, int) and t == EARLY // 2:
                        normalise_input(1, EARLY, NCH)
                        dve.wait_ge(s["loaded_w"], 16 * N_W)
                    lo, hi = (0 if on(0) else 2), (4 if on(6) else 2)
                    v4, v5 = (u - 4) % RING, (u - 5) % RING
                    if on(0):
                        wait(dve, s["x_next"], t - 7)
                    if on(3):
                        masked(t - 3, 0)
                    if on(0):
                        for c in range(2):
                            ins = dve.bn_stats(stats[:, c], resid[:, bass.ds((t & 7) * 2 + c, 1), :])
                    if on(6):
                        g = t - 6
                        x2 = pair(resid, g)
                        wait(dve, s["wo_ready"], g + 1)
                        dve.tensor_tensor(x2, b_sum[:, 0:256].rearrange("p (c d) -> p c d", c=2), x2,
                                          ALU.add).then_inc(s["yr_ready"], 1)
                    if on(6):
                        wait(dve, s["yr_ready"], t - 5)
                    if on(5):
                        wait(dve, s["sq_ready"], t - 4)
                        dve.tensor_reduce(vv[:, 4:20], sq[:].rearrange("p c (a d) -> p (c a) d", d=DH),
                                          AX.X, ALU.add).then_inc(s["var_ready"], 1)
                    if on(6):
                        for c in range(2):
                            ins = dve.bn_stats(stats[:, 2 + c],
                                               resid[:, bass.ds(((t - 6) & 7) * 2 + c, 1), :])
                    if hi > lo:
                        ins.then_inc(s["bn_stats_done"], 1)
                        wait(dve, s["bn_stats_done"], t + 1)
                    chain = RS_LINKS + 2
                    if on(5):
                        wait(dve, s["var_ready"], t - 4)
                    dve.tensor_scalar(vv[:, 4:20], vv[:, 4:20], 1.0 / DH, EPS, ALU.mult, ALU.add) \
                       .then_inc(s["rs_chain"], 1)
                    if hi > lo:
                        for n in range(lo, hi):
                            ins = dve.bn_aggr(mv[:, n], stats[:, n])
                        ins.then_inc(s["bn_aggr_done"], 1)
                        wait(dve, s["bn_aggr_done"], t + 1)
                    dve.tensor_scalar(vv[:, 0:4], mv[:, :, 1], EPS, None, ALU.add) \
                       .then_inc(s["rs_chain"], 1)
                    dve.wait_ge(s["rs_chain"], chain * t + 2)
                    newton = rsqrt_steps(dve, vv[:], vy[:], vt[:], s["rs_chain"], chain * t + 2,
                                         s["rs_ready"], rs[:])
                    if on(3):
                        next(newton)
                        keys_values(t - 3, 0)
                        next(newton)
                        keys_values(t - 3, 1)
                        next(newton)
                        new_state(t - 3, 0)
                    if on(1):
                        next(newton)
                        gates(t - 1, (u - 1) % RING)
                    for _ in newton:
                        pass
                    dve.wait_ge(s["rs_ready"], t + 1)
                    if hi > lo:
                        wait(dve, s["xzt_ready"], t)
                        for n in range(lo, hi):
                            g = t if n < 2 else t - 6
                            ins = dve.tensor_scalar(xz[:, n], resid[:, bass.ds((g & 7) * 2 + n % 2, 1), :],
                                                    mv[:, n, 0:1], rs[:, n:n + 1],
                                                    ALU.subtract, ALU.mult)
                        ins.then_inc(s["xz_ready"], 1)
                    if on(3):
                        masked(t - 3, 1)
                    if on(5):
                        g, yv = t - 5, yc[:, v5].rearrange("p c (a d) -> p (c a) d", d=DH)
                        dve.tensor_tensor(yv, yv, spread(rs[:, 4:20].unsqueeze(2), 2, DH), ALU.mult) \
                           .then_inc(s["gy_chain"], 1)
                    if on(1):
                        rotate_cos(t - 1)
                    if on(5):
                        wait(dve, s["gsb_ready"], g + 1)
                        wait(dve, s["gy_chain"], 2 * g + 1)
                        dve.tensor_tensor(yc[:, v5], yc[:, v5], gs[:, v5], ALU.mult) \
                           .then_inc(s["gy_chain"], 1)
                    if on(1):
                        rotate_sin(t - 1)
                    if on(5):
                        wait(dve, s["gy_chain"], 2 * g + 2)
                        dve.tensor_tensor(yc[:, v5], yc[:, v5], gb[:, v5], ALU.add).then_inc(s["gy_ready"], 1)
                    y = ytok[:, u % 2].rearrange("p (a d) -> p a d", d=DH)
                    if on(4):
                        wait(dve, s["ytok_sb"], t - 3)
                        dve.tensor_reduce(gsum[:], y, AX.X, ALU.add).then_inc(s["gn_sum"], 1)
                    if on(7):
                        mlp_added(t - 7)
                    if on(4):
                        wait(dve, s["gyt_ready"], t - 7)
                        wait(dve, s["gn_sum"], t - 3)
                        dve.scalar_tensor_tensor(
                            out=yc[:, v4].rearrange("p c (a d) -> p (c a) d", d=DH),
                            in0=spread(gsum[:].unsqueeze(2), 2, DH),
                            scalar=-1.0 / DH, in1=y, op0=ALU.mult, op1=ALU.add).then_inc(s["yc_ready"], 1)
                    if on(3):
                        new_state(t - 3, 1)
                    if isinstance(t, int) and t >= STEPS:
                        for g in ([GROUPS - LAG - 1] if t == STEPS else []) + [GROUPS - LAG + t - STEPS]:
                            dve.wait_ge(s["x_next"], STEPS - GROUPS + g + 1)
                            p2 = slice(2 * g, 2 * g + 2)
                            dve.tensor_tensor(xin[:, p2], xin[:, p2], resid[:, p2], ALU.add) \
                               .then_inc(s["joined"], 1)
                            dve.wait_ge(s["joined"], g + 1)
                            for c in range(2 * g, 2 * g + 2):
                                dve.bn_stats(out_stats[:, c], xin[:, c])

                run(step)(dve)


def ffn_semaphores(nc, ctx):
    names = ("ones_set", "aggr_done", "rs_chain", "rs_ready", "xn_ready", "xnT_psum",
             "xnT_ready", "logits_ready", "route_chain", "hot_ready", "ranks_ready", "slot_ready",
             "expert_ready", "top_ready", "score_tanh", "xs_ready", "gate_psum", "up_psum", "gate_silu", "hs_ready",
             "shared_ready", "shared_added", "scattered", "xt_psum", "xtT_ready",
             "gu_ready", "silr_ready", "hr_ready", "y_psum", "yt_ready",
             "added", "out_stored", "wt_ready", "wt_rest")
    one = {n: ctx.enter_context(nc.semaphore("ffn_" + n)) for n in names}
    ring = {n: [ctx.enter_context(nc.semaphore(f"ffn_{n}{r}")) for r in range(RING)]
            for n in ("x_loaded", "stored", "gathered")}
    return {"one": one, **ring}


def clear_ffn_semaphores(pool, sems):
    for name, one in sems["one"].items():
        if name != "scattered":
            pool.sem_clear(one)
    for one in sems["x_loaded"] + sems["stored"]:
        pool.sem_clear(one)


def ffn(nc, call, x, stats, w, rows_in, rows_out, eye, route, banks, loaded_ffn, sems, tables, outs):
    BLK = 4
    ctx = ExitStack()
    with ctx:
        def sb(name, shape, dt=F32):
            return ctx.enter_context(nc.sbuf_tensor(f"ffn{call}_{name}", shape, dt))

        mv = sb("mv", [P, NCH, 2])
        var, vy, vt, rs = (sb(n, [P, NCH]) for n in ("var", "vy", "vt", "rs"))
        xn = sb("xn", [P, NCH, D])
        xnT = sb("xnT", [P, NCH, P])
        top_logit = sb("top_logit", [P, NCH])
        tied = sb("tied", [P, NCH, EXPERTS])
        first = sb("first", [P, NCH])
        hot = sb("hot", [P, EXPERTS, NCH])
        upto = sb("upto", [P, EXPERTS, NCH])
        place = sb("place", [P, EXPERTS, NCH])
        ntiles, tiles_upto, tiles_before, all_one = (sb(n, [P, EXPERTS]) for n in
                                                     ("ntiles", "tiles_upto", "tiles_before", "all_one"))
        slot_f = sb("slot_f", [P, NCH])
        slot = sb("slot", [P, NCH], mybir.dt.uint32)
        past = sb("past", [P, TILES, EXPERTS])
        expert_f = sb("expert_f", [P, TILES])
        expert_of = sb("expert_of", [P, TILES], I32)
        score = sb("score", [P, NCH])
        xs = sb("xs", [P, NCH, D])
        sil = sb("sil", [P, 2, 512])
        hs = sb("hs", [P, 2, 2, 512])
        s, x_loaded, stored, gathered = (sems[n] for n in ("one", "x_loaded", "stored", "gathered"))
        xt = sb("xt", [P, RING, D])
        xtT = sb("xtT", [P, 2, P])
        wt = sb("wt", [P, RING, 2 * FE + 2 * D])
        silr = sb("silr", [P, 2, FE])
        hr = sb("hr", [P, 2, FE])
        yt = sb("yt", [P, RING, D])
        yg = sb("yg", [P, NCH, D])

        POOL_COLS = 320
        LAG = 3
        PRO, UN = 8, 4

        def run(step):
            def go(eng):
                for t in range(PRO):
                    step(t, t % UN, t // UN, lambda lag: t - lag >= 0)
                with eng.Fori(PRO // UN, TILES // UN, 1) as k:
                    for u in range(UN):
                        step(k * UN + u, u, k, lambda lag: True)
                for t in range(TILES, TILES + LAG):
                    step(t, t % UN, t // UN, lambda lag: t - lag < TILES)
            return go

        with nc.Block() as blk:
            @blk.sync
            def _(sp):
                if tables:
                    tables.load(sp)
                sp.wait_ge(s["scattered"], 16 * NCH * (call + 1))

                def step(t, u, k, on):
                    if on(0):
                        wait(sp, s["xt_psum"], t - RING + 1)
                        if isinstance(t, int):
                            row = t * P
                            src = rows_in[row:row + P, :]
                        else:
                            src = rows_in[bass.ds(t * P, P), :]
                        sp.dma_start(xt[:, u], src).then_inc(x_loaded[u], 16)
                run(step)(sp)
                if tables:
                    tables.load_inverse(sp)
                if outs is not None:
                    rows = outs.rearrange("b (c p) d -> p (b c) d", p=P)
                    for b in range(NCH // BLK):
                        sp.wait_ge(s["added"], b + 1)
                        part = slice(BLK * b, BLK * b + BLK)
                        sp.dma_start(rows[:, part], x[:, part]).then_inc(s["out_stored"], 16)
                    sp.wait_ge(s["out_stored"], 16 * NCH // BLK)

            @blk.gpsimd
            def _(pool):
                pool.memset(all_one[:], 1.0).then_inc(s["ones_set"], 1)
                if tables:
                    tables.decays(pool)
                pool.wait_ge(s["slot_ready"], 1)
                pool.wait_ge(loaded_ffn, 16 * 5)
                for c in range(NCH):
                    pool.wait_ge(s["xs_ready"], c // BLK + 1)
                    pool.indirect_dma_start(
                        rows_in, bass.IndirectOffsetOnAxis(ap=slot[:, c:c + 1], axis=0),
                        xs[:, c], None).then_inc(s["scattered"], 16)
                pool.wait_ge(s["expert_ready"], 1)

                def step(t, u, k, on):
                    if on(0):
                        at = expert_of[0:1, t:t + 1] if isinstance(t, int) else \
                            expert_of[0:1, bass.ds(t, 1)]
                        e = pool.value_load(at, min_val=0, max_val=EXPERTS - 1)
                        wait(pool, s["y_psum"], t - RING + 1)
                        part = w["routed"][:, bass.ds(e, 1), 0:POOL_COLS]
                        pool.tensor_copy(wt[:, u, 0:POOL_COLS], part) \
                            .then_inc(s["wt_ready"], 1)
                run(step)(pool)
                for r in range(RING):
                    pool.wait_ge(stored[r], 16 * TILES // RING)
                for c in range(NCH):
                    pool.indirect_dma_start(
                        yg[:, c], None, rows_out,
                        bass.IndirectOffsetOnAxis(ap=slot[:, c:c + 1], axis=0)).then_inc(gathered[c // BLK], 16)

            @blk.scalar
            def _(act):
                for b in range(NCH // 4):
                    act.wait_ge(s["xnT_psum"], b + 1)
                    act.activation(xnT[:, 4 * b:4 * b + 4].rearrange("p a b -> p (a b)"), banks[:, b, :],
                                   ACT.Copy).then_inc(s["xnT_ready"], 1)
                act.wait_ge(s["top_ready"], 1)
                act.activation(score[:], top_logit[:], ACT.Tanh, scale=0.5).then_inc(s["score_tanh"], 1)
                for b in range(NCH // BLK):
                    act.wait_ge(s["gate_psum"], b + 1)
                    wait(act, s["hs_ready"], b)
                    act.activation(sil[:].rearrange("p a b -> p (a b)"),
                                   banks[:, 0:2, :].rearrange("p a b -> p (a b)"), ACT.Silu) \
                       .then_inc(s["gate_silu"], 1)

                def step(t, u, k, on):
                    if on(0):
                        v = u % 2
                        act.wait_ge(s["xt_psum"], t + 1)
                        wait(act, s["gu_ready"], t - 1)
                        act.activation(xtT[:, v], banks[:, v, 0:P], ACT.Copy).then_inc(s["xtT_ready"], 1)
                    if on(1):
                        j, v = t - 1, (u + 1) % 2
                        wait(act, s["gu_ready"], j + 1)
                        wait(act, s["hr_ready"], j - 1)
                        act.activation(silr[:, v], banks[:, 2 + v, 0:FE], ACT.Silu) \
                           .then_inc(s["silr_ready"], 1)
                    if on(3):
                        j = t - 3
                        wait(act, s["yt_ready"], j + 1)
                        dst = rows_out[j * P:j * P + P, :] if isinstance(j, int) else \
                            rows_out[bass.ds(j * P, P), :]
                        act.dma_start(dst, yt[:, (u - 3) % RING]).then_inc(stored[(u - 3) % RING], 16)
                run(step)(act)
                if tables:
                    tables.sine(act)

            @blk.tensor
            def _(pe):
                pe.wait_ge(loaded_ffn, 16 * 5)
                for b in range(NCH // 4):
                    pe.wait_ge(s["xn_ready"], 4 * b + 4)
                    for c in range(4 * b, 4 * b + 4):
                        ins = pe.transpose(banks[:, b, (c % 4) * P:(c % 4) * P + P], xn[:, c], eye)
                    ins.then_inc(s["xnT_psum"], 1)
                for c in range(NCH):
                    pe.wait_ge(s["xnT_ready"], c // 4 + 1)
                    ins = pe.matmul(banks[:, 4, c * EXPERTS:(c + 1) * EXPERTS], xnT[:, c], w["gate"][:],
                                    start=True, stop=True)
                ins.then_inc(s["logits_ready"], 1)

                def shared_up(b):
                    pe.wait_ge(s["xnT_ready"], NCH // 4)
                    rhs = xnT[:, BLK * b:BLK * b + BLK].rearrange("p a b -> p (a b)")
                    for first, freed, done in ((0, "gate_silu", "gate_psum"), (2, "hs_ready", "up_psum")):
                        wait(pe, s[freed], b)
                        for n in range(first, first + 2):
                            ins = pe.matmul(banks[:, n, :], w["s_gu"][:, n], rhs, start=True, stop=True)
                        ins.then_inc(s[done], 1)

                def shared_down(b):
                    pe.wait_ge(s["hs_ready"], b + 1)
                    wait(pe, s["shared_added"], b)
                    for c in range(BLK):
                        for f in range(2):
                            ins = pe.matmul(banks[:, 6, c * P:c * P + P], hs[:, b % 2, f, c * P:c * P + P],
                                            w["s_down"][:, f], start=(f == 0), stop=(f == 1))
                    ins.then_inc(s["shared_ready"], 1)

                pe.wait_ge(s["hot_ready"], 1)
                hot2 = hot[:].rearrange("p e c -> p (e c)")
                pe.matmul(banks[:, 5, 0:P], route["earlier"], hot2, start=True, stop=True)
                pe.matmul(banks[:, 5, P:2 * P], route["ones"], hot2, start=True, stop=True) \
                  .then_inc(s["ranks_ready"], 1)
                shared_up(0)
                for b in range(NCH // BLK):
                    if b + 1 < NCH // BLK:
                        shared_up(b + 1)
                    shared_down(b)

                pe.wait_ge(s["shared_added"], NCH // BLK)

                def step(t, u, k, on):
                    if on(0):
                        v = u % 2
                        wait(pe, x_loaded[u], k * 16 + 16)
                        wait(pe, s["xtT_ready"], t - 1)
                        pe.transpose(banks[:, v, 0:P], xt[:, u], eye).then_inc(s["xt_psum"], 1)
                    if on(1):
                        j, v = t - 1, (u + 1) % 2
                        wait(pe, s["wt_ready"], j + 1)
                        wait(pe, s["wt_rest"], j + 1)
                        wait(pe, s["xtT_ready"], j + 1)
                        wait(pe, s["hr_ready"], j - 1)
                        for n in range(4):
                            ins = pe.matmul(banks[:, 2 + v, n * P:n * P + P],
                                            wt[:, (u - 1) % RING, n * P:n * P + P], xtT[:, v],
                                            start=True, stop=True)
                        ins.then_inc(s["gu_ready"], 1)
                    if on(2):
                        j, v = t - 2, u % 2
                        wait(pe, s["yt_ready"], j - 1)
                        wait(pe, s["hr_ready"], j + 1)
                        for f in range(2):
                            ins = pe.matmul(banks[:, 4 + v, 0:P], hr[:, v, f * P:f * P + P],
                                            wt[:, (u - 2) % RING, 2 * FE + f * D:2 * FE + f * D + D],
                                            start=(f == 0), stop=(f == 1))
                        ins.then_inc(s["y_psum"], 1)
                run(step)(pe)

            @blk.vector
            def _(dve):
                for c in range(NCH):
                    ins = dve.bn_aggr(mv[:, c], stats[:, c])
                ins.then_inc(s["aggr_done"], 1)
                dve.wait_ge(s["aggr_done"], 1)
                dve.tensor_scalar(var[:], mv[:, :, 1], EPS, None, ALU.add).then_inc(s["rs_chain"], 1)
                dve.wait_ge(s["rs_chain"], 1)
                rsqrt(dve, var[:], vy[:], vt[:], s["rs_chain"], 1, s["rs_ready"], rs[:])
                dve.wait_ge(s["rs_ready"], 1)
                for c in range(NCH):
                    dve.tensor_scalar(xn[:, c], x[:, c], mv[:, c, 0:1], rs[:, c:c + 1],
                                      ALU.subtract, ALU.mult).then_inc(s["xn_ready"], 1)

                n = [0]

                def link(ins):
                    n[0] += 1
                    ins.then_inc(s["route_chain"], 1)
                    dve.wait_ge(s["route_chain"], n[0])

                if tables:
                    tables.angle(dve)
                rev = route["rev"]
                logits = banks[:, 4, 0:NCH * EXPERTS].rearrange("p (c e) -> p c e", e=EXPERTS)
                dve.wait_ge(s["logits_ready"], 1)
                dve.tensor_reduce(top_logit[:], logits, AX.X, ALU.max).then_inc(s["top_ready"], 1)
                dve.wait_ge(s["top_ready"], 1)
                link(dve.tensor_tensor(tied[:], logits, spread(top_logit[:].unsqueeze(2), 2, EXPERTS),
                                       ALU.is_equal))
                link(dve.tensor_tensor(tied[:], tied[:], spread(rev.unsqueeze(1), 1, NCH), ALU.mult))
                link(dve.tensor_reduce(first[:], tied[:], AX.X, ALU.max))
                dve.tensor_tensor(hot[:], spread(first[:].unsqueeze(1), 1, EXPERTS),
                                  spread(rev.unsqueeze(2), 2, NCH), ALU.is_equal).then_inc(s["hot_ready"], 1)

                def shared_hidden(b):
                    dve.wait_ge(s["gate_silu"], b + 1)
                    dve.wait_ge(s["up_psum"], b + 1)
                    wait(dve, s["shared_ready"], b - 1)
                    dve.tensor_tensor(hs[:, b % 2], sil[:], banks[:, 2:4, :], ALU.mult) \
                       .then_inc(s["hs_ready"], 1)

                def shared_add(b):
                    dve.wait_ge(s["shared_ready"], b + 1)
                    part = x[:, BLK * b:BLK * b + BLK]
                    dve.tensor_tensor(part, part, banks[:, 6, :].rearrange("p (c d) -> p c d", c=BLK),
                                      ALU.add).then_inc(s["shared_added"], 1)

                def scaled(b):
                    part = slice(BLK * b, BLK * b + BLK)
                    dve.tensor_tensor(xs[:, part], xn[:, part], spread(score[:, part].unsqueeze(2), 2, D),
                                      ALU.mult).then_inc(s["xs_ready"], 1)

                dve.wait_ge(s["score_tanh"], 1)
                link(dve.tensor_scalar(score[:], score[:], 0.5, 0.5, ALU.mult, ALU.add))
                scaled(0)
                dve.wait_ge(s["ranks_ready"], 1)
                within, total = banks[:, 5, 0:P], banks[:, 5, P:2 * P]
                up2, pl2 = upto[:].rearrange("p e c -> p (e c)"), place[:].rearrange("p e c -> p (e c)")
                link(dve.tensor_tensor_scan(up2, route["restart"], total, 0.0, ALU.mult, ALU.add))
                link(dve.tensor_scalar(ntiles[:], upto[:, :, NCH - 1], 63.5, 1.0 / P, ALU.add, ALU.mult))
                link(dve.tensor_scalar(ntiles[:], ntiles[:], ROUND, None, ALU.add))
                link(dve.tensor_scalar(ntiles[:], ntiles[:], ROUND, None, ALU.subtract))
                dve.wait_ge(s["ones_set"], 1)
                link(dve.tensor_tensor_scan(tiles_upto[:], all_one[:], ntiles[:], 0.0, ALU.mult, ALU.add))
                link(dve.tensor_tensor(tiles_before[:], tiles_upto[:], ntiles[:], ALU.subtract))
                link(dve.tensor_tensor(pl2, up2, total, ALU.subtract))
                link(dve.tensor_tensor(pl2, pl2, within, ALU.add))
                link(dve.scalar_tensor_tensor(out=place[:], in0=spread(tiles_before[:].unsqueeze(2), 2, NCH),
                                              scalar=float(P), in1=place[:], op0=ALU.mult, op1=ALU.add))
                link(dve.tensor_tensor(place[:], place[:], hot[:], ALU.mult))
                link(dve.tensor_reduce(slot_f[:], place[:].rearrange("p e c -> p c e"), AX.X, ALU.add))
                dve.tensor_copy(slot[:], slot_f[:]).then_inc(s["slot_ready"], 1)
                for b in range(1, NCH // BLK):
                    scaled(b)
                shared_hidden(0)
                link(dve.tensor_tensor(past[:], spread(route["tile_no"].unsqueeze(2), 2, EXPERTS),
                                       spread(tiles_upto[:].unsqueeze(1), 1, TILES), ALU.is_ge))
                link(dve.tensor_reduce(expert_f[:], past[:], AX.X, ALU.add))
                dve.tensor_scalar(expert_of[:], expert_f[:], float(EXPERTS - 1), None, ALU.min) \
                   .then_inc(s["expert_ready"], 1)
                dve.wait_ge(s["expert_ready"], 1)
                for b in range(NCH // BLK):
                    if b + 1 < NCH // BLK:
                        shared_hidden(b + 1)
                        if tables and b == 0:
                            tables.last_decays(dve)
                        elif tables:
                            tables.whole_turns(dve, b - 1)
                    elif tables:
                        tables.whole_turns(dve, 2)
                    shared_add(b)

                def step(t, u, k, on):
                    if on(0):
                        at = expert_of[0:1, t:t + 1] if isinstance(t, int) else \
                            expert_of[0:1, bass.ds(t, 1)]
                        e = dve.value_load(at, min_val=0, max_val=EXPERTS - 1)
                        wait(dve, s["y_psum"], t - RING + 1)
                        dve.tensor_copy(wt[:, u, POOL_COLS:], w["routed"][:, bass.ds(e, 1), POOL_COLS:]) \
                           .then_inc(s["wt_rest"], 1)
                    if on(1):
                        j, v = t - 1, (u + 1) % 2
                        wait(dve, s["silr_ready"], j + 1)
                        wait(dve, s["y_psum"], j - 1)
                        dve.tensor_tensor(hr[:, v], silr[:, v], banks[:, 2 + v, FE:2 * FE], ALU.mult) \
                           .then_inc(s["hr_ready"], 1)
                    if on(2):
                        j, v, r = t - 2, u % 2, (u - 2) % RING
                        wait(dve, s["y_psum"], j + 1)
                        wait(dve, stored[r], (k if u >= 2 else k - 1) * 16)
                        dve.tensor_copy(yt[:, r], banks[:, 4 + v, 0:P]).then_inc(s["yt_ready"], 1)
                run(step)(dve)
                if tables:
                    tables.inverse(dve)
                    tables.finish(dve)
                for b in range(NCH // BLK):
                    part = slice(BLK * b, BLK * b + BLK)
                    dve.wait_ge(gathered[b], 16 * BLK * (call + 1))
                    dve.tensor_tensor(x[:, part], x[:, part], yg[:, part], ALU.add).then_inc(s["added"], 1)
                    if call == 0:
                        dve.wait_ge(s["added"], b + 1)
                        for c in range(BLK * b, BLK * b + BLK):
                            dve.bn_stats(stats[:, c], x[:, c])


def oscillator(nc, a, x, stats, eye, banks, w, tabs, ffn_sems):
    NB, W = 4, T // 4
    HALF = 2
    OUT_BANKS = (1, 1, 1, 0)
    XT_BANKS = (1, 4, 5, 6)
    ctx = ExitStack()
    with ctx:
        def sb(name, shape, dt=F32):
            return ctx.enter_context(nc.sbuf_tensor("osc_" + name, shape, dt))

        cos, dec, rdec = tabs["cos"], tabs["dec"], tabs["rdec"]
        mv = sb("mv", [P, NCH, 2])
        var, vy, vt, rs = (sb(n, [P, NCH]) for n in ("var", "vy", "vt", "rs"))
        xn = sb("xn", [P, NCH, D])
        xT = sb("xT", [P, 3 + T])
        xc = sb("xc", [P, T])
        taps = sb("taps", [P, 4, P])
        sq = sb("sq", [P, 4, 256])
        ss, sy, st, srs = (sb(n, [P, 64]) for n in ("ss", "sy", "st", "srs"))
        qn = sb("qn", [P, 2, 4, 256])
        qT = sb("qT", [P, HALF, 1 + T])
        th = sb("th", [P, HALF, W])
        m = sb("m", [P, HALF, W])
        ak = sb("ak", [P, 2, HALF, W])
        mem = sb("mem", [P, 2, HALF, W])
        qr = sb("qr", [P, 2, HALF, W])
        read = sb("read", [P, 2, HALF, W])
        one = sb("one", [P, W])
        ostats = sb("ostats", [P, 4, 6])
        omv = sb("omv", [P, 4, 2])
        ov, oy, ot, ors = (sb(n, [P, 4]) for n in ("ov", "oy", "ot", "ors"))
        on = sb("on", [P, 2, 4, D])

        s = {n: ctx.enter_context(nc.semaphore(f"osc_{n}")) for n in (
            "edges", "aggr_done", "rs_chain", "rs_ready", "xn_ready", "xt_psum", "xT_ready",
            "taps_ready", "conv_ready", "qr_ready", "xc_ready", "qk_ready", "sq_ready", "raw_ready",
            "ss_ready", "q_chain", "q_rs", "qn_ready",
            "qt_psum", "qT_ready", "v_ready", "g_ready", "th_ready", "m_ready", "ak_ready", "kchain",
            "sum_chain", "mem_chain", "read_ready", "o_ready", "o_chain", "o_rs", "on_ready", "affine", "out_ready",
            "halved")}
        RL = RS_LINKS

        def affine(eng, b):
            eng.wait_ge(s["on_ready"], b + 1)
            row = lambda n: spread(w[n][:].unsqueeze(1), 1, 4)
            eng.tensor_tensor(on[:, b % 2], on[:, b % 2], row("ln_g"), ALU.mult).then_inc(s["affine"], 1)
            eng.wait_ge(s["affine"], 2 * b + 1)
            eng.tensor_tensor(on[:, b % 2], on[:, b % 2], row("ln_b"), ALU.add).then_inc(s["affine"], 1)

        with nc.Block() as blk:
            @blk.gpsimd
            def _(pool):
                pool.memset(xT[:, 0:3], 0.0).then_inc(s["edges"], 1)
                pool.memset(qT[:, :, 0:1], 0.0).then_inc(s["edges"], 1)
                pool.memset(one[:], 1.0).then_inc(s["edges"], 1)
                pool.tensor_scalar(w["g_b"][:], w["g_b"][:], 0.5, None, ALU.mult).then_inc(s["halved"], 1)

                for k in range(4):
                    pool.tensor_scalar(taps[:, k], eye, w["conv_w"][:, k:k + 1], None, ALU.mult) \
                        .then_inc(s["taps_ready"], 1)

                def keys(b):
                    pool.wait_ge(s["qT_ready"], b + 1)
                    wait(pool, s["sum_chain"], b - 1)
                    blk_t = slice(W * b, W * b + W)
                    pool.tensor_tensor(ak[:, b % 2], cos[:, :, blk_t], qT[:, :, blk_t], ALU.add) \
                        .then_inc(s["kchain"], 1)
                    pool.wait_ge(s["kchain"], b + 1)
                    pool.tensor_tensor(ak[:, b % 2], ak[:, b % 2], dec[:, :, blk_t], ALU.mult) \
                        .then_inc(s["ak_ready"], 1)
                    wait(pool, s["read_ready"], b - 1)
                    pool.tensor_tensor(qr[:, b % 2], rdec[:, :, blk_t],
                                       qT[:, :, 1 + W * b:1 + W * b + W], ALU.mult) \
                        .then_inc(s["qr_ready"], 1)

                for b in range(NB + 2):
                    if b < NB:
                        keys(b)
                    if 2 <= b <= NB:
                        affine(pool, b - 2)
                clear_ffn_semaphores(pool, ffn_sems)

            @blk.scalar
            def _(act):
                act.wait_ge(s["edges"], 3)
                act.wait_ge(s["halved"], 1)
                def transposed(b):
                    act.wait_ge(s["xt_psum"], b + 1)
                    act.activation(xT[:, 3 + W * b:3 + W * b + W], banks[:, XT_BANKS[b], :], ACT.Copy) \
                       .then_inc(s["xT_ready"], 1)

                def convolved(b):
                    act.wait_ge(s["conv_ready"], b + 1)
                    act.activation(xc[:, W * b:W * b + W], banks[:, 0, :], ACT.Identity,
                                   bias=w["conv_b"][:, 0:1]).then_inc(s["xc_ready"], 1)

                def squares(b):
                    raw = banks[:, 2:4, :].rearrange("p a b -> p (a b)")
                    act.wait_ge(s["qk_ready"], b + 1)
                    wait(act, s["ss_ready"], b)
                    act.activation(sq[:].rearrange("p a b -> p (a b)"), raw, ACT.Square) \
                       .then_inc(s["sq_ready"], 1)
                    wait(act, s["qt_psum"], b - 1)
                    act.activation(qn[:, b % 2].rearrange("p a b -> p (a b)"), raw, ACT.Copy) \
                       .then_inc(s["raw_ready"], 1)

                def gate(b):
                    act.wait_ge(s["g_ready"], b + 1)
                    wait(act, s["m_ready"], b)
                    for f in range(HALF):
                        ins = act.activation(th[:, f], banks[:, 6 + f, :], ACT.Tanh, scale=0.5,
                                             bias=w["g_b"][:, f:f + 1])
                    ins.then_inc(s["th_ready"], 1)

                def by_channel(b):
                    act.wait_ge(s["qt_psum"], b + 1)
                    act.activation(qT[:, :, 1 + W * b:1 + W * b + W], banks[:, 2:4, :], ACT.Copy) \
                       .then_inc(s["qT_ready"], 1)

                transposed(0)
                transposed(1)
                convolved(0)
                transposed(2)
                transposed(3)
                squares(0)
                convolved(1)
                gate(0)
                squares(1)
                for b in range(NB):
                    by_channel(b)
                    if b + 2 < NB:
                        convolved(b + 2)
                        squares(b + 2)
                    if b + 1 < NB:
                        gate(b + 1)

            @blk.tensor
            def _(pe):
                pe.wait_ge(s["taps_ready"], 4)
                pe.wait_ge(s["edges"], 3)

                def convolution(b):
                    pe.wait_ge(s["xT_ready"], b + 1)
                    wait(pe, s["xc_ready"], b)
                    for k in range(4):
                        at = k + W * b
                        ins = pe.matmul(banks[:, 0, :], taps[:, k], xT[:, at:at + W],
                                        start=(k == 0), stop=(k == 3))
                    ins.then_inc(s["conv_ready"], 1)

                def transposes(b):
                    pe.wait_ge(s["xn_ready"], 4 * b + 4)
                    for c in range(4):
                        ins = pe.transpose(banks[:, XT_BANKS[b], c * P:c * P + P], xn[:, 4 * b + c], eye)
                    ins.then_inc(s["xt_psum"], 1)

                def queries_keys(b):
                    pe.wait_ge(s["xc_ready"], b + 1)
                    if b == 1:
                        pe.wait_ge(s["sq_ready"], 1)
                        pe.wait_ge(s["raw_ready"], 1)
                    elif b > 1:
                        pe.wait_ge(s["qT_ready"], b - 1)
                    for c in range(4):
                        at = W * b + c * P
                        ins = pe.matmul(banks[:, 2 + c // 2, (c % 2) * 256:(c % 2) * 256 + 256],
                                        xc[:, at:at + P], w["qk"][:], start=True, stop=True)
                    ins.then_inc(s["qk_ready"], 1)

                def gates(b):
                    wait(pe, s["th_ready"], b)
                    if b == 0:
                        pe.wait_ge(s["xT_ready"], NB)
                    for f in range(HALF):
                        ins = pe.matmul(banks[:, 6 + f, :], w["g"][:, f], xc[:, W * b:W * b + W],
                                        start=True, stop=True)
                    ins.then_inc(s["g_ready"], 1)

                def values(b):
                    wait(pe, s["m_ready"], b)
                    for f in range(HALF):
                        ins = pe.matmul(banks[:, 4 + f, :], w["v"][:, f], xc[:, W * b:W * b + W],
                                        start=True, stop=True)
                    ins.then_inc(s["v_ready"], 1)

                def by_channel(b):
                    pe.wait_ge(s["qn_ready"], b + 1)
                    pe.wait_ge(s["sq_ready"], min(b + 2, NB))
                    pe.wait_ge(s["raw_ready"], min(b + 2, NB))
                    if b == NB - 1:
                        pe.wait_ge(s["qT_ready"], b)
                    for f in range(HALF):
                        for c in range(4):
                            ins = pe.transpose(banks[:, 2 + f, c * P:c * P + P],
                                               qn[:, b % 2, c, f * P:f * P + P], eye)
                    ins.then_inc(s["qt_psum"], 1)

                def out(b):
                    pe.wait_ge(s["read_ready"], b + 1)
                    if b < NB - 1:
                        wait(pe, s["on_ready"], b)
                    else:
                        pe.wait_ge(s["xc_ready"], NB)
                    for c in range(4):
                        for f in range(HALF):
                            ins = pe.matmul(banks[:, OUT_BANKS[b], c * P:c * P + P], read[:, b % 2, f, c * P:c * P + P],
                                            w["o"][:, f], start=(f == 0), stop=(f == 1))
                    ins.then_inc(s["o_ready"], 1)

                transposes(0)
                transposes(1)
                convolution(0)
                transposes(2)
                transposes(3)
                queries_keys(0)
                convolution(1)
                gates(0)
                queries_keys(1)
                values(0)
                for b in range(NB):
                    by_channel(b)
                    if b + 2 < NB:
                        convolution(b + 2)
                    if b + 1 < NB:
                        gates(b + 1)
                    if b + 2 < NB:
                        queries_keys(b + 2)
                    if b >= 1:
                        out(b - 1)
                    if b + 1 < NB:
                        values(b + 1)
                out(NB - 1)

            @blk.vector
            def _(dve):
                for c in range(NCH):
                    ins = dve.bn_aggr(mv[:, c], stats[:, c])
                ins.then_inc(s["aggr_done"], 1)
                dve.wait_ge(s["aggr_done"], 1)
                dve.tensor_scalar(var[:], mv[:, :, 1], EPS, None, ALU.add).then_inc(s["rs_chain"], 1)
                dve.wait_ge(s["rs_chain"], 1)
                rsqrt(dve, var[:], vy[:], vt[:], s["rs_chain"], 1, s["rs_ready"], rs[:])
                dve.wait_ge(s["rs_ready"], 1)
                for c in range(NCH):
                    dve.tensor_scalar(xn[:, c], x[:, c], mv[:, c, 0:1], rs[:, c:c + 1],
                                      ALU.subtract, ALU.mult).then_inc(s["xn_ready"], 1)
                dve.wait_ge(s["edges"], 3)

                def gated(b):
                    dve.wait_ge(s["th_ready"], b + 1)
                    dve.wait_ge(s["v_ready"], b + 1)
                    wait(dve, s["mem_chain"], 2 * b)
                    dve.scalar_tensor_tensor(out=m[:], in0=th[:], scalar=1.0, in1=banks[:, 4:6, :],
                                             op0=ALU.add, op1=ALU.mult).then_inc(s["m_ready"], 1)

                def keyed(b):
                    dve.wait_ge(s["m_ready"], b + 1)
                    dve.wait_ge(s["ak_ready"], b + 1)
                    dve.tensor_tensor(m[:], m[:], ak[:, b % 2], ALU.mult).then_inc(s["sum_chain"], 1)

                def summed(b, f):
                    dve.wait_ge(s["sum_chain"], b + 1)
                    wait(dve, s["mem_chain"], 2 * b)
                    first = 0.0 if b == 0 else mem[:, (b - 1) % 2, f, W - 1:W]
                    dve.tensor_tensor_scan(mem[:, b % 2, f], one[:], m[:, f], first, ALU.mult,
                                           ALU.add).then_inc(s["mem_chain"], 1)

                def read_out(b):
                    dve.wait_ge(s["mem_chain"], 2 * b + 2)
                    dve.wait_ge(s["qr_ready"], b + 1)
                    wait(dve, s["o_ready"], b - 1)
                    dve.tensor_tensor(read[:, b % 2], mem[:, b % 2], qr[:, b % 2], ALU.mult) \
                       .then_inc(s["read_ready"], 1)

                def normalise(b):
                    dve.wait_ge(s["sq_ready"], b + 1)
                    dve.tensor_reduce(ss[:], sq[:].rearrange("p c (a d) -> p (c a) d", d=DH), AX.X,
                                      ALU.add).then_inc(s["ss_ready"], 1)
                    dve.wait_ge(s["ss_ready"], b + 1)
                    at = (RL + 1) * b
                    dve.tensor_scalar(ss[:], ss[:], 1e-24, None, ALU.max).then_inc(s["q_chain"], 1)
                    dve.wait_ge(s["q_chain"], at + 1)
                    newton = rsqrt_steps(dve, ss[:], sy[:], st[:], s["q_chain"], at + 1, s["q_rs"], srs[:])
                    if b >= 1:
                        next(newton)
                        gated(b - 1)
                    for _ in newton:
                        pass
                    dve.wait_ge(s["q_rs"], b + 1)
                    dve.wait_ge(s["raw_ready"], b + 1)
                    heads = qn[:, b % 2].rearrange("p c (a d) -> p (c a) d", d=DH)
                    dve.tensor_tensor(heads, heads, spread(srs[:].unsqueeze(2), 2, DH), ALU.mult) \
                       .then_inc(s["qn_ready"], 1)

                def memory(b):
                    keyed(b)
                    yield
                    for f in range(HALF):
                        summed(b, f)
                        yield
                    read_out(b)
                    yield

                def norm_out(b, between):
                    dve.wait_ge(s["o_ready"], b + 1)
                    n = (RL + 3) * b
                    for c in range(4):
                        ins = dve.bn_stats(ostats[:, c], banks[:, OUT_BANKS[b], c * P:c * P + P])
                    ins.then_inc(s["o_chain"], 1)
                    dve.wait_ge(s["o_chain"], n + 1)
                    for c in range(4):
                        ins = dve.bn_aggr(omv[:, c], ostats[:, c])
                    ins.then_inc(s["o_chain"], 1)
                    dve.wait_ge(s["o_chain"], n + 2)
                    dve.tensor_scalar(ov[:], omv[:, :, 1], EPS, None, ALU.add).then_inc(s["o_chain"], 1)
                    dve.wait_ge(s["o_chain"], n + 3)
                    for _ in rsqrt_steps(dve, ov[:], oy[:], ot[:], s["o_chain"], n + 3, s["o_rs"], ors[:]):
                        next(between, None)
                    for _ in between:
                        pass
                    dve.wait_ge(s["o_rs"], b + 1)
                    wait(dve, s["out_ready"], b - 1)
                    for c in range(4):
                        ins = dve.tensor_scalar(on[:, b % 2, c], banks[:, OUT_BANKS[b], c * P:c * P + P],
                                                omv[:, c, 0:1], ors[:, c:c + 1], ALU.subtract, ALU.mult)
                    ins.then_inc(s["on_ready"], 1)

                def add_out(b):
                    dve.wait_ge(s["affine"], 2 * b + 2)
                    part = x[:, 4 * b:4 * b + 4]
                    dve.tensor_tensor(part, part, on[:, b % 2], ALU.add).then_inc(s["out_ready"], 1)
                    dve.wait_ge(s["out_ready"], b + 1)
                    for c in range(4 * b, 4 * b + 4):
                        dve.bn_stats(stats[:, c], x[:, c])

                for b in range(NB + 2):
                    if b < NB:
                        normalise(b)
                    elif b == NB:
                        gated(b - 1)
                    between = memory(b - 1) if 1 <= b <= NB else iter(())
                    if b >= 2:
                        norm_out(b - 2, between)
                    for _ in between:
                        pass
                    if 3 <= b <= NB:
                        add_out(b - 3)
                add_out(NB - 2)
                affine(dve, NB - 1)
                add_out(NB - 1)


class OscillatorTables:

    def __init__(self, nc, a, tabs, weights, sem, scratch):
        self.nc, self.a, self.weights = nc, a, weights
        self.cos, self.dec, self.rdec = tabs["cos"], tabs["dec"], tabs["rdec"]
        def sb(name, shape):
            return scratch.enter_context(nc.sbuf_tensor(name, shape, F32))

        self.times, self.turns = sb("times", [P, T]), sb("turns", [P, 2, T])
        self.flat = sb("flat", [P, 256])
        self.rows = [nc.dram_tensor(f"power_rows{n}", (16, T), F32).ap() for n in range(2)]
        self.rows_out, self.flat_in, self.inverted, self.inverse_out, self.spread_in = (
            sem("tab_" + n) for n in ("rows_out", "flat_in", "inverted", "inverse_out", "spread_in"))
        self.freqs = sb("freqs_sb", [P, 2])
        self.gam = sb("gam_sb", [P, 12, 2])
        self.loaded, self.chain, self.powers, self.squares, self.angles, self.done = (
            sem("tab_" + n) for n in ("loaded", "chain", "powers", "squares", "angles", "done"))
        self.quarter = sb("quarter", [P, 1])
        self.quarter_set = sem("tab_quarter_set")
        self.links = 0

    def load(self, sp):
        a, w = self.a, self.weights
        sp.dma_start(self.times[:], a["times"].partition_broadcast(P)).then_inc(self.loaded, 16)
        sp.dma_start(self.freqs[:], a["freqs"]).then_inc(self.loaded, 16)
        sp.dma_start(self.gam[:, 0], a["gamma"]).then_inc(self.loaded, 16)
        for n in ("qk", "v", "g", "o", "conv_w", "g_b"):
            sp.dma_start(w[n][:], a["o_" + n]).then_inc(self.loaded, 16)
        sp.dma_start(w["conv_b"][:], a["o_conv_b"].rearrange("(p o) -> p o", o=1)) \
          .then_inc(self.loaded, 16)
        for n in ("ln_g", "ln_b"):
            sp.dma_start(w[n][:], a["o_" + n].partition_broadcast(P)).then_inc(self.loaded, 16)
        sp.wait_ge(self.powers, 24)
        for f in range(2):
            sp.dma_start(self.rows[0][8 * f:8 * f + 8, :], self.dec[0:P:DH, f, :]).then_inc(self.rows_out, 16)
        sp.wait_ge(self.rows_out, 32)
        sp.dma_start(self.flat[:], self.rows[0].rearrange("h (b t) -> (h b) t", t=256)) \
          .then_inc(self.flat_in, 16)

    def load_inverse(self, sp):
        sp.wait_ge(self.inverted, 2)
        sp.dma_start(self.rows[1].rearrange("h (b t) -> (h b) t", t=256), self.flat[:]) \
          .then_inc(self.inverse_out, 16)
        sp.wait_ge(self.inverse_out, 16)
        for f in range(2):
            for h in range(8):
                sp.dma_start(self.rdec[DH * h:DH * h + DH, f, :],
                             self.rows[1][8 * f + h, :].partition_broadcast(DH)).then_inc(self.spread_in, 16)

    LOADS = 12

    DOUBLINGS, BY_POOL = 11, 9

    def decays(self, pool):
        gam = self.gam
        pool.memset(self.quarter[:], float(np.pi / 2)).then_inc(self.quarter_set, 1)
        pool.memset(self.dec[:, :, 0:1], 0.5).then_inc(self.powers, 2)
        pool.wait_ge(self.loaded, 16 * self.LOADS)
        for k in range(self.DOUBLINGS - 1):
            if k:
                pool.wait_ge(self.squares, k)
            pool.tensor_tensor(gam[:, k + 1], gam[:, k], gam[:, k], ALU.mult) \
                .then_inc(self.squares, 1)
            if k < self.BY_POOL:
                self.double(pool, k)

    def last_decays(self, dve):
        for k in range(self.BY_POOL, self.DOUBLINGS):
            dve.wait_ge(self.squares, k)
            self.double(dve, k)

    def double(self, eng, k):
        dec, n = self.dec, 1 << k
        eng.wait_ge(self.powers, 2 * k + 2)
        for f in range(2):
            eng.tensor_scalar(dec[:, f, n:2 * n], dec[:, f, 0:n], self.gam[:, k, f:f + 1], None,
                              ALU.mult).then_inc(self.powers, 1)

    def link(self, dve, ins):
        self.links += 1
        ins.then_inc(self.chain, 1)
        dve.wait_ge(self.chain, self.links)

    def angle(self, dve):
        cos = self.cos
        dve.wait_ge(self.loaded, 16 * self.LOADS)
        for f in range(2):
            self.link(dve, dve.tensor_scalar(cos[:, f], self.times[:], self.freqs[:, f:f + 1], None, ALU.mult))

    def whole_turns(self, dve, part):
        cos, turns = self.cos, self.turns
        if part == 0:
            self.link(dve, dve.tensor_scalar(turns[:], cos[:], float(np.pi / 2), 1 / (2 * np.pi), ALU.add,
                                             ALU.mult))
        elif part == 1:
            self.link(dve, dve.tensor_scalar(turns[:], turns[:], ROUND, None, ALU.add))
        else:
            self.link(dve, dve.tensor_scalar(turns[:], turns[:], ROUND, None, ALU.subtract))

    def finish(self, dve):
        cos = self.cos
        two_pi, c1 = 2 * np.pi, 6.28125
        c2 = float(np.float32(np.floor((two_pi - c1) * 2.0 ** 16) / 2.0 ** 16))
        for c in (c1, c2, float(np.float32(two_pi - c1 - c2))):
            self.link(dve, dve.scalar_tensor_tensor(out=cos[:], in0=self.turns[:], scalar=-c, in1=cos[:],
                                                    op0=ALU.mult, op1=ALU.add))
        dve.tensor_scalar(cos[:], cos[:], 1.570796, -4.712388, ALU.min, ALU.max).then_inc(self.angles, 1)
        dve.wait_ge(self.spread_in, 16 * 16)

    def inverse(self, dve):
        flat = self.flat
        dve.wait_ge(self.flat_in, 16)
        dve.tensor_scalar(flat[:], flat[:], 2.0, 1e-6, ALU.mult, ALU.add).then_inc(self.inverted, 1)
        dve.wait_ge(self.inverted, 1)
        dve.reciprocal(flat[:], flat[:]).then_inc(self.inverted, 1)

    def sine(self, act):
        act.wait_ge(self.angles, 1)
        act.wait_ge(self.quarter_set, 1)
        act.activation(self.cos[:], self.cos[:], ACT.Sin, bias=self.quarter[:, 0:1]).then_inc(self.done, 1)


NAMES = ("X", "Wq", "Wk", "Wv", "Wg", "Wo", "W1", "W2", "ln_scale", "ln_bias", "gn_scale", "gn_bias")


def kernel(**inputs):
    import concourse.bacc as bacc
    from concourse.bass_utils import run_bass_kernel_spmd

    nc = bacc.Bacc("TRN2", target_bir_lowering=False, num_devices=1)
    inputs = {n: np.asarray(v) for n, v in inputs.items()}
    arrays = {n: np.ascontiguousarray(inputs["L0_attn_a_" + n]) for n in NAMES}
    arrays["rot"], arrays["small"] = retention_tables()
    arrays["gateT"] = np.ascontiguousarray(inputs["L0_ffn_gate_w"].T)
    sh = [np.asarray(inputs["L0_ffn_shared_" + n]) for n in ("gate", "up", "down")]
    ro = [np.asarray(inputs["L0_ffn_r_" + n]) for n in ("gate", "up", "down")]
    arrays["s_gu"] = np.ascontiguousarray(np.concatenate([sh[0], sh[1]], 0).T).reshape(D, 4, P)
    arrays["s_down"] = np.ascontiguousarray(sh[2].T.reshape(2, P, D).transpose(1, 0, 2))
    up = np.concatenate([ro[0], ro[1]], 1).transpose(2, 0, 1)
    down = ro[2].transpose(0, 2, 1).reshape(EXPERTS, 2, P, D).transpose(2, 0, 1, 3)
    arrays["routed"] = np.ascontiguousarray(np.concatenate([up, down.reshape(P, EXPERTS, 2 * D)], 2))
    b = {n: inputs["L0_attn_b_" + n] for n in ("qk_w", "v_w", "g_w", "g_b", "o_w", "conv_w", "conv_b",
                                               "ln_g", "ln_b", "freqs", "gamma")}
    arrays["o_qk"] = np.ascontiguousarray(b["qk_w"].T)
    arrays["o_v"] = np.ascontiguousarray(b["v_w"].T).reshape(D, 2, P)
    arrays["o_g"] = np.ascontiguousarray(b["g_w"].T).reshape(D, 2, P)
    arrays["o_o"] = np.ascontiguousarray(b["o_w"].T.reshape(2, P, D).transpose(1, 0, 2))
    arrays["o_conv_w"] = np.ascontiguousarray(b["conv_w"].reshape(D, 4))
    arrays["o_g_b"] = np.ascontiguousarray(b["g_b"].reshape(2, P).T)
    for n in ("conv_b", "ln_g", "ln_b"):
        arrays["o_" + n] = b[n]
    arrays["freqs"] = np.ascontiguousarray(b["freqs"].reshape(2, P).T)
    arrays["gamma"] = np.ascontiguousarray(np.repeat(b["gamma"].reshape(-1), DH).reshape(2, P).T)
    arrays["times"] = np.arange(T, dtype=np.float32)
    aps = {n: nc.dram_tensor("in_" + n, v.shape, mybir.dt.from_np(v.dtype), kind="ExternalInput").ap()
           for n, v in arrays.items()}
    out = nc.dram_tensor("out", (1, T, D), F32, kind="ExternalOutput").ap()
    build(nc, aps, out)
    r = run_bass_kernel_spmd(nc, [{"in_" + n: v for n, v in arrays.items()}], core_ids=[0])
    return r.results[0]["out"]
```
